# Optimizing a Trainium2 kernel written in Bass

```python
import numpy as np
import jax
import jax.numpy as jnp

def _softmax(x, axis=-1):
    return jax.nn.softmax(x, axis=axis)

def _gelu(x):
    return jax.nn.gelu(x, approximate=True)

def _silu(x):
    return jax.nn.silu(x)

def _sigmoid(x):
    return jax.nn.sigmoid(x)

def _layernorm(x, axis=-1, eps=1e-05):
    m = jnp.mean(x, axis=axis, keepdims=True)
    v = jnp.var(x, axis=axis, keepdims=True)
    return (x - m) / jnp.sqrt(v + eps)

def _scatter_add(tgt, idx, src, axis=0):
    return tgt.at[idx].add(src)

def _segment_sum(src, seg, n):
    return jax.ops.segment_sum(src, seg, n)
kernel_name = 'mk_early_fusion_d1_tok_img512_r4_da2f59'

def setup_inputs(seed: int=0):
    np.random.seed(seed)
    _w = jnp.asarray

    def _rec_inputs():
        import jax
        import jax.numpy as jnp
        _rk = jax.random.key(seed)
        x = -0.000121822 + 0.999869 * jax.random.normal(jax.random.fold_in(_rk, 1), (128, 3, 196, 196), jnp.float32)
        txt = 0.322801 + 1.18033 * jax.random.normal(jax.random.fold_in(_rk, 2), (128, 128, 128), jnp.float32)
        return (x, txt)
    x, txt = _rec_inputs()

    def _L0_tok_setup():
        import jax, jax.numpy as jnp
        import numpy as np
        B, C, H, N_P, HID = (64, 3, 196, 14, 128)
        P = H // N_P
        IN_DIM = C * P * P
        SEQ = N_P * N_P + 1

        def sinusoidal_position(length, d):
            pos = jnp.arange(length, dtype=jnp.float32)[:, None]
            i = jnp.arange(d)[None, :]
            angle = pos / jnp.power(10000.0, (2 * (i // 2)).astype(jnp.float32) / d)
            return jnp.where(i % 2 == 0, jnp.sin(angle), jnp.cos(angle)).astype(jnp.float32)
        key = jax.random.key(seed)
        k_img, k_w, k_b, k_tok = jax.random.split(key, 4)
        img = jax.random.normal(k_img, (B, C, H, H), dtype=jnp.float32)
        W = jax.random.normal(k_w, (HID, IN_DIM), dtype=jnp.float32) / np.sqrt(IN_DIM)
        b = jax.random.normal(k_b, (HID,), dtype=jnp.float32) * 0.01
        token = jax.random.uniform(k_tok, (1, HID), dtype=jnp.float32)
        pos = sinusoidal_position(SEQ, HID)
        return {'img': img, 'W': W, 'b': b, 'token': token, 'pos': pos}
    _L0_tok_all = _L0_tok_setup()
    _L0_tok_in = {k: v for k, v in _L0_tok_all.items() if k in ('W', 'b', 'token', 'pos')}
    del _L0_tok_all

    def _L0_attn_setup():
        import jax, jax.numpy as jnp
        import numpy as np
        import math
        B, L, D = (2, 512, 128)
        N_SETS, PLANES = (4, 8)
        key = jax.random.key(seed)
        ks = jax.random.split(key, 10)
        s = 1.0 / math.sqrt(D)
        return {'x': jax.random.normal(ks[0], (B, L, D), jnp.float32), 'Wk': jax.random.normal(ks[1], (D, N_SETS * PLANES), jnp.float32) * s, 'bk': jnp.zeros((N_SETS * PLANES,), jnp.float32), 'Wq': jax.random.normal(ks[2], (D, N_SETS * PLANES), jnp.float32) * s, 'bq': jnp.zeros((N_SETS * PLANES,), jnp.float32), 'Wv': jax.random.normal(ks[3], (D, D), jnp.float32) * s, 'bv': jnp.zeros((D,), jnp.float32), 'set_weights': jax.random.normal(ks[4], (N_SETS,), jnp.float32), 'pos_freqs': jax.random.uniform(ks[5], (PLANES,), jnp.float32), 'Wg': jax.random.normal(ks[6], (D, D), jnp.float32) * s, 'bg': jnp.zeros((D,), jnp.float32), 'pos_weight': jax.random.normal(ks[7], (1,), jnp.float32), 'Wo': jax.random.normal(ks[8], (D, D), jnp.float32) * s, 'bo': jnp.zeros((D,), jnp.float32)}
    _L0_attn_all = _L0_attn_setup()
    _L0_attn_in = {k: v for k, v in _L0_attn_all.items() if k in ('Wk', 'bk', 'Wq', 'bq', 'Wv', 'bv', 'set_weights', 'pos_freqs', 'Wg', 'bg', 'pos_weight', 'Wo', 'bo')}
    del _L0_attn_all

    def _L0_ffn_setup():
        import jax, jax.numpy as jnp
        import numpy as np
        E = 64
        K = 2
        D = 128
        H = 64
        NSH = 2
        ROUTE_SCALE = 2.5
        CAP = 256
        STD = 0.02
        key = jax.random.key(seed)
        ks = jax.random.split(key, 8)
        x = jax.random.normal(ks[0], (4, 512, D), dtype=jnp.float32)
        gate_w = jax.random.normal(ks[1], (E, D), dtype=jnp.float32) * STD
        w1 = jax.random.normal(ks[2], (E, D, H), dtype=jnp.float32) * STD
        w3 = jax.random.normal(ks[3], (E, D, H), dtype=jnp.float32) * STD
        w2 = jax.random.normal(ks[4], (E, H, D), dtype=jnp.float32) * STD
        sw1 = jax.random.normal(ks[5], (D, H * NSH), dtype=jnp.float32) * STD
        sw3 = jax.random.normal(ks[6], (D, H * NSH), dtype=jnp.float32) * STD
        sw2 = jax.random.normal(ks[7], (H * NSH, D), dtype=jnp.float32) * STD
        return {'x': x, 'gate_w': gate_w, 'w1': w1, 'w3': w3, 'w2': w2, 'sw1': sw1, 'sw3': sw3, 'sw2': sw2}
    _L0_ffn_all = _L0_ffn_setup()
    _L0_ffn_in = {k: v for k, v in _L0_ffn_all.items() if k in ('gate_w', 'w1', 'w3', 'w2', 'sw1', 'sw3', 'sw2')}
    del _L0_ffn_all
    return {'x': x, 'txt': txt, 'L0_tok_W': _L0_tok_in['W'], 'L0_tok_b': _L0_tok_in['b'], 'L0_tok_token': _L0_tok_in['token'], 'L0_tok_pos': _L0_tok_in['pos'], 'L0_attn_Wk': _L0_attn_in['Wk'], 'L0_attn_bk': _L0_attn_in['bk'], 'L0_attn_Wq': _L0_attn_in['Wq'], 'L0_attn_bq': _L0_attn_in['bq'], 'L0_attn_Wv': _L0_attn_in['Wv'], 'L0_attn_bv': _L0_attn_in['bv'], 'L0_attn_set_weights': _L0_attn_in['set_weights'], 'L0_attn_pos_freqs': _L0_attn_in['pos_freqs'], 'L0_attn_Wg': _L0_attn_in['Wg'], 'L0_attn_bg': _L0_attn_in['bg'], 'L0_attn_pos_weight': _L0_attn_in['pos_weight'], 'L0_attn_Wo': _L0_attn_in['Wo'], 'L0_attn_bo': _L0_attn_in['bo'], 'L0_ffn_gate_w': _L0_ffn_in['gate_w'], 'L0_ffn_w1': _L0_ffn_in['w1'], 'L0_ffn_w3': _L0_ffn_in['w3'], 'L0_ffn_w2': _L0_ffn_in['w2'], 'L0_ffn_sw1': _L0_ffn_in['sw1'], 'L0_ffn_sw3': _L0_ffn_in['sw3'], 'L0_ffn_sw2': _L0_ffn_in['sw2']}

def reference(x, txt, L0_tok_W, L0_tok_b, L0_tok_token, L0_tok_pos, L0_attn_Wk, L0_attn_bk, L0_attn_Wq, L0_attn_bq, L0_attn_Wv, L0_attn_bv, L0_attn_set_weights, L0_attn_pos_freqs, L0_attn_Wg, L0_attn_bg, L0_attn_pos_weight, L0_attn_Wo, L0_attn_bo, L0_ffn_gate_w, L0_ffn_w1, L0_ffn_w3, L0_ffn_w2, L0_ffn_sw1, L0_ffn_sw3, L0_ffn_sw2):
    import jax
    import jax.numpy as jnp

    def _L0_tok_ref(img, W, b, token, pos):
        import jax, jax.numpy as jnp
        import numpy as np
        B, C, H, N_P, HID = (64, 3, 196, 14, 128)
        P = H // N_P
        IN_DIM = C * P * P
        SEQ = N_P * N_P + 1

        def sinusoidal_position(length, d):
            pos = jnp.arange(length, dtype=jnp.float32)[:, None]
            i = jnp.arange(d)[None, :]
            angle = pos / jnp.power(10000.0, (2 * (i // 2)).astype(jnp.float32) / d)
            return jnp.where(i % 2 == 0, jnp.sin(angle), jnp.cos(angle)).astype(jnp.float32)
        Bn = img.shape[0]
        patches = img.reshape(Bn, C, N_P, P, N_P, P)
        patches = patches.transpose(0, 2, 4, 1, 3, 5).reshape(Bn, N_P * N_P, IN_DIM)
        tokens = jnp.einsum('bsd,hd->bsh', patches, W) + b
        cls = jnp.broadcast_to(token[None, :, :], (Bn, 1, HID))
        out = jnp.concatenate([cls, tokens], axis=1) + pos
        return out

    def _L0_attn_ref(x, Wk, bk, Wq, bq, Wv, bv, set_weights, pos_freqs, Wg, bg, pos_weight, Wo, bo):
        import jax, jax.numpy as jnp
        import numpy as np
        import math
        B, L, D = (2, 512, 128)
        N_SETS, PLANES = (4, 8)
        Bx, Lx, Dx = x.shape
        pi = jnp.float32(math.pi)
        key_phase = jnp.tanh(x @ Wk + bk) * pi
        query_phase = jnp.tanh(x @ Wq + bq) * pi
        key_ph = jnp.exp(1j * key_phase.astype(jnp.complex64)).reshape(Bx, Lx, N_SETS, PLANES)
        qry_ph = jnp.exp(1j * query_phase.astype(jnp.complex64)).reshape(Bx, Lx, N_SETS, PLANES)
        V = (x @ Wv + bv).astype(jnp.complex64)
        weights = jax.nn.softmax(set_weights, axis=0)
        total = jnp.zeros((Bx, Lx, Dx), jnp.float32)
        for s in range(N_SETS):
            bound = key_ph[:, :, s, :, None] * V[:, :, None, :]
            memory = jnp.cumsum(bound, axis=1)
            retrieved = (memory * jnp.conj(qry_ph[:, :, s, :, None])).sum(axis=2).real
            total = total + weights[s] * retrieved
        pos = jnp.arange(Lx, dtype=jnp.float32)[:, None]
        pos_phase = pos * pos_freqs * (2.0 * pi)
        pos_ph = jnp.exp(1j * pos_phase.astype(jnp.complex64))
        bound_pos = pos_ph[None, :, :, None] * V[:, :, None, :]
        memory_pos = jnp.cumsum(bound_pos, axis=1)
        retrieved_pos = (memory_pos * jnp.conj(pos_ph)[None, :, :, None]).sum(axis=2).real
        gate = jax.nn.sigmoid(x @ Wg + bg)
        pos_contrib = jax.nn.sigmoid(pos_weight[0]) * retrieved_pos
        total = gate * total + (1.0 - gate) * pos_contrib
        positions = jnp.arange(1, Lx + 1, dtype=jnp.float32)
        norm = jnp.sqrt(positions * PLANES)[None, :, None]
        return x + total / norm @ Wo + bo

    def _L0_ffn_ref(x, gate_w, w1, w3, w2, sw1, sw3, sw2):
        import jax, jax.numpy as jnp
        import numpy as np
        E = 64
        K = 2
        D = 128
        H = 64
        NSH = 2
        ROUTE_SCALE = 2.5
        CAP = 256
        STD = 0.02
        bs, slen, d = x.shape
        xf = x.reshape(-1, d)
        logits = xf @ gate_w.T
        scores = jax.nn.sigmoid(logits.astype(jnp.float32))
        top_scores, top_idx = jax.lax.top_k(scores, K)
        top_scores = top_scores / (top_scores.sum(-1, keepdims=True) + 1e-20)
        top_scores = top_scores * ROUTE_SCALE
        flat_e = top_idx.reshape(-1)
        x_pairs = jnp.repeat(xf, K, axis=0)
        oh = jax.nn.one_hot(flat_e, E, dtype=jnp.int32)
        pos = jnp.take_along_axis(jnp.cumsum(oh, axis=0), flat_e[:, None], axis=1)[:, 0] - 1
        buf = jnp.zeros((E, CAP, d), dtype=xf.dtype).at[flat_e, pos].set(x_pairs, mode='drop')
        h = jax.nn.silu(jnp.einsum('ecd,edh->ech', buf, w1)) * jnp.einsum('ecd,edh->ech', buf, w3)
        y = jnp.einsum('ech,ehd->ecd', h, w2)
        valid = (pos < CAP)[:, None]
        y_pairs = jnp.where(valid, y[flat_e, jnp.minimum(pos, CAP - 1)], 0.0)
        routed = (y_pairs.reshape(-1, K, d) * top_scores[..., None].astype(xf.dtype)).sum(axis=1)
        shared = jax.nn.silu(xf @ sw1) * (xf @ sw3) @ sw2
        return (shared + routed).reshape(bs, slen, d)
    h = _L0_tok_ref(x, L0_tok_W, L0_tok_b, L0_tok_token, L0_tok_pos)
    h = jnp.concatenate([h, txt], axis=1)
    h = h + _L0_attn_ref(_layernorm(h, axis=-1), L0_attn_Wk, L0_attn_bk, L0_attn_Wq, L0_attn_bq, L0_attn_Wv, L0_attn_bv, L0_attn_set_weights, L0_attn_pos_freqs, L0_attn_Wg, L0_attn_bg, L0_attn_pos_weight, L0_attn_Wo, L0_attn_bo)
    h = h + _L0_ffn_ref(_layernorm(h, axis=-1), L0_ffn_gate_w, L0_ffn_w1, L0_ffn_w3, L0_ffn_w2, L0_ffn_sw1, L0_ffn_sw3, L0_ffn_sw2)
    return h

_drawn_inputs = setup_inputs


def setup_inputs(seed=0):
    import zlib

    import numpy as np

    out = dict(_drawn_inputs(seed))
    spreads = {'L0_attn_bk': (0.0, 0.1),
     'L0_attn_bq': (0.0, 0.298),
     'L0_attn_bv': (0.0, 0.1),
     'L0_attn_bg': (0.0, 0.8),
     'L0_attn_bo': (0.0, 0.1)}
    factors = {'L0_tok_b': 7.261,
     'L0_attn_pos_freqs': 8.0,
     'L0_ffn_gate_w': 8.0,
     'L0_ffn_w1': 8.0,
     'L0_ffn_w3': 8.0,
     'L0_ffn_w2': 8.0,
     'L0_ffn_sw1': 8.0,
     'L0_ffn_sw3': 8.0,
     'L0_ffn_sw2': 8.0}
    for name, (base, spread) in spreads.items():
        noise = np.random.default_rng([zlib.crc32(name.encode()), seed]).standard_normal(out[name].shape)
        drawn = base * np.exp(spread * noise) if base else spread * noise
        out[name] = jnp.asarray(drawn.astype(out[name].dtype))
    for name, factor in factors.items():
        out[name] = (out[name] * factor).astype(out[name].dtype)
    return out
```

```python
from contextlib import ExitStack

import numpy as np

import concourse.bass as bass
from concourse import mybir

F32 = mybir.dt.float32
BF16 = mybir.dt.bfloat16
I32 = mybir.dt.int32
U32 = mybir.dt.uint32
ALU = mybir.AluOpType
ACT = mybir.ActivationFunctionType
AX = mybir.AxisListType

B, C, H, G = 128, 3, 196, 14
P = H // G
D = 128
NIMG = G * G + 1
NTXT = 128
L = NIMG + NTXT
SETS, PLANES = 4, 8
HF = SETS * PLANES
E, TOPK, CAP, FH = 64, 2, 256, 64
PAIRS = B // 2
TILE = 128
TILES = [(0, TILE), (TILE, NIMG - TILE), (NIMG, NTXT)]
NT = len(TILES)
T1 = TILES[1][1]
CP = C * P
XW = P + G * H
COPIES = 3
SHIFT = 5
KROWS = COPIES * CP
ROW = D + 4
SLOTS = E * CAP
TOKENS = B * L
LN_EPS = 1e-5
ROUTE = 2.5
SIG_M1 = 1.0 / (1.0 + float(np.exp(1.0)))
PI_LOW = 3.1415925
TWO_PI = float(np.float32(2.0) * np.float32(np.pi))
TP1 = 6.28125
TP2 = float(np.float32(np.round((2 * np.pi - TP1) * 2**20) / 2**20))
TP3 = float(np.float32(2 * np.pi - TP1 - TP2))
ROUND = 1.5 * 2.0**23
FAR = 1.0e6

CONST = {}
_at = 0
for _n, _w in (("ident", 128), ("below", 128), ("mask", 2 * L), ("maskn", 2 * L), ("invn", L), ("iota", E),
               ("pos", L), ("tok", 2 * NT), ("sel", SETS), ("delta", 1), ("dpos", 1), ("dump", 8)):
    CONST[_n] = (_at, _at + _w)
    _at += _w
CW = _at


def constants():
    t = np.zeros((128, CW), np.float32)

    def put(name, v):
        a, b = CONST[name]
        t[:, a:b] = v

    p = np.arange(128)[:, None]
    put("ident", np.eye(128))
    put("below", p < np.arange(128)[None, :])
    l = np.arange(L)[None, :]
    invn = (0.5 / np.sqrt((l + 1) * PLANES)).astype(np.float32)
    m0 = p <= l
    q1 = np.arange(TILE, L)[None, :]
    m1 = (p + TILE <= q1) & (p < T1)
    q2 = np.arange(NIMG, L)[None, :]
    m2 = p + NIMG <= q2
    mask = np.concatenate([m0, m1, m2], 1).astype(np.float32)
    n = np.concatenate([invn[:, 0:L], invn[:, TILE:L], invn[:, NIMG:L]], 1)
    put("mask", mask)
    put("maskn", mask * n)
    put("invn", invn)
    put("iota", np.arange(E)[None, :])
    put("pos", l)
    put("tok", np.concatenate([s * L + t0 + p for s in range(2) for t0, _ in TILES], 1))
    put("sel", (p % HF) // PLANES == np.arange(SETS)[None, :])
    put("delta", -0.5 * (p % (2 * HF) < HF))
    put("dpos", np.pi / 2 * (p < PLANES))
    put("dump", TOKENS + p + 128 * (np.arange(8)[None, :] % 2))
    return t


class Pair:

    def __init__(self, twice, j, c):
        self.twice, self.j, self.c = twice, j, c

    def back(self, n):
        return Pair(self.twice, self.j, self.c - n)

    @property
    def u(self):
        return self.c % 2

    def runs(self):
        return self.j is not None or 0 <= self.c < PAIRS

    def count(self):
        return self.c + 1 if self.j is None else self.twice + (self.c + 1)

    def uses(self):
        return self.c // 2 + 1 if self.j is None else self.j + (self.c // 2 + 1)

    def number(self):
        return self.c if self.j is None else self.twice + self.c


SKEW = 3
HEAD = 4
TAIL0 = PAIRS


def steps(eng, body):
    for k in range(HEAD):
        body(Pair(None, None, k))
    with_loop = (TAIL0 - HEAD) // 2
    assert HEAD + 2 * with_loop == TAIL0 and HEAD % 2 == 0
    with eng.Fori(HEAD // 2, HEAD // 2 + with_loop) as j:
        twice = j * 2
        for u in range(2):
            body(Pair(twice, j, u))
    for k in range(TAIL0, TAIL0 + SKEW):
        body(Pair(None, None, k))


def wait(eng, sem, pair, back=0):
    q = pair.back(back)
    if q.j is not None or 0 <= q.c < PAIRS:
        eng.wait_ge(sem, q.count())


def wait_dma(eng, sems, pair, each, back=0):
    q = pair.back(back)
    if q.j is not None or q.c >= 0:
        eng.wait_ge(sems[q.u], q.uses() * (16 * each))


def program(nc, t, out, slots_d):
    ctx = ExitStack()
    with ctx:
        def sb(name, shape, dt=F32):
            return ctx.enter_context(nc.sbuf_tensor(name, shape, dt))

        def sem(name):
            return ctx.enter_context(nc.semaphore(name))

        def sems(name):
            return [sem(f"{name}{u}") for u in range(2)]

        const = sb("const", [128, CW])

        def cst(name, p=128):
            a, b = CONST[name]
            return const[0:p, a:b]

        ident = cst("ident")
        w_tok = sb("w_tok", [KROWS, SHIFT, D])
        pos_raw = sb("pos_raw", [128, 2, D])
        tok_col = sb("tok_col", [D, 1])
        b_col = sb("b_col", [D, 1])
        pos_t = sb("pos_t", [D, NIMG])
        wk = sb("wk", [D, 2 * HF])
        wq = sb("wq", [D, 2 * HF])
        bk_col = sb("bk_col", [128, 1])
        bq_col = sb("bq_col", [128, 1])
        wv = sb("wv", [D, D])
        wg = sb("wg", [D, D])
        wo = sb("wo", [D, D])
        bg_col = sb("bg_col", [D, 1])
        bg_half = sb("bg_half", [D, 1])
        bv_row = sb("bv_row", [128, D])
        bo_row = sb("bo_row", [128, D])
        gate_raw = sb("gate_raw", [E, D])
        gate_t = sb("gate_t", [D, E])
        sw1 = sb("sw1", [D, D])
        sw3 = sb("sw3", [D, D])
        sw2 = sb("sw2", [D, D])
        below = sb("below", [128, 128], BF16)
        ones = sb("ones", [128, 128], BF16)
        setw = sb("setw", [128, SETS])
        setx = sb("setx", [128, 4 * SETS])
        wcol = sb("wcol", [128, 8])
        wn = sb("wn", [128, L])
        freq = sb("freq", [40, 1])
        feat = sb("feat", [40, L])
        pos_a = sb("pos_a", [128, 2 * L])
        half_pi = sb("half_pi", [128, 1])
        pw_col = sb("pw_col", [128, 1])
        neg_half = sb("neg_half", [128, 2 * NT])

        xin = sb("xin", [128, 2, 2, XW])
        h_t = sb("h_t", [D, 2, 2, 2 * TILE])
        h = sb("h", [128, 2, 2, NT, D])
        xh = sb("xh", [128, 2, 2 * NT, D])
        st1 = sb("st1", [128, 2, 2 * NT, 6])
        ms1 = sb("ms1", [128, 2, 2 * NT])
        dm1 = sb("dm1", [128, 2 * NT])
        m21 = sb("m21", [128, 2 * NT])
        dd1 = sb("dd1", [128, 2 * NT])
        vs1 = sb("vs1", [128, 2 * NT])
        ve1 = sb("ve1", [128, 2, 2 * NT])
        rs1 = sb("rs1", [128, 2, 2 * NT])
        nb1 = sb("nb1", [128, 2, 2 * NT])
        hb = sb("hb", [128, 2, 2 * NT, D])
        hbo = sb("hbo", [128, 2 * NT, D])
        x_t = sb("x_t", [D, 2, 2, L])
        ph_t = sb("ph_t", [128, 2, 2, L])
        ph_a = sb("ph_a", [128, 2, 2, L])
        kq = sb("kq", [128, 2, 2, L])
        qn = sb("qn", [128, 2, L])
        v = sb("v", [128, 2, 2, NT, D])
        gt = sb("gt", [D, 2, 2, L])
        a_t = sb("a_t", [128, 2, 2, 2, L])
        pos_o = sb("pos_o", [D, 2, L])
        dif = sb("dif", [D, 2, L])
        gdif = sb("gdif", [D, 2, L])
        tot = sb("tot", [D, 2, L])
        h2 = sb("h2", [128, 2, 2 * NT, D])
        st2 = sb("st2", [128, 2, 2 * NT, 6])
        ms2 = sb("ms2", [128, 2, 2 * NT])
        dm2 = sb("dm2", [128, 2 * NT])
        m22 = sb("m22", [128, 2 * NT])
        dd2 = sb("dd2", [128, 2 * NT])
        vs2 = sb("vs2", [128, 2 * NT])
        ve2 = sb("ve2", [128, 2, 2 * NT])
        rs2 = sb("rs2", [128, 2, 2 * NT])
        nb2 = sb("nb2", [128, 2, 2 * NT])
        xs = sb("xs", [128, 2, 2 * NT, ROW])
        x2_t = sb("x2_t", [D, 2, L])
        lg = sb("lg", [128, 2 * NT, E])
        top = sb("top", [128, 2 * NT, 8])
        topi = sb("topi", [128, 2 * NT, 8], U32)
        idx = sb("idx", [128, 2, 2 * NT])
        hot = sb("hot", [128, 2, 2 * NT, E], BF16)
        both = sb("both", [128, 2 * NT + 1, E], BF16)
        cnt = sb("cnt", [128, 2 * NT, E], BF16)
        picked = sb("picked", [128, 2, 2 * NT, E], BF16)
        place = sb("place", [128, 2, 2 * NT])
        over = sb("over", [128, 2, 2 * NT])
        slotf = sb("slotf", [128, 2, 2 * NT])
        slot = sb("slot", [128, 2, 2, 2 * NT], I32)
        carry = sb("carry", [128, 2, E])
        tokn = sb("tokn", [128, 2, 2 * NT])
        lo = sb("lo", [128, 2 * NT, 2])
        hi = sb("hi", [128, 2 * NT, 2])
        slo = sb("slo", [128, 2 * NT, 2])
        thi = sb("thi", [128, 2 * NT, 2])
        rlo = sb("rlo", [128, 2 * NT, 2])
        sgl = sb("sgl", [128, 2 * NT, 2])
        sg = sb("sg", [128, 2 * NT, 2])
        ssum = sb("ssum", [128, 2 * NT])
        sinv = sb("sinv", [128, 2 * NT])
        sl = sb("sl", [D, 2, L])
        su = sb("su", [D, 2, L])
        fin = sb("fin", [128, 2, 2 * NT, D])

        flat_a = a_t[:, :, :, :, :].rearrange("p u s a l -> p (u s a l)")
        w_raw = flat_a[:, 0:CP * P].rearrange("p (a b) -> p a b", b=P)
        w_pad = flat_a[:, CP * P:CP * P + SHIFT * KROWS].rearrange("p (m k) -> p m k", k=KROWS)
        ph = x_t[0:40, :, :, :].rearrange("p u s l -> p (u s) l")
        init_rows = fin[:, :, :, :].rearrange("p u t d -> p (u t d)")[:, 0:8 * ROW].rearrange("p (i r) -> p i r", r=ROW)

        flat_x = xin[:, :, :, :].rearrange("p u s w -> p (u s w)")
        at = [0]

        def part(*shape):
            n = int(np.prod(shape))
            a = flat_x[:, at[0]:at[0] + n]
            at[0] += n
            names = "abcd"[:len(shape)]
            return a.rearrange(f"p ({' '.join(names)}) -> p {' '.join(names)}", **dict(zip(names, shape)))

        spare = sb("spare", [128, 2])
        rows = part(2, 4, ROW)
        w13 = part(2, 2, 2 * FH)
        w2 = part(2, D)
        xe_t = part(2, 4 * TILE)
        ae = part(2, CAP)
        ge = part(2, CAP)
        ecur = sb("ecur", [128, 2, 4])
        esel = sb("esel", [128, 4])
        ewd = sb("ewd", [128, 4])
        ewm = sb("ewm", [128, 4])
        ew = sb("ew", [128, 2, 4])
        etok = sb("etok", [128, 2, 4], I32)
        ye = part(2, 4, D)

        bank = ctx.enter_context(nc.psum_tensor("bank", [128, 8, 512], F32))

        s_const, s_wload, s_init, s_small = sem("s_const"), sem("s_wload"), sem("s_init"), sem("s_small")
        s_zero = sem("s_zero")
        s_pre_v, s_pre_a, s_pre_p, s_pre_pe = sem("s_pre_v"), sem("s_pre_a"), sem("s_pre_p"), sem("s_pre_pe")
        s_setup = sem("s_setup")
        s_xin, s_txt, s_store, s_scat = sems("s_xin"), sems("s_txt"), sems("s_store"), sems("s_scat")
        s_shift = sems("s_shift")
        s_pad = sem("s_pad")
        names = """pe_tok pe_th pe_tx pe_k pe_q pe_va pe_vb pe_ga pe_gb pe_sc pe_ta pe_pa pe_tb pe_pb pe_woa pe_wob
            pe_tx2a pe_tx2b pe_lg pe_ffa pe_ffb pe_pf pe_oa pe_ob
            v_ht v_st1 v_mm1 v_dd1 v_vs1 v_ve1 v_nb1 v_m3a v_m3b v_max v_ma v_mb v_imax v_idx v_hot v_both v_lohi v_rlo v_sgl v_sg
            v_ssum v_seps v_sinv v_meta v_fina v_finb v_da v_db v_ea v_eb v_tota v_totb v_cnt v_pick v_place v_over v_slotf v_sloti
            v_carry v_tok v_va v_vb v_qn v_h2a v_h2b v_st2 v_mm2 v_dd2 v_vs2 v_ve2 v_nb2 v_hbo
            a_x2ta a_x2tb a_h a_lg a_sia a_sib a_small a_xh a_pa a_pb a_xta a_xtb a_thk a_thq a_ga a_gb a_abs a_sin a_x2
            p_rs1 p_hb p_rs2""".split()
        S = {n: sem(n) for n in names}
        enames = "e_rows e_tr e_xt e_z e_silu e_g e_y0 e_y1 e_sel e_wd e_wm e_w e_tokn e_yv e_cur e_spare0 e_spare1".split()
        X = {n: sem(n) for n in enames}
        e_load = sems("e_load")
        e_add = sems("e_add")

        block = ctx.enter_context(nc.Block())

        N_W = 18

        @block.sync
        def _(sp):
            sp.dma_start(const[:, :], t["consts"]).then_inc(s_const, 16)
            sp.dma_start(w_raw[:, :, :], t["L0_tok_W"].rearrange("h (a b) -> h a b", b=P)).then_inc(s_wload, 16)
            sp.dma_start(pos_raw[:, 0, :], t["L0_tok_pos"][0:TILE, :]).then_inc(s_wload, 16)
            sp.dma_start(pos_raw[0:T1, 1, :], t["L0_tok_pos"][TILE:NIMG, :]).then_inc(s_wload, 16)
            sp.dma_start(tok_col[:, :], t["L0_tok_token"].rearrange("o h -> h o")).then_inc(s_wload, 16)
            col = lambda n: t[n].rearrange("(h o) -> h o", o=1)
            sp.dma_start(b_col[:, :], col("L0_tok_b")).then_inc(s_wload, 16)
            for i in range(2):
                sp.dma_start(wk[:, i * HF:(i + 1) * HF], t["L0_attn_Wk"]).then_inc(s_wload, 16)
                sp.dma_start(wq[:, i * HF:(i + 1) * HF], t["L0_attn_Wq"]).then_inc(s_wload, 16)
            for name, dst in (("L0_attn_Wv", wv), ("L0_attn_Wg", wg), ("L0_attn_Wo", wo), ("L0_ffn_sw1", sw1),
                              ("L0_ffn_sw3", sw3), ("L0_ffn_sw2", sw2), ("L0_ffn_gate_w", gate_raw)):
                sp.dma_start(dst[:, :], t[name]).then_inc(s_wload, 16)
            sp.dma_start(bg_col[:, :], col("L0_attn_bg")).then_inc(s_wload, 16)
            sp.dma_start(bv_row[:, :], t["L0_attn_bv"].rearrange("(o h) -> o h", o=1).to_broadcast([128, D])).then_inc(s_wload, 16)
            sp.wait_ge(s_pre_p, 2)
            init_v = slots_d.rearrange("(n i p) r -> n p i r", p=128, i=8)
            for n in range(SLOTS // (128 * 8)):
                sp.dma_start(init_v[n], init_rows[:, :, :]).then_inc(s_init, 16)
            sp.dma_start(out[TOKENS:TOKENS + CAP, :].rearrange("(i p) d -> p i d", p=128), init_rows[:, 0:2, 0:D])\
                .then_inc(s_init, 16)
            def load(q):
                n = q.number()
                for i in range(2):
                    img = t["x"][bass.ds(n * 2 + i, 1)] if q.j is not None else t["x"][2 * q.c + i:2 * q.c + i + 1]
                    for c in range(C):
                        src = img[:, c].rearrange("o (g r) w -> r (o g) w", r=P)
                        dst = xin[c * P:(c + 1) * P, q.u, i, P:XW].rearrange("r (g w) -> r g w", w=H)
                        sp.dma_start(dst, src).then_inc(s_xin[q.u], 16)
                txt = t["txt"][bass.ds(n * 2, 2)] if q.j is not None else t["txt"][2 * q.c:2 * q.c + 2]
                return txt

            def shift(q):
                wait_dma(sp, s_xin, q, 2 * C)
                for i in range(2):
                    for n in range(1, COPIES):
                        sp.dma_start(xin[n * CP:(n + 1) * CP, q.u, i, P - n * SHIFT:XW - n * SHIFT],
                                     xin[0:CP, q.u, i, P:XW]).then_inc(s_shift[q.u], 16)

            def body(k):
                q = k
                if q.runs():
                    wait(sp, S["pe_tok"], q, 2)
                    txt = load(q)
                    wait(sp, S["a_xh"], q, 2)
                    wait(sp, S["p_hb"], q, 2)
                    sp.dma_start(h[:, q.u, :, 2, :], txt.rearrange("s p d -> p s d")).then_inc(s_txt[q.u], 16)
                if k.runs():
                    shift(k)
                q = k.back(3)
                if q.runs():
                    wait(sp, S["v_fina"], q)
                    wait(sp, S["v_finb"], q)
                    n = q.number()
                    o = out[bass.ds(n * (2 * L), 2 * L), :] if q.j is not None else out[q.c * 2 * L:(q.c + 1) * 2 * L, :]
                    o = o.rearrange("(s l) d -> l s d", s=2)
                    f = fin[:, q.u, :, :].rearrange("p (s t) d -> p t s d", s=2)
                    for i, (t0, nt) in enumerate(TILES):
                        sp.dma_start(o[t0:t0 + nt], f[0:nt, i]).then_inc(s_store[q.u], 16)

            sp.wait_ge(s_pad, 1)
            steps(sp, body)
            for u in range(2):
                sp.wait_ge(s_scat[u], 16 * 4 * NT * (PAIRS // 2))
                sp.wait_ge(s_store[u], 16 * NT * (PAIRS // 2))
            rows_v = slots_d.rearrange("(a q p) r -> a p q r", p=128, q=4)
            w13_v = [t[n].rearrange("(a e) d h -> a d e h", e=2) for n in ("L0_ffn_w1", "L0_ffn_w3")]
            w2_v = t["L0_ffn_w2"].rearrange("(a e) h d -> a (e h) d", e=2)

            def fetch(a, m, j):
                u = m % 2
                if j is not None:
                    sp.wait_ge(X["e_yv"], a - 1)
                one = lambda v: (v[bass.ds(a, 1)] if j is not None else v[a:a + 1])
                sp.dma_start(rows[:, u, :, :], one(rows_v).rearrange("o p q r -> (o p) q r")).then_inc(e_load[u], 16)
                for i in range(2):
                    sp.dma_start(w13[:, u, i, :].rearrange("p (e h) -> p e h", e=2), one(w13_v[i]).rearrange("o d e h -> (o d) e h")).then_inc(e_load[u], 16)
                sp.dma_start(w2[:, u, :], one(w2_v).rearrange("o k d -> (o k) d")).then_inc(e_load[u], 16)

            for n in range(2):
                fetch(n, n, None)
            with sp.Fori(1, E // 4) as j:
                for n in range(2):
                    fetch(j * 2 + n, n, j)

        @block.gpsimd
        def _(pool):
            g = nc.gpsimd
            g.memset(init_rows[:, :, 0:D + 2], 0.0).then_inc(s_pre_p, 1)
            g.memset(init_rows[:, :, D + 2:D + 3], -1.0)
            pool.wait_ge(s_const, 16)
            g.tensor_copy(init_rows[:, :, D + 3], cst("dump")).then_inc(s_pre_p, 1)
            g.memset(neg_half[:, :], -0.5).then_inc(s_pre_p, 1)
            colr = lambda n: t[n].rearrange("(h o) -> h o", o=1)
            for i in range(4):
                pool.dma_start(bk_col[i * HF:(i + 1) * HF, :], colr("L0_attn_bk")).then_inc(s_small, 16)
                pool.dma_start(bq_col[i * HF:(i + 1) * HF, :], colr("L0_attn_bq")).then_inc(s_small, 16)
            row = lambda n, w: t[n].rearrange("(o h) -> o h", o=1).to_broadcast([128, w])
            pool.dma_start(bo_row[:, :], row("L0_attn_bo", D)).then_inc(s_small, 16)
            pool.dma_start(setw[:, :], row("L0_attn_set_weights", SETS)).then_inc(s_small, 16)
            pool.dma_start(pw_col[:, :], row("L0_attn_pos_weight", 1)).then_inc(s_small, 16)
            g.memset(freq[:, :], 0.0).then_inc(s_pre_p, 1)
            pool.wait_ge(s_pre_p, 4)
            for i in range(2):
                pool.dma_start(freq[i * 32:i * 32 + PLANES, :], colr("L0_attn_pos_freqs")).then_inc(s_small, 16)
            pool.wait_ge(s_init, 16 * (SLOTS // 1024 + 1))

            def rstd(ve, rs, q, s_ve, s_rs):
                wait(pool, s_ve, q)
                g.tensor_tensor(out=rs[:, q.u], in0=ve[:, q.u], in1=neg_half[:, :], op=ALU.pow).then_inc(s_rs, 1)

            def scatter(q, s):
                for i, (t0, nt) in enumerate(TILES):
                    for r in range(TOPK):
                        g.indirect_dma_start(
                            out=slots_d, out_offset=bass.IndirectOffsetOnAxis(
                                ap=slot[0:nt, q.u, r, s * NT + i:s * NT + i + 1], axis=0),
                            in_=xs[0:nt, q.u, s * NT + i, :], in_offset=None, bounds_check=SLOTS - 1,
                            oob_is_err=False).then_inc(s_scat[q.u], 16)

            def body(k):
                if k.back(3).runs():
                    wait(pool, S["v_sloti"], k, 3)
                    wait(pool, S["v_meta"], k, 3)
                if k.runs():
                    rstd(ve1, rs1, k, S["v_ve1"], S["p_rs1"])
                if k.back(3).runs():
                    for s in range(2):
                        scatter(k.back(3), s)
                if k.runs():
                    wait(pool, S["a_xh"], k)
                    wait(pool, S["v_hbo"], k, 2)
                    g.tensor_tensor(out=hb[:, k.u], in0=h[:, k.u].rearrange("p s t d -> p (s t) d"),
                                    in1=xh[:, k.u], op=ALU.add).then_inc(S["p_hb"], 1)
                if k.back(1).runs():
                    rstd(ve2, rs2, k.back(1), S["v_ve2"], S["p_rs2"])

            steps(pool, body)
            for u in range(2):
                pool.wait_ge(s_store[u], 16 * NT * (PAIRS // 2))

            last_row = pool.to_reg(TOKENS + CAP - 1)

            def add(a, n, j):
                pool.wait_ge(X["e_yv"], a + 1)
                for e in range(2):
                    if j is not None or n > 0:
                        pool.wait_ge(X["e_spare0"] if e == 0 else X["e_spare1"], a)
                    if e == 1:
                        pool.wait_ge(e_add[0], (a + 1) * 32)
                    elif j is not None or n > 0:
                        pool.wait_ge(e_add[1], a * 32)
                    g.tensor_tensor(out=spare[:, e:e + 1], in0=neg_half[:, 0:1], in1=neg_half[:, 1:2], op=ALU.add)\
                        .then_inc(X["e_spare0"] if e == 0 else X["e_spare1"], 1)
                    for i in range(2):
                        m = 2 * e + i
                        g.indirect_dma_start(
                            out=out, out_offset=bass.IndirectOffsetOnAxis(ap=etok[:, n % 2, m:m + 1], axis=0),
                            in_=ye[:, n % 2, m, :], in_offset=None, bounds_check=last_row,
                            compute_op=ALU.add).then_inc(e_add[e], 16)

            for n in range(2):
                add(n, n, None)
            with pool.Fori(1, E // 4) as j:
                for n in range(2):
                    add(j * 2 + n, n, j)
            for e in range(2):
                pool.wait_ge(e_add[e], (E // 2) * 32)

        @block.scalar
        def _(act):
            a = nc.scalar
            act.wait_ge(s_pre_v, 1)
            a.activation(setx[:, SETS:2 * SETS], setx[:, 0:SETS], ACT.Exp, accum_out=wcol[:, 1:2]).then_inc(s_pre_a, 1)
            a.activation(wcol[:, 2:3], pw_col[:, :], ACT.Exp, scale=-1.0).then_inc(s_pre_a, 1)
            act.wait_ge(s_pre_v, 2)
            a.activation(feat[0:PLANES, :], ph[0:PLANES, 1, :], ACT.Sin)
            a.activation(feat[32:40, :], ph[32:40, 1, :], ACT.Sin).then_inc(s_pre_a, 1)
            act.wait_ge(s_setup, 1)

            def body(k):
                y, z = k.back(1), k.back(2)
                if k.runs():
                    wait(act, S["pe_th"], k)
                    wait(act, S["p_hb"], k, 2)
                    wait(act, S["v_st1"], k, 2)
                    a.activation(h[:, k.u, :, 0:2, :], bank[:, 6, :].rearrange("p (s t d) -> p s t d", s=2, t=2),
                                 ACT.Copy).then_inc(S["a_h"], 1)
                if y.runs():
                    for s, (done, ready, used) in enumerate((("a_pa", "pe_pa", "v_tota"), ("a_pb", "pe_pb", "v_totb"))):
                        wait(act, S[ready], y)
                        wait(act, S[used], y, 1)
                        a.activation(pos_o[:, s, :], bank[:, 1 if s == 0 else 3, 0:L], ACT.Copy).then_inc(S[done], 1)
                if z.runs():
                    for s, (done, ready) in enumerate((("a_x2ta", "pe_tx2a"), ("a_x2tb", "pe_tx2b"))):
                        if s == 0:
                            wait(act, S["pe_lg"], z, 1)
                            wait(act, S["pe_ffb"], z, 1)
                        wait(act, S[ready], z)
                        a.activation(x2_t[:, s, :], bank[:, 4 + s, 0:L], ACT.Copy).then_inc(S[done], 1)
                    wait(act, S["pe_lg"], z)
                    wait(act, S["v_imax"], z, 1)
                    a.activation(lg[:, :, :], bank[:, 7, 0:2 * NT * E].rearrange("p (t e) -> p t e", e=E),
                                 ACT.Copy).then_inc(S["a_lg"], 1)
                    for s, (done, ready, used) in enumerate((("a_sia", "pe_ffa", "v_m3a"), ("a_sib", "pe_ffb", "v_m3b"))):
                        wait(act, S[ready], z)
                        wait(act, S[used], z, 1)
                        a.activation(sl[:, s, :], bank[:, 6 if s == 0 else 1, 0:L], ACT.Silu).then_inc(S[done], 1)
                if k.runs():
                    wait(act, S["v_nb1"], k)
                    wait(act, S["pe_tx"], k, 2)
                    for i in range(2 * NT):
                        ins = a.activation(xh[:, k.u, i, :], h[:, k.u, i // NT, i % NT, :], ACT.Identity,
                                           bias=nb1[:, k.u, i:i + 1], scale=rs1[:, k.u, i:i + 1])
                    ins.then_inc(S["a_xh"], 1)
                    wait(act, S["pe_tx"], k)
                    wait(act, S["pe_gb"], k, 2)
                    for s, (b, done) in enumerate(((3, "a_xta"), (7, "a_xtb"))):
                        a.activation(x_t[:, k.u, s, :], bank[:, b, 0:L], ACT.Copy).then_inc(S[done], 1)
                    wait(act, S["a_abs"], k, 2)
                    wait(act, S["pe_k"], k)
                    a.activation(ph_t[:, k.u, 0, :], bank[:, 6, 0:L], ACT.Tanh, bias=bk_col[:, :]).then_inc(S["a_thk"], 1)
                    wait(act, S["pe_q"], k)
                    a.activation(ph_t[:, k.u, 1, :], bank[:, 0, 0:L], ACT.Tanh, bias=bq_col[:, :]).then_inc(S["a_thq"], 1)
                    wait(act, S["a_thk"], k)
                    wait(act, S["a_thq"], k)
                    wait(act, S["a_sin"], k, 2)
                    a.activation(ph_a[:, k.u, :, :], ph_t[:, k.u, :, :], ACT.Abs, bias=cst("delta")).then_inc(S["a_abs"], 1)
                    wait(act, S["v_ea"], k, 2)
                    wait(act, S["v_eb"], k, 2)
                    for s, (done, ready, b) in enumerate((("a_ga", "pe_ga", 3), ("a_gb", "pe_gb", 7))):
                        wait(act, S[ready], k)
                        a.activation(gt[:, k.u, s, :], bank[:, b, 0:L], ACT.Tanh, bias=bg_half[:, :], scale=0.5)\
                            .then_inc(S[done], 1)
                    wait(act, S["a_abs"], k)
                    wait(act, S["pe_sc"], k, 2)
                    wait(act, S["v_qn"], k, 2)
                    a.activation(kq[:, k.u, :, :], ph_a[:, k.u, :, :], ACT.Sin, bias=half_pi[:, :], scale=-PI_LOW)\
                        .then_inc(S["a_sin"], 1)
                if z.runs():
                    wait(act, S["v_lohi"], z)
                    wait(act, S["v_sg"], z, 1)
                    a.activation(slo[:, :, :], lo[:, :, :], ACT.Silu)
                    a.activation(thi[:, :, :], hi[:, :, :], ACT.Tanh, scale=0.5).then_inc(S["a_small"], 1)
                if y.runs():
                    wait(act, S["v_nb2"], y)
                    wait_dma(act, s_scat, y, 4 * NT, 2)
                    wait(act, S["pe_tx2b"], y, 2)
                    for i in range(2 * NT):
                        ins = a.activation(xs[:, y.u, i, 0:D], h2[:, y.u, i, :], ACT.Identity,
                                           bias=nb2[:, y.u, i:i + 1], scale=rs2[:, y.u, i:i + 1])
                    ins.then_inc(S["a_x2"], 1)

            steps(act, body)

            def expert(n, m, j):
                act.wait_ge(X["e_tr"], n + 1)
                if j is not None:
                    act.wait_ge(X["e_z"], n - 1)
                a.activation(xe_t[:, m % 2, :], bank[:, m % 2, :], ACT.Copy).then_inc(X["e_xt"], 1)
                act.wait_ge(X["e_z"], n + 1)
                if j is not None:
                    act.wait_ge(X["e_g"], n - 1)
                a.activation(ae[:, m % 2, :], bank[:, 2 + m % 2, 0:CAP], ACT.Silu).then_inc(X["e_silu"], 1)

            for n in range(2):
                expert(n, n, None)
            with act.Fori(1, E // 4) as j:
                for n in range(2):
                    expert(j * 2 + n, n, j)

        @block.tensor
        def _(pe):
            mm = nc.tensor.matmul
            tr = nc.tensor.transpose
            pe.wait_ge(s_const, 16)
            pe.wait_ge(s_pre_v, 1)
            for m in range(SHIFT):
                ins = tr(bank[0:KROWS, m // 4, (m % 4) * D:(m % 4 + 1) * D], w_pad[:, m, :], ident)
            ins.then_inc(s_pre_pe, 1)
            tr(bank[:, 4, 0:TILE], pos_raw[:, 0, :], ident)
            tr(bank[:, 4, TILE:NIMG], pos_raw[0:T1, 1, :], ident[0:T1, 0:T1])
            tr(bank[:, 5, 0:E], gate_raw[:, :], ident[0:E, 0:E]).then_inc(s_pre_pe, 1)
            pe.wait_ge(s_pre_a, 3)
            mm(bank[:, 6, 0:L], feat[:, 0:TILE], feat[:, :], start=True, stop=True)
            mm(bank[:, 7, 0:L - TILE], feat[:, TILE:2 * TILE], feat[:, TILE:L], start=True, stop=False,
               skip_group_check=True)
            mm(bank[:, 7, L - TILE:L], feat[:, NIMG:L], feat[:, NIMG:L], start=False, stop=True,
               skip_group_check=True).then_inc(s_pre_pe, 1)
            pe.wait_ge(s_setup, 1)

            def body(k):
                y, z = k.back(1), k.back(2)
                if k.runs():
                    wait_dma(pe, s_shift, k, 2 * (COPIES - 1))
                    wait(pe, S["a_thq"], k, 1)
                    wait(pe, S["v_va"], k, 1)
                    for s in range(2):
                        for m in range(SHIFT):
                            r = slice(0, KROWS if m + (COPIES - 1) * SHIFT < P else KROWS - CP)
                            ins = mm(bank[:, s, 0:NIMG], w_tok[r, m, :], xin[r, k.u, s, m:m + P * (NIMG - 1) + 1:P],
                                     start=(m == 0), stop=(m == SHIFT - 1))
                    ins.then_inc(S["pe_tok"], 1)
                if y.runs():
                    wait(pe, S["a_sin"], y)
                    wait(pe, S["v_qn"], y)
                    wait(pe, S["v_vb"], y)
                    wait(pe, S["a_ga"], y)
                    wait(pe, S["v_fina"], y, 2)
                    wait(pe, S["v_finb"], y, 2)
                    for i, (t0, _) in enumerate(TILES):
                        for s in range(2):
                            r = slice(64 * s, 64 * s + 64)
                            dst = (bank[:, 2 + 2 * s, 0:L], bank[:, 3 + 2 * s, 0:L - TILE], bank[:, 3 + 2 * s, L - TILE:L])[i]
                            ins = mm(dst, kq[r, y.u, 0, t0:t0 + TILE], qn[r, y.u, t0:L], start=(i < 2), stop=(i != 1),
                                     skip_group_check=True)
                    ins.then_inc(S["pe_sc"], 1)
                if k.runs():
                    wait(pe, S["v_ht"], k)
                    wait(pe, S["v_cnt"], k, 3)
                    for s in range(2):
                        for i in range(2):
                            ins = tr(bank[:, 6, (2 * s + i) * D:(2 * s + i + 1) * D],
                                     h_t[:, k.u, s, i * TILE:(i + 1) * TILE], ident)
                    ins.then_inc(S["pe_th"], 1)
                if y.runs():
                    for s, (m, done_t, done_p) in enumerate((("v_ma", "pe_ta", "pe_pa"), ("v_mb", "pe_tb", "pe_pb"))):
                        wait(pe, S[m], y)
                        if s == 0:
                            wait(pe, S["v_ht"], y, -1)
                        for b, done in ((0, done_t), (1, done_p)):
                            for i, (t0, nt) in enumerate(TILES):
                                c0 = (0, L, L + L - TILE)[i]
                                src = a_t[0:nt, y.u, s].rearrange("p a l -> p (a l)") if b == 0 else pos_a[0:nt, :]
                                ins = mm(bank[:, 2 * s + b, t0:L], v[0:nt, y.u, s, i, :], src[:, c0:c0 + L - t0],
                                         start=(i == 0), stop=(i == NT - 1))
                            ins.then_inc(S[done], 1)
                if z.runs():
                    wait(pe, S["a_x2"], z)
                    wait(pe, S["v_mb"], z, -1)
                    wait(pe, S["v_fina"], z, 1)
                    wait(pe, S["v_finb"], z, 1)
                    for s, done in enumerate(("pe_tx2a", "pe_tx2b")):
                        for i, (t0, nt) in enumerate(TILES):
                            ins = tr(bank[:, 4 + s, t0:t0 + nt], xs[0:nt, z.u, s * NT + i, 0:D], ident[0:nt, 0:nt])
                        ins.then_inc(S[done], 1)
                    wait(pe, S["a_gb"], z, -1)
                    wait(pe, S["a_lg"], z, 1)
                    wait(pe, S["a_x2ta"], z)
                    wait(pe, S["a_x2tb"], z)
                    for s in range(2):
                        for i, (t0, _) in enumerate(TILES):
                            ins = mm(bank[:, 7, (s * NT + i) * E:(s * NT + i + 1) * E], x2_t[:, s, t0:t0 + TILE],
                                     gate_t[:, :], start=True, stop=True)
                    ins.then_inc(S["pe_lg"], 1)
                    wait(pe, S["v_cnt"], z, 1)
                    wait(pe, S["a_h"], z, -2)
                    mm(bank[:, 6, 0:L], sw1[:, :], x2_t[:, 0, :], start=True, stop=True)
                    wait(pe, S["v_da"], z, -1)
                    wait(pe, S["v_m3a"], z, 1)
                    mm(bank[:, 0, 0:L], sw3[:, :], x2_t[:, 0, :], start=True, stop=True).then_inc(S["pe_ffa"], 1)
                    wait(pe, S["a_pa"], z, -1)
                    wait(pe, S["a_sib"], z, 1)
                    mm(bank[:, 1, 0:L], sw1[:, :], x2_t[:, 1, :], start=True, stop=True)
                    wait(pe, S["v_db"], z, -1)
                    wait(pe, S["v_m3b"], z, 1)
                    mm(bank[:, 2, 0:L], sw3[:, :], x2_t[:, 1, :], start=True, stop=True).then_inc(S["pe_ffb"], 1)
                if y.runs():
                    for s, (src, done, free) in enumerate((("v_tota", "pe_woa", "a_x2ta"), ("v_totb", "pe_wob", "a_x2tb"))):
                        wait(pe, S[src], y)
                        wait(pe, S[free], y, 1)
                        for i, (t0, _) in enumerate(TILES):
                            ins = mm(bank[:, 4 + s, i * D:(i + 1) * D], tot[:, s, t0:t0 + TILE], wo[:, :],
                                     start=True, stop=True)
                        ins.then_inc(S[done], 1)
                if k.runs():
                    wait(pe, S["a_xh"], k)
                    wait(pe, S["a_pb"], k, 1)
                    wait(pe, S["a_lg"], k, 2)
                    for s, b in enumerate((3, 7)):
                        for i, (t0, nt) in enumerate(TILES):
                            ins = tr(bank[:, b, t0:t0 + nt], xh[0:nt, k.u, s * NT + i, :], ident[0:nt, 0:nt])
                    ins.then_inc(S["pe_tx"], 1)
                    wait(pe, S["a_xta"], k)
                    wait(pe, S["a_xtb"], k)
                    wait(pe, S["a_h"], k)
                    wait(pe, S["a_sia"], k, 2)
                    wait(pe, S["v_da"], k, 1)
                    wait(pe, S["v_m3a"], k, 2)
                    for b, w, done in ((6, wk, "pe_k"), (0, wq, "pe_q")):
                        for s in range(2):
                            ins = mm(bank[64 * s:64 * s + 64, b, 0:L], w[:, :], x_t[:, k.u, s, :], start=True, stop=True)
                        ins.then_inc(S[done], 1)
                    wait(pe, S["a_pa"], k, 1)
                    wait(pe, S["a_sib"], k, 2)
                    wait(pe, S["v_db"], k, 1)
                    wait(pe, S["v_m3b"], k, 2)
                    for s, done in enumerate(("pe_va", "pe_vb")):
                        for i, (t0, _) in enumerate(TILES):
                            ins = mm(bank[:, 1 + s, i * D:(i + 1) * D], x_t[:, k.u, s, t0:t0 + TILE], wv[:, :],
                                     start=True, stop=True)
                        ins.then_inc(S[done], 1)
                    for s, (b, done) in enumerate(((3, "pe_ga"), (7, "pe_gb"))):
                        ins = mm(bank[:, b, 0:L], wg[:, :], x_t[:, k.u, s, :], start=True, stop=True)
                        ins.then_inc(S[done], 1)
                if z.runs():
                    for s, (done, g, used) in enumerate((("pe_oa", "v_m3a", "v_h2a"), ("pe_ob", "v_m3b", "v_h2b"))):
                        wait(pe, S[g], z)
                        wait(pe, S[used], z, -1)
                        for i, (t0, _) in enumerate(TILES):
                            ins = mm(bank[:, 4 + s, i * D:(i + 1) * D], su[:, s, t0:t0 + TILE], sw2[:, :],
                                     start=True, stop=True)
                        ins.then_inc(S[done], 1)
                    wait(pe, S["v_both"], z)
                    wait(pe, S["a_thk"], z, -2)
                    wait(pe, S["a_sia"], z)
                    flat = both[:, :, :].rearrange("p t e -> p (t e)")
                    n = 2 * NT + 1
                    mm(bank[:, 6, 0:n * E], below[:, :], flat, start=True, stop=False)
                    for i in range(2 * NT):
                        nt = TILES[i % NT][1]
                        src = both[0:nt, i:i + 1, :].to_broadcast([nt, n - 1 - i, E])
                        ins = mm(bank[:, 6, (i + 1) * E:n * E], ones[0:nt, :], src, start=False, stop=(i == 2 * NT - 1))
                    ins.then_inc(S["pe_pf"], 1)

            steps(pe, body)

            def expert(n, m, j):
                u = m % 2
                later = j is not None
                pe.wait_ge(e_load[u], (j + 1) * 64 if later else 64)
                if later:
                    pe.wait_ge(X["e_xt"], n - 1)
                for i in range(4):
                    ins = tr(bank[:, u, i * TILE:(i + 1) * TILE], rows[:, u, i, 0:D], ident)
                ins.then_inc(X["e_tr"], 1)
                pe.wait_ge(X["e_xt"], n + 1)
                if later:
                    pe.wait_ge(X["e_g"], n - 1)
                for i in range(2):
                    for e in range(2):
                        ins = mm(bank[64 * e:64 * e + 64, 2 + u, i * CAP:(i + 1) * CAP], w13[:, u, i, e * FH:(e + 1) * FH],
                                 xe_t[:, u, e * CAP:(e + 1) * CAP], start=True, stop=True)
                ins.then_inc(X["e_z"], 1)
                pe.wait_ge(X["e_g"], n + 1)
                if later:
                    pe.wait_ge(X["e_yv"], n - 1)
                for i in range(2):
                    for e in range(2):
                        r = slice(64 * e, 64 * e + 64)
                        ins = mm(bank[:, 4 + 2 * e + u, i * D:(i + 1) * D], ge[r, u, i * TILE:(i + 1) * TILE],
                                 w2[r, u, :], start=True, stop=True)
                ins.then_inc(X["e_y0"], 1)

            for n in range(2):
                expert(n, n, None)
            with pe.Fori(1, E // 4) as j:
                for n in range(2):
                    expert(j * 2 + n, n, j)

        @block.vector
        def _(dve):
            vv = nc.vector
            TS, TT, STT = vv.tensor_scalar, vv.tensor_tensor, vv.scalar_tensor_tensor
            chain = [0]

            def link(ins):
                chain[0] += 1
                ins.then_inc(s_zero, 1)
                dve.wait_ge(s_zero, chain[0])

            vv.memset(w_pad[:, SHIFT - 1, (COPIES - 1) * CP:KROWS], 0.0)
            vv.memset(xin[:, :, :, 0:P], 0.0).then_inc(s_pad, 1)
            vv.memset(h_t[:, :, :, NIMG:2 * TILE], 0.0)
            vv.memset(both[:, 2 * NT, :], 0.0)
            vv.memset(carry[:, 1, :], 0.0)
            vv.memset(ones[:, :], 1.0)
            vv.memset(half_pi[:, :], float(np.pi / 2))
            for i in range(4):
                vv.memset(ecur[:, 1, i:i + 1], float(i // 2 - 2))
            link(vv.memset(feat[:, :], 0.0))
            dve.wait_ge(s_const, 16)
            dve.wait_ge(s_wload, 16 * N_W)
            dve.wait_ge(s_small, 16 * 13)
            vv.tensor_copy(below[:, :], cst("below"))
            TS(tokn[:, 1, :], cst("tok"), -2.0 * L, None, ALU.add)
            for n in range(COPIES):
                cols = min(SHIFT, P - n * SHIFT)
                vv.tensor_copy(w_pad[:, 0:cols, n * CP:(n + 1) * CP],
                               w_raw[:, :, n * SHIFT:n * SHIFT + cols].rearrange("h a b -> h b a"))
            vv.tensor_scalar(bg_half[:, :], bg_col[:, :], 0.5, None, ALU.mult)
            link(vv.reduce_max(wcol[:, 0:1], setw[:, :], AX.X))
            vv.tensor_scalar(setx[:, 0:SETS], setw[:, :], wcol[:, 0:1], None, ALU.subtract).then_inc(s_pre_v, 1)
            l_row = cst("pos", 40)
            link(TS(ph[:, 0, :], l_row, freq[:, :], TWO_PI, ALU.mult, ALU.mult))
            link(TS(ph[:, 1, :], ph[:, 0, :], float(1 / (2 * np.pi)), None, ALU.mult))
            link(TS(ph[:, 2, :], ph[:, 1, :], ROUND, None, ALU.add))
            link(TS(ph[:, 1, :], ph[:, 2, :], -ROUND, None, ALU.add))
            link(STT(ph[:, 2, :], ph[:, 1, :], -TP1, ph[:, 0, :], ALU.mult, ALU.add))
            link(STT(ph[:, 3, :], ph[:, 1, :], -TP2, ph[:, 2, :], ALU.mult, ALU.add))
            link(STT(ph[:, 2, :], ph[:, 1, :], -TP3, ph[:, 3, :], ALU.mult, ALU.add))
            link(TS(ph[:, 0, :], ph[:, 2, :], cst("dpos", 40), None, ALU.subtract))
            link(STT(ph[:, 3, :], ph[:, 0, :], -1.0, ph[:, 0, :], ALU.mult, ALU.max))
            link(TS(ph[:, 2, :], ph[:, 3, :], -1.0, float(np.pi / 2), ALU.mult, ALU.add))
            TS(ph[:, 1, :], ph[:, 2, :], -PI_LOW, PI_LOW, ALU.max, ALU.min).then_inc(s_pre_v, 1)
            dve.wait_ge(s_pre_a, 2)
            link(vv.reciprocal(wcol[:, 3:4], wcol[:, 1:2]))
            link(TS(setx[:, 2 * SETS:3 * SETS], setx[:, SETS:2 * SETS], wcol[:, 3:4], None, ALU.mult))
            link(TT(setx[:, 3 * SETS:4 * SETS], setx[:, 2 * SETS:3 * SETS], cst("sel"), ALU.mult))
            link(vv.reduce_sum(wcol[:, 4:5], setx[:, 3 * SETS:4 * SETS], AX.X))
            TS(wn[:, :], cst("invn"), wcol[:, 4:5], None, ALU.mult)
            link(TS(wcol[:, 5:6], wcol[:, 2:3], 1.0, None, ALU.add))
            link(vv.reciprocal(wcol[:, 6:7], wcol[:, 5:6]))
            dve.wait_ge(s_pre_pe, 2)
            for m in range(SHIFT):
                vv.tensor_copy(w_tok[:, m, :], bank[0:KROWS, m // 4, (m % 4) * D:(m % 4 + 1) * D])
            TS(pos_t[:, 1:NIMG], bank[:, 4, 1:NIMG], b_col[:, :], None, ALU.add)
            TS(pos_t[:, 0:1], bank[:, 4, 0:1], tok_col[:, :], None, ALU.add)
            vv.tensor_copy(gate_t[:, :], bank[:, 5, 0:E])
            dve.wait_ge(s_pre_pe, 3)
            link(STT(pos_a[:, 0:L], bank[:, 6, 0:L], wcol[:, 6:7], cst("maskn")[:, 0:L], ALU.mult, ALU.mult))
            link(STT(pos_a[:, L:2 * L], bank[:, 7, 0:L], wcol[:, 6:7], cst("maskn")[:, L:2 * L], ALU.mult, ALU.mult))
            dve.wait_ge(s_init, 16 * (SLOTS // 1024 + 1))
            vv.memset(wcol[:, 7:8], 0.0).then_inc(s_setup, 1)

            def variance(q, st, ms, dm, m2, dd, vs, ve, n):
                mean, square = (1, 4), (2, 5)
                wait(dve, S["v_st" + n], q)
                TT(ms[:, q.u], st[:, q.u, :, mean[0]], st[:, q.u, :, mean[1]], ALU.add)
                TT(dm[:, :], st[:, q.u, :, mean[0]], st[:, q.u, :, mean[1]], ALU.subtract)
                TT(m2[:, :], st[:, q.u, :, square[0]], st[:, q.u, :, square[1]], ALU.add).then_inc(S["v_mm" + n], 1)
                wait(dve, S["v_mm" + n], q)
                TT(dd[:, :], dm[:, :], dm[:, :], ALU.mult).then_inc(S["v_dd" + n], 1)
                wait(dve, S["v_dd" + n], q)
                STT(vs[:, :], dd[:, :], D / 4.0, m2[:, :], ALU.mult, ALU.add).then_inc(S["v_vs" + n], 1)
                wait(dve, S["v_vs" + n], q)
                TS(ve[:, q.u], vs[:, :], 1.0 / D, LN_EPS, ALU.mult, ALU.add).then_inc(S["v_ve" + n], 1)

            def bias_scale(q, ms, rs, nb, s_rs, s_nb):
                wait(dve, s_rs, q)
                STT(nb[:, q.u, :], ms[:, q.u, :], -0.5, rs[:, q.u, :], ALU.mult, ALU.mult).then_inc(s_nb, 1)

            def mix(y, s, pt, ap, d, e, f, used):
                wait(dve, S[pt], y)
                wait(dve, S[ap], y)
                TT(dif[:, s, :], bank[:, 2 * s, 0:L], pos_o[:, s, :], ALU.subtract).then_inc(S[d], 1)
                if s == 0:
                    wait(dve, S["a_gb"], y)
                wait(dve, S[d], y)
                STT(gdif[:, s, :], gt[:, y.u, s, :], 1.0, dif[:, s, :], ALU.add, ALU.mult).then_inc(S[e], 1)
                wait(dve, S[e], y)
                wait(dve, S[used], y, 1)
                STT(tot[:, s, :], pos_o[:, s, :], 2.0, gdif[:, s, :], ALU.mult, ALU.add).then_inc(S[f], 1)

            def body(k):
                y, z = k.back(1), k.back(2)
                if k.runs():
                    wait(dve, S["pe_tok"], k)
                    wait(dve, S["pe_th"], k, 2)
                    for s in range(2):
                        ins = TT(h_t[:, k.u, s, 0:NIMG], bank[:, s, 0:NIMG], pos_t[:, :], ALU.add)
                    ins.then_inc(S["v_ht"], 1)
                if y.runs():
                    wait(dve, S["pe_sc"], y)
                    wait(dve, S["pe_tb"], y, 2)
                    for s, done in enumerate(("v_ma", "v_mb")):
                        TT(a_t[:, y.u, s, :, :], bank[:, 2 + 2 * s:4 + 2 * s, 0:L],
                           cst("mask").rearrange("p (a l) -> p a l", a=2), ALU.mult).then_inc(S[done], 1)
                if k.runs():
                    wait(dve, S["a_h"], k)
                    wait_dma(dve, s_txt, k, 1)
                    for i in range(2 * NT):
                        ins = vv.bn_stats(st1[:, k.u, i, :], h[:, k.u, i // NT, i % NT, :])
                    ins.then_inc(S["v_st1"], 1)
                    variance(k, st1, ms1, dm1, m21, dd1, vs1, ve1, "1")
                if y.runs():
                    mix(y, 0, "pe_ta", "a_pa", "v_da", "v_ea", "v_tota", "pe_woa")
                if k.runs():
                    bias_scale(k, ms1, rs1, nb1, S["p_rs1"], S["v_nb1"])
                if y.runs():
                    mix(y, 1, "pe_tb", "a_pb", "v_db", "v_eb", "v_totb", "pe_wob")
                if z.runs():
                    for s, (a, f, done, prev) in enumerate((("a_sia", "pe_ffa", "v_m3a", "pe_oa"),
                                                            ("a_sib", "pe_ffb", "v_m3b", "pe_ob"))):
                        wait(dve, S[prev], z, 1)
                        wait(dve, S[a], z)
                        TT(su[:, s, :], sl[:, s, :], bank[:, 0 if s == 0 else 2, 0:L], ALU.mult).then_inc(S[done], 1)
                    wait(dve, S["v_tok"], z, 1)
                    wait(dve, S["a_lg"], z)
                    TS(tokn[:, z.u, :], tokn[:, 1 - z.u, :], 2.0 * L, None, ALU.add).then_inc(S["v_tok"], 1)
                    for i in range(2 * NT):
                        ins = vv.max(top[:, i, :], lg[:, i, :])
                    ins.then_inc(S["v_max"], 1)
                    wait(dve, S["a_small"], z, 1)
                    wait(dve, S["v_max"], z)
                    TS(lo[:, :, :], top[:, :, 0:2], -1.0, None, ALU.min)
                    TS(hi[:, :, :], top[:, :, 0:2], -1.0, None, ALU.max).then_inc(S["v_lohi"], 1)
                    for i in range(2 * NT):
                        ins = vv.max_index(topi[:, i, :], top[:, i, :], lg[:, i, :])
                    ins.then_inc(S["v_imax"], 1)
                    wait(dve, S["v_imax"], z)
                    vv.tensor_copy(idx[:, :, :].rearrange("p r t -> p t r"), topi[:, :, 0:2]).then_inc(S["v_idx"], 1)
                    wait(dve, S["v_idx"], z)
                    wait(dve, S["v_pick"], z, 1)
                    for r in range(2):
                        ins = TT(hot[:, r, :, :], cst("iota").rearrange("p (o e) -> p o e", o=1).to_broadcast([128, 2 * NT, E]),
                                 idx[:, r, :].rearrange("p (t o) -> p t o", o=1).to_broadcast([128, 2 * NT, E]), ALU.is_equal)
                    ins.then_inc(S["v_hot"], 1)
                    wait(dve, S["v_hot"], z)
                    wait(dve, S["pe_pf"], z, 1)
                    TT(both[:, 0:2 * NT, :], hot[:, 0, :, :], hot[:, 1, :, :], ALU.add).then_inc(S["v_both"], 1)
                if y.runs():
                    wait(dve, S["p_hb"], y)
                    wait(dve, S["v_h2b"], y, 1)
                    TT(hbo[:, :, :], hb[:, y.u, :, :],
                       bo_row[:, :].rearrange("p (o d) -> p o d", o=1).to_broadcast([128, 2 * NT, D]), ALU.add)\
                        .then_inc(S["v_hbo"], 1)
                    wait(dve, S["v_hbo"], y)
                    wait(dve, S["v_finb"], y, 2)
                    wait(dve, S["a_x2"], y, 2)
                    for s, (done, ready) in enumerate((("v_h2a", "pe_woa"), ("v_h2b", "pe_wob"))):
                        wait(dve, S[ready], y)
                        TT(h2[:, y.u, s * NT:(s + 1) * NT, :], bank[:, 4 + s, 0:NT * D].rearrange("p (t d) -> p t d", d=D),
                           hbo[:, s * NT:(s + 1) * NT, :], ALU.add).then_inc(S[done], 1)
                if k.runs():
                    for s, (done, ready, prev) in enumerate((("v_va", "pe_va", "pe_pa"), ("v_vb", "pe_vb", "pe_pb"))):
                        wait(dve, S[ready], k)
                        wait(dve, S[prev], k, 2)
                        TT(v[:, k.u, s, :, :], bank[:, 1 + s, 0:NT * D].rearrange("p (t d) -> p t d", d=D),
                           bv_row[:, :].rearrange("p (o d) -> p o d", o=1).to_broadcast([128, NT, D]), ALU.add)\
                            .then_inc(S[done], 1)
                if y.runs():
                    wait(dve, S["v_h2b"], y)
                    for i in range(2 * NT):
                        ins = vv.bn_stats(st2[:, y.u, i, :], h2[:, y.u, i, :])
                    ins.then_inc(S["v_st2"], 1)
                    variance(y, st2, ms2, dm2, m22, dd2, vs2, ve2, "2")
                if k.runs():
                    wait(dve, S["a_sin"], k)
                    wait(dve, S["pe_sc"], k, 2)
                    TT(qn[:, k.u, :], kq[:, k.u, 1, :], wn[:, :], ALU.mult).then_inc(S["v_qn"], 1)
                if z.runs():
                    wait(dve, S["a_small"], z)
                    vv.reciprocal(rlo[:, :, :], lo[:, :, :]).then_inc(S["v_rlo"], 1)
                    wait(dve, S["v_rlo"], z)
                    STT(sgl[:, :, :], rlo[:, :, :], 0.5 / SIG_M1, slo[:, :, :], ALU.mult, ALU.mult).then_inc(S["v_sgl"], 1)
                    wait(dve, S["v_sgl"], z)
                    STT(sg[:, :, :], thi[:, :, :], 1.0, sgl[:, :, :], ALU.add, ALU.mult).then_inc(S["v_sg"], 1)
                    wait(dve, S["v_sg"], z)
                    TT(ssum[:, :], sg[:, :, 0], sg[:, :, 1], ALU.add).then_inc(S["v_ssum"], 1)
                    wait(dve, S["v_ssum"], z)
                    TS(ssum[:, :], ssum[:, :], 1e-20, None, ALU.add).then_inc(S["v_seps"], 1)
                    wait(dve, S["v_seps"], z)
                    vv.reciprocal(sinv[:, :], ssum[:, :]).then_inc(S["v_sinv"], 1)
                    wait(dve, S["v_sinv"], z)
                    for r in range(2):
                        STT(xs[:, z.u, :, D + r], sg[:, :, r], ROUTE, sinv[:, :], ALU.mult, ALU.mult)
                    vv.tensor_copy(xs[:, z.u, :, D + 2], idx[:, 0, :])
                    wait(dve, S["v_tok"], z)
                    vv.tensor_copy(xs[:, z.u, :, D + 3], tokn[:, z.u, :]).then_inc(S["v_meta"], 1)
                if y.runs():
                    bias_scale(y, ms2, rs2, nb2, S["p_rs2"], S["v_nb2"])
                if z.runs():
                    wait_dma(dve, s_store, z, NT, 2)
                    for s, (done, ready) in enumerate((("v_fina", "pe_oa"), ("v_finb", "pe_ob"))):
                        wait(dve, S[ready], z)
                        TT(fin[:, z.u, s * NT:(s + 1) * NT, :], bank[:, 4 + s, 0:NT * D].rearrange("p (t d) -> p t d", d=D),
                           h2[:, z.u, s * NT:(s + 1) * NT, :], ALU.add).then_inc(S[done], 1)
                    wait(dve, S["pe_pf"], z)
                    prev, now = carry[:, 1 - z.u, :], carry[:, z.u, :]
                    TT(cnt[:, :, :], bank[:, 6, 0:2 * NT * E].rearrange("p (t e) -> p t e", e=E),
                       prev.rearrange("p (o e) -> p o e", o=1).to_broadcast([128, 2 * NT, E]), ALU.add)
                    TT(now, bank[:, 6, 2 * NT * E:(2 * NT + 1) * E], prev, ALU.add).then_inc(S["v_cnt"], 1)
                    wait(dve, S["v_cnt"], z)
                    for r in range(2):
                        ins = TT(picked[:, r, :, :], hot[:, r, :, :], cnt[:, :, :], ALU.mult)
                    ins.then_inc(S["v_pick"], 1)
                    wait(dve, S["v_pick"], z)
                    vv.reduce_sum(place[:, :, :].rearrange("p r t -> p (r t)"),
                                  picked[:, :, :, :].rearrange("p r t e -> p (r t) e"), AX.X).then_inc(S["v_place"], 1)
                    wait(dve, S["v_place"], z)
                    TS(over[:, :, :], place[:, :, :], CAP - 0.5, FAR, ALU.is_gt, ALU.mult)
                    STT(slotf[:, :, :], idx[:, :, :], float(CAP), place[:, :, :], ALU.mult, ALU.add).then_inc(S["v_over"], 1)
                    wait(dve, S["v_over"], z)
                    wait_dma(dve, s_scat, z, 4 * NT, 2)
                    TT(slot[:, z.u, :, :], slotf[:, :, :], over[:, :, :], ALU.add).then_inc(S["v_sloti"], 1)

            steps(dve, body)

            def expert(n, m, j):
                u = m % 2
                later = j is not None
                dve.wait_ge(e_load[u], (j + 1) * 64 if j is not None else 64)
                TS(ecur[:, u, :], ecur[:, 1 - u, :], 2.0, None, ALU.add).then_inc(X["e_cur"], 1)
                TT(ewd[:, :], rows[:, u, :, D], rows[:, u, :, D + 1], ALU.subtract).then_inc(X["e_wd"], 1)
                dve.wait_ge(X["e_cur"], n + 1)
                TT(esel[:, :], rows[:, u, :, D + 2], ecur[:, u, :], ALU.is_equal).then_inc(X["e_sel"], 1)
                dve.wait_ge(X["e_wd"], n + 1)
                dve.wait_ge(X["e_sel"], n + 1)
                TT(ewm[:, :], esel[:, :], ewd[:, :], ALU.mult).then_inc(X["e_wm"], 1)
                dve.wait_ge(X["e_wm"], n + 1)
                TT(ew[:, u, :], ewm[:, :], rows[:, u, :, D + 1], ALU.add).then_inc(X["e_w"], 1)
                if later:
                    dve.wait_ge(e_add[0], (n - 1) * 32)
                    dve.wait_ge(e_add[1], (n - 1) * 32)
                vv.tensor_copy(etok[:, u, :], rows[:, u, :, D + 3]).then_inc(X["e_tokn"], 1)
                dve.wait_ge(X["e_silu"], n + 1)
                TT(ge[:, u, :], ae[:, u, :], bank[:, 2 + u, CAP:2 * CAP], ALU.mult).then_inc(X["e_g"], 1)
                dve.wait_ge(X["e_w"], n + 1)
                dve.wait_ge(X["e_y0"], n + 1)
                for i in range(4):
                    e = i // 2
                    ins = TS(ye[:, u, i, :], bank[:, 4 + 2 * e + u, (i % 2) * D:(i % 2 + 1) * D], ew[:, u, i:i + 1], None,
                             ALU.mult)
                ins.then_inc(X["e_yv"], 1)

            for n in range(2):
                expert(n, n, None)
            with dve.Fori(1, E // 4) as j:
                for n in range(2):
                    expert(j * 2 + n, n, j)


_INS = ['x', 'txt', 'L0_tok_W', 'L0_tok_b', 'L0_tok_token', 'L0_tok_pos', 'L0_attn_Wk', 'L0_attn_bk', 'L0_attn_Wq',
        'L0_attn_bq', 'L0_attn_Wv', 'L0_attn_bv', 'L0_attn_set_weights', 'L0_attn_pos_freqs', 'L0_attn_Wg',
        'L0_attn_bg', 'L0_attn_pos_weight', 'L0_attn_Wo', 'L0_attn_bo', 'L0_ffn_gate_w', 'L0_ffn_w1', 'L0_ffn_w3',
        'L0_ffn_w2', 'L0_ffn_sw1', 'L0_ffn_sw3', 'L0_ffn_sw2']


def build(nc, arrays):
    t = {n: nc.dram_tensor(f"in_{n}", a.shape, F32, kind="ExternalInput").ap() for n, a in arrays.items()}
    out = nc.dram_tensor("out_rows", (TOKENS + CAP, D), F32, kind="ExternalOutput").ap()
    slots_d = nc.dram_tensor("slot_rows", (SLOTS, ROW), F32, kind="Internal").ap()
    program(nc, t, out, slots_d)


def kernel(**inputs):
    import concourse.bacc as _bacc
    from concourse.bass_utils import run_bass_kernel_spmd as _run

    nc = _bacc.Bacc("TRN2", target_bir_lowering=False, num_devices=1)
    arrays = {n: np.ascontiguousarray(inputs[n]) for n in _INS}
    arrays["consts"] = constants()
    build(nc, arrays)
    r = _run(nc, [{f"in_{n}": a for n, a in arrays.items()}], core_ids=[0])
    return r.results[0]["out_rows"][0:TOKENS].reshape(B, L, D)
```

```python
from contextlib import ExitStack

import numpy as np

import concourse.bass as bass
from concourse import mybir

F32 = mybir.dt.float32
BF16 = mybir.dt.bfloat16
I32 = mybir.dt.int32
U32 = mybir.dt.uint32
ALU = mybir.AluOpType
ACT = mybir.ActivationFunctionType
AX = mybir.AxisListType

B, C, H, G = 128, 3, 196, 14
P = H // G
D = 128
NIMG = G * G + 1
NTXT = 128
L = NIMG + NTXT
SETS, PLANES = 4, 8
HF = SETS * PLANES
E, TOPK, CAP, FH = 64, 2, 256, 64
PAIRS = B // 2
TILE = 128
TILES = [(0, TILE), (TILE, NIMG - TILE), (NIMG, NTXT)]
NT = len(TILES)
T1 = TILES[1][1]
CP = C * P
XW = P + G * H
COPIES = 3
SHIFT = 5
KROWS = COPIES * CP
ROW = D + 4
SLOTS = E * CAP
TOKENS = B * L
LN_EPS = 1e-5
ROUTE = 2.5
SIG_M1 = 1.0 / (1.0 + float(np.exp(1.0)))
PI_LOW = 3.1415925
TWO_PI = float(np.float32(2.0) * np.float32(np.pi))
TP1 = 6.28125
TP2 = float(np.float32(np.round((2 * np.pi - TP1) * 2**20) / 2**20))
TP3 = float(np.float32(2 * np.pi - TP1 - TP2))
ROUND = 1.5 * 2.0**23
FAR = 1.0e6

CONST = {}
_at = 0
for _n, _w in (("ident", 128), ("below", 128), ("mask", 2 * L), ("maskn", 2 * L), ("invn", L), ("iota", E),
               ("pos", L), ("tok", 2 * NT), ("sel", SETS), ("delta", 1), ("dpos", 1), ("dump", 8)):
    CONST[_n] = (_at, _at + _w)
    _at += _w
CW = _at


def constants():
    t = np.zeros((128, CW), np.float32)

    def put(name, v):
        a, b = CONST[name]
        t[:, a:b] = v

    p = np.arange(128)[:, None]
    put("ident", np.eye(128))
    put("below", p < np.arange(128)[None, :])
    l = np.arange(L)[None, :]
    invn = (0.5 / np.sqrt((l + 1) * PLANES)).astype(np.float32)
    m0 = p <= l
    q1 = np.arange(TILE, L)[None, :]
    m1 = (p + TILE <= q1) & (p < T1)
    q2 = np.arange(NIMG, L)[None, :]
    m2 = p + NIMG <= q2
    mask = np.concatenate([m0, m1, m2], 1).astype(np.float32)
    n = np.concatenate([invn[:, 0:L], invn[:, TILE:L], invn[:, NIMG:L]], 1)
    put("mask", mask)
    put("maskn", mask * n)
    put("invn", invn)
    put("iota", np.arange(E)[None, :])
    put("pos", l)
    put("tok", np.concatenate([s * L + t0 + p for s in range(2) for t0, _ in TILES], 1))
    put("sel", (p % HF) // PLANES == np.arange(SETS)[None, :])
    put("delta", -0.5 * (p % (2 * HF) < HF))
    put("dpos", np.pi / 2 * (p < PLANES))
    put("dump", TOKENS + p + 128 * (np.arange(8)[None, :] % 2))
    return t


class Pair:

    def __init__(self, twice, j, c):
        self.twice, self.j, self.c = twice, j, c

    def back(self, n):
        return Pair(self.twice, self.j, self.c - n)

    @property
    def u(self):
        return self.c % 2

    def runs(self):
        return self.j is not None or 0 <= self.c < PAIRS

    def count(self):
        return self.c + 1 if self.j is None else self.twice + (self.c + 1)

    def uses(self):
        return self.c // 2 + 1 if self.j is None else self.j + (self.c // 2 + 1)

    def number(self):
        return self.c if self.j is None else self.twice + self.c


def first(pair):
    return pair.j is None and pair.c == 0


SKEW = 3
HEAD = 4
TAIL0 = PAIRS


def steps(eng, body):
    for k in range(HEAD):
        body(Pair(None, None, k))
    with_loop = (TAIL0 - HEAD) // 2
    assert HEAD + 2 * with_loop == TAIL0 and HEAD % 2 == 0
    with eng.Fori(HEAD // 2, HEAD // 2 + with_loop) as j:
        twice = j * 2
        for u in range(2):
            body(Pair(twice, j, u))
    for k in range(TAIL0, TAIL0 + SKEW):
        body(Pair(None, None, k))


def wait(eng, sem, pair, back=0):
    q = pair.back(back)
    if q.j is not None or 0 <= q.c < PAIRS:
        eng.wait_ge(sem, q.count())


def wait_dma(eng, sems, pair, each, back=0):
    q = pair.back(back)
    if q.j is not None or q.c >= 0:
        eng.wait_ge(sems[q.u], q.uses() * (16 * each))


def program(nc, t, out, slots_d):
    ctx = ExitStack()
    with ctx:
        def sb(name, shape, dt=F32):
            return ctx.enter_context(nc.sbuf_tensor(name, shape, dt))

        def sem(name):
            return ctx.enter_context(nc.semaphore(name))

        def sems(name):
            return [sem(f"{name}{u}") for u in range(2)]

        const = sb("const", [128, CW])

        def cst(name, p=128):
            a, b = CONST[name]
            return const[0:p, a:b]

        ident = cst("ident")
        w_tok = sb("w_tok", [KROWS, SHIFT, D])
        pos_raw = sb("pos_raw", [128, 2, D])
        tok_col = sb("tok_col", [D, 1])
        b_col = sb("b_col", [D, 1])
        pos_t = sb("pos_t", [D, NIMG])
        wk = sb("wk", [D, 2 * HF])
        wq = sb("wq", [D, 2 * HF])
        bk_col = sb("bk_col", [128, 1])
        bq_col = sb("bq_col", [128, 1])
        wv = sb("wv", [D, D])
        wg = sb("wg", [D, D])
        wo = sb("wo", [D, D])
        bg_col = sb("bg_col", [D, 1])
        bg_half = sb("bg_half", [D, 1])
        bv_row = sb("bv_row", [128, D])
        bo_row = sb("bo_row", [128, D])
        gate_raw = sb("gate_raw", [E, D])
        gate_t = sb("gate_t", [D, E])
        sw1 = sb("sw1", [D, D])
        sw3 = sb("sw3", [D, D])
        sw2 = sb("sw2", [D, D])
        below = sb("below", [128, 128], BF16)
        ones = sb("ones", [128, 128], BF16)
        setw = sb("setw", [128, SETS])
        setx = sb("setx", [128, 4 * SETS])
        wcol = sb("wcol", [128, 8])
        wn = sb("wn", [128, L])
        freq = sb("freq", [40, 1])
        feat = sb("feat", [40, L])
        pos_a = sb("pos_a", [128, 2 * L])
        half_pi = sb("half_pi", [128, 1])
        pw_col = sb("pw_col", [128, 1])
        neg_half = sb("neg_half", [128, 2 * NT])

        xin = sb("xin", [128, 2, 2, XW])
        h_t = sb("h_t", [D, 2, 2, 2 * TILE])
        h = sb("h", [128, 2, 2, NT, D])
        xh = sb("xh", [128, 2, 2 * NT, D])
        st1 = sb("st1", [128, 2, 2 * NT, 6])
        ms1 = sb("ms1", [128, 2, 2 * NT])
        dm1 = sb("dm1", [128, 2 * NT])
        m21 = sb("m21", [128, 2 * NT])
        dd1 = sb("dd1", [128, 2 * NT])
        vs1 = sb("vs1", [128, 2 * NT])
        ve1 = sb("ve1", [128, 2, 2 * NT])
        rs1 = sb("rs1", [128, 2, 2 * NT])
        nb1 = sb("nb1", [128, 2, 2 * NT])
        hb = sb("hb", [128, 2 * NT, D])
        hbo = sb("hbo", [128, 2, 2 * NT, D])
        x_t = sb("x_t", [D, 2, 2, L])
        ph_t = sb("ph_t", [128, 2, 2, L])
        ph_a = sb("ph_a", [128, 2, 2, L])
        kq = sb("kq", [128, 2, 2, L])
        qn = sb("qn", [128, 2, L])
        v = sb("v", [128, 2, 2, NT, D])
        gt = sb("gt", [D, 2, 2, L])
        a_t = sb("a_t", [128, 2, 2, 2, L])
        pos_o = sb("pos_o", [D, 2, L])
        dif = sb("dif", [D, 2, L])
        gdif = sb("gdif", [D, 2, L])
        tot = sb("tot", [D, 2, L])
        h2 = sb("h2", [128, 2, 2 * NT, D])
        st2 = sb("st2", [128, 2, 2 * NT, 6])
        ms2 = sb("ms2", [128, 2, 2 * NT])
        dm2 = sb("dm2", [128, 2 * NT])
        m22 = sb("m22", [128, 2 * NT])
        dd2 = sb("dd2", [128, 2 * NT])
        vs2 = sb("vs2", [128, 2 * NT])
        ve2 = sb("ve2", [128, 2, 2 * NT])
        rs2 = sb("rs2", [128, 2, 2 * NT])
        nb2 = sb("nb2", [128, 2, 2 * NT])
        xs = sb("xs", [128, 2, 2 * NT, ROW])
        x2_t = sb("x2_t", [D, 2, L])
        lg_t = sb("lg_t", [2 * E, L])
        lg = sb("lg", [128, 2 * NT, E])
        top = sb("top", [128, 2 * NT, 8])
        topi = sb("topi", [128, 2 * NT, 8], U32)
        idx = sb("idx", [128, 2, 2 * NT])
        hot = sb("hot", [128, 2, 2 * NT, E], BF16)
        both = sb("both", [128, 2 * NT + 1, E], BF16)
        cnt = sb("cnt", [128, 2 * NT, E], BF16)
        picked = sb("picked", [128, 2, 2 * NT, E], BF16)
        place = sb("place", [128, 2, 2 * NT])
        over = sb("over", [128, 2, 2 * NT])
        slotf = sb("slotf", [128, 2, 2 * NT])
        slot = sb("slot", [128, 2, 2, 2 * NT], I32)
        carry = sb("carry", [128, 2, E])
        tokn = sb("tokn", [128, 2, 2 * NT])
        lo = sb("lo", [128, 2 * NT, 2])
        hi = sb("hi", [128, 2 * NT, 2])
        slo = sb("slo", [128, 2 * NT, 2])
        thi = sb("thi", [128, 2 * NT, 2])
        rlo = sb("rlo", [128, 2 * NT, 2])
        sgl = sb("sgl", [128, 2 * NT, 2])
        sg = sb("sg", [128, 2 * NT, 2])
        ssum = sb("ssum", [128, 2 * NT])
        sinv = sb("sinv", [128, 2 * NT])
        sl = sb("sl", [D, 2, L])
        su = sb("su", [D, 2, L])
        fin = sb("fin", [128, 2, 2 * NT, D])

        flat_a = a_t[:, :, :, :, :].rearrange("p u s a l -> p (u s a l)")
        w_raw = flat_a[:, 0:CP * P].rearrange("p (a b) -> p a b", b=P)
        w_pad = flat_a[:, CP * P:CP * P + SHIFT * KROWS].rearrange("p (m k) -> p m k", k=KROWS)
        ph = x_t[0:40, :, :, :].rearrange("p u s l -> p (u s) l")
        init_rows = sb("init_rows", [128, 8, ROW])

        flat_x = xin[:, :, :, :].rearrange("p u s w -> p (u s w)")
        at = [0]

        def part(*shape):
            n = int(np.prod(shape))
            a = flat_x[:, at[0]:at[0] + n]
            at[0] += n
            names = "abcd"[:len(shape)]
            return a.rearrange(f"p ({' '.join(names)}) -> p {' '.join(names)}", **dict(zip(names, shape)))

        spare = sb("spare", [128, 3])
        rows = part(2, 4, ROW)
        w13 = part(2, 2, 2 * FH)
        w2 = part(2, D)
        xe_t = part(2, 4 * TILE)
        ae = part(2, CAP)
        ge = part(2, CAP)
        ecur = sb("ecur", [128, 2, 4])
        esel = sb("esel", [128, 4])
        ewd = sb("ewd", [128, 4])
        ewm = sb("ewm", [128, 4])
        ew = sb("ew", [128, 2, 4])
        etok = sb("etok", [128, 2, 4], I32)
        ye = part(2, 4, D)

        bank = ctx.enter_context(nc.psum_tensor("bank", [128, 8, 512], F32))

        s_const, s_wload, s_init, s_small = sem("s_const"), sem("s_wload"), sem("s_init"), sem("s_small")
        s_zero = sem("s_zero")
        s_late, s_wtok = sem("s_late"), sem("s_wtok")
        s_pre_v, s_pre_a, s_pre_p, s_pre_pe = sem("s_pre_v"), sem("s_pre_a"), sem("s_pre_p"), sem("s_pre_pe")
        s_setup = sem("s_setup")
        s_xin, s_txt, s_store, s_scat = sems("s_xin"), sems("s_txt"), sems("s_store"), sems("s_scat")
        s_shift = sems("s_shift")
        s_pad = sem("s_pad")
        names = """pe_toka pe_tok pe_th pe_tx pe_k pe_q pe_va pe_vb pe_ga pe_gb pe_sc pe_ta pe_pa pe_tb pe_pb pe_woa pe_wob
            pe_tx2a pe_tx2b pe_lgt pe_lg pe_ffa pe_ffb pe_pf pe_oa pe_ob
            v_ht v_st1 v_mm1 v_dd1 v_vs1 v_ve1 v_nb1 v_m3a v_m3b v_max v_ma v_mb v_imax v_idx v_hot v_both v_lohi v_rlo v_sgl v_sg
            v_ssum v_sinv v_meta v_fina v_finb v_da v_db v_ea v_eb v_tota v_totb v_cnt v_pick v_place v_over v_slotf v_sloti
            v_carry v_tok v_va v_vb v_qn v_h2a v_h2b v_st2 v_mm2 v_dd2 v_vs2 v_ve2 v_nb2
            a_x2ta a_x2tb a_h a_lgt a_lg a_sia a_sib a_small a_xh a_pa a_pb a_xta a_xtb a_thk a_thq a_ga a_gb a_abs a_sin a_x2
            p_rs1 p_hb p_rs2 p_go p_hbo""".split()
        S = {n: sem(n) for n in names}
        enames = "e_rows e_tr e_xt e_z e_silu e_g e_y0 e_y1 e_sel e_wd e_wm e_w e_tokn e_yv e_cur e_spare0 e_spare1".split()
        X = {n: sem(n) for n in enames}
        e_load = sems("e_load")
        e_add = sems("e_add")

        block = ctx.enter_context(nc.Block())

        N_W = 6
        N_SMALL = 4
        N_LATE = 8 + 4 + 6 + 3

        colr = lambda n: t[n].rearrange("(h o) -> h o", o=1)
        row = lambda n, w: t[n].rearrange("(o h) -> o h", o=1).to_broadcast([128, w])

        @block.sync
        def _(sp):
            sp.dma_start(w_raw[:, :, :], t["L0_tok_W"].rearrange("h (a b) -> h a b", b=P)).then_inc(s_wload, 16)
            sp.dma_start(const[:, :], t["consts"]).then_inc(s_const, 16)
            sp.dma_start(pos_raw[:, 0, :], t["L0_tok_pos"][0:TILE, :]).then_inc(s_wload, 16)
            sp.dma_start(pos_raw[0:T1, 1, :], t["L0_tok_pos"][TILE:NIMG, :]).then_inc(s_wload, 16)
            sp.dma_start(tok_col[:, :], t["L0_tok_token"].rearrange("o h -> h o")).then_inc(s_wload, 16)
            sp.dma_start(b_col[:, :], t["L0_tok_b"].rearrange("(h o) -> h o", o=1)).then_inc(s_wload, 16)
            sp.dma_start(gate_raw[:, :], t["L0_ffn_gate_w"]).then_inc(s_wload, 16)

            def late_loads():
                for i in range(4):
                    sp.dma_start(bk_col[i * HF:(i + 1) * HF, :], colr("L0_attn_bk")).then_inc(s_late, 16)
                    sp.dma_start(bq_col[i * HF:(i + 1) * HF, :], colr("L0_attn_bq")).then_inc(s_late, 16)
                for i in range(2):
                    sp.dma_start(wk[:, i * HF:(i + 1) * HF], t["L0_attn_Wk"]).then_inc(s_late, 16)
                    sp.dma_start(wq[:, i * HF:(i + 1) * HF], t["L0_attn_Wq"]).then_inc(s_late, 16)
                for name, dst in (("L0_attn_Wv", wv), ("L0_attn_Wg", wg), ("L0_attn_Wo", wo), ("L0_ffn_sw1", sw1),
                                  ("L0_ffn_sw3", sw3), ("L0_ffn_sw2", sw2)):
                    sp.dma_start(dst[:, :], t[name]).then_inc(s_late, 16)
                sp.dma_start(bg_col[:, :], colr("L0_attn_bg")).then_inc(s_late, 16)
                sp.dma_start(bv_row[:, :], row("L0_attn_bv", D)).then_inc(s_late, 16)
                sp.dma_start(bo_row[:, :], row("L0_attn_bo", D)).then_inc(s_late, 16)

            def empty_slots(part):
                sp.wait_ge(s_pre_p, 3)
                init_v = slots_d.rearrange("(n i p) r -> n p i r", p=128, i=8)
                for n in range(part * SLOTS // (128 * 8 * 2), (part + 1) * SLOTS // (128 * 8 * 2)):
                    sp.dma_start(init_v[n], init_rows[:, :, :]).then_inc(s_init, 16)
                if part == 1:
                    sp.dma_start(out[TOKENS:TOKENS + CAP, :].rearrange("(i p) d -> p i d", p=128), init_rows[:, 0:2, 0:D])\
                        .then_inc(s_init, 16)

            def load(q):
                n = q.number()
                for i in range(2):
                    img = t["x"][bass.ds(n * 2 + i, 1)] if q.j is not None else t["x"][2 * q.c + i:2 * q.c + i + 1]
                    for c in range(C):
                        src = img[:, c].rearrange("o (g r) w -> r (o g) w", r=P)
                        dst = xin[c * P:(c + 1) * P, q.u, i, P:XW].rearrange("r (g w) -> r g w", w=H)
                        sp.dma_start(dst, src).then_inc(s_xin[q.u], 16)
                txt = t["txt"][bass.ds(n * 2, 2)] if q.j is not None else t["txt"][2 * q.c:2 * q.c + 2]
                return txt

            def shift(q):
                wait_dma(sp, s_xin, q, 2 * C)
                for i in range(2):
                    for n in range(1, COPIES):
                        sp.dma_start(xin[n * CP:(n + 1) * CP, q.u, i, P - n * SHIFT:XW - n * SHIFT],
                                     xin[0:CP, q.u, i, P:XW]).then_inc(s_shift[q.u], 16)

            def body(k):
                q = k
                if q.runs():
                    wait(sp, S["pe_tok"], q, 2)
                    txt = load(q)
                    wait(sp, S["a_xh"], q, 2)
                    wait(sp, S["p_hb"], q, 2)
                    sp.dma_start(h[:, q.u, :, 2, :], txt.rearrange("s p d -> p s d")).then_inc(s_txt[q.u], 16)
                if k.runs():
                    shift(k)
                if first(k):
                    late_loads()
                for part in range(2):
                    if first(k.back(part + 1)):
                        empty_slots(part)
                q = k.back(3)
                if q.runs():
                    wait(sp, S["v_fina"], q)
                    wait(sp, S["v_finb"], q)
                    n = q.number()
                    o = out[bass.ds(n * (2 * L), 2 * L), :] if q.j is not None else out[q.c * 2 * L:(q.c + 1) * 2 * L, :]
                    o = o.rearrange("(s l) d -> l s d", s=2)
                    f = fin[:, q.u, :, :].rearrange("p (s t) d -> p t s d", s=2)
                    for i, (t0, nt) in enumerate(TILES):
                        sp.dma_start(o[t0:t0 + nt], f[0:nt, i]).then_inc(s_store[q.u], 16)

            sp.wait_ge(s_pad, 1)
            steps(sp, body)
            for u in range(2):
                sp.wait_ge(s_scat[u], 16 * 4 * NT * (PAIRS // 2))
                sp.wait_ge(s_store[u], 16 * NT * (PAIRS // 2))
            rows_v = slots_d.rearrange("(a q p) r -> a p q r", p=128, q=4)
            w13_v = [t[n].rearrange("(a e) d h -> a d e h", e=2) for n in ("L0_ffn_w1", "L0_ffn_w3")]
            w2_v = t["L0_ffn_w2"].rearrange("(a e) h d -> a (e h) d", e=2)

            def fetch(a, m, j):
                u = m % 2
                if j is not None:
                    sp.wait_ge(X["e_yv"], a - 1)
                one = lambda v: (v[bass.ds(a, 1)] if j is not None else v[a:a + 1])
                sp.dma_start(rows[:, u, :, :], one(rows_v).rearrange("o p q r -> (o p) q r")).then_inc(e_load[u], 16)
                for i in range(2):
                    sp.dma_start(w13[:, u, i, :].rearrange("p (e h) -> p e h", e=2), one(w13_v[i]).rearrange("o d e h -> (o d) e h")).then_inc(e_load[u], 16)
                sp.dma_start(w2[:, u, :], one(w2_v).rearrange("o k d -> (o k) d")).then_inc(e_load[u], 16)

            for n in range(2):
                fetch(n, n, None)
            with sp.Fori(1, E // 4) as j:
                for n in range(2):
                    fetch(j * 2 + n, n, j)

        @block.gpsimd
        def _(pool):
            g = nc.gpsimd
            g.memset(neg_half[:, :], -0.5)
            g.memset(freq[:, :], 0.0).then_inc(s_pre_p, 1)
            g.memset(init_rows[:, :, 0:D + 2], 0.0).then_inc(s_pre_p, 1)
            g.memset(init_rows[:, :, D + 2:D + 3], -1.0)
            pool.wait_ge(s_const, 16)
            g.tensor_copy(init_rows[:, :, D + 3], cst("dump")).then_inc(s_pre_p, 1)
            pool.wait_ge(s_pre_p, 3)

            def rstd(ve, rs, q, s_ve, s_rs):
                wait(pool, s_ve, q)
                g.tensor_tensor(out=rs[:, q.u], in0=ve[:, q.u], in1=neg_half[:, :], op=ALU.pow).then_inc(s_rs, 1)

            def scatter(q, s):
                for i, (t0, nt) in enumerate(TILES):
                    for r in range(TOPK):
                        g.indirect_dma_start(
                            out=slots_d, out_offset=bass.IndirectOffsetOnAxis(
                                ap=slot[0:nt, q.u, r, s * NT + i:s * NT + i + 1], axis=0),
                            in_=xs[0:nt, q.u, s * NT + i, :], in_offset=None, bounds_check=SLOTS - 1,
                            oob_is_err=False).then_inc(s_scat[q.u], 16)

            def body(k):
                if k.runs():
                    rstd(ve1, rs1, k, S["v_ve1"], S["p_rs1"])
                if k.back(3).runs():
                    wait(pool, S["v_sloti"], k, 3)
                    wait(pool, S["v_meta"], k, 3)
                    if first(k.back(3)):
                        pool.wait_ge(s_init, 16 * (SLOTS // 1024 + 1))
                    wait(pool, S["p_go"], k, 4)
                    g.tensor_tensor(out=spare[:, 2:3], in0=neg_half[:, 0:1], in1=neg_half[:, 1:2], op=ALU.add)\
                        .then_inc(S["p_go"], 1)
                    for s in range(2):
                        scatter(k.back(3), s)
                if k.back(1).runs():
                    rstd(ve2, rs2, k.back(1), S["v_ve2"], S["p_rs2"])
                if k.runs():
                    wait(pool, S["a_xh"], k)
                    wait(pool, S["p_hbo"], k, 1)
                    g.tensor_tensor(out=hb[:, :, :], in0=h[:, k.u].rearrange("p s t d -> p (s t) d"),
                                    in1=xh[:, k.u], op=ALU.add).then_inc(S["p_hb"], 1)
                    wait(pool, S["p_hb"], k)
                    wait(pool, S["v_h2b"], k, 2)
                    g.tensor_tensor(out=hbo[:, k.u], in0=hb[:, :, :],
                                    in1=bo_row[:, :].rearrange("p (o d) -> p o d", o=1).to_broadcast([128, 2 * NT, D]),
                                    op=ALU.add).then_inc(S["p_hbo"], 1)

            steps(pool, body)
            for u in range(2):
                pool.wait_ge(s_store[u], 16 * NT * (PAIRS // 2))

            last_row = pool.to_reg(TOKENS + CAP - 1)

            def add(a, n, j):
                pool.wait_ge(X["e_yv"], a + 1)
                for e in range(2):
                    if j is not None or n > 0:
                        pool.wait_ge(X["e_spare0"] if e == 0 else X["e_spare1"], a)
                    if e == 1:
                        pool.wait_ge(e_add[0], (a + 1) * 32)
                    elif j is not None or n > 0:
                        pool.wait_ge(e_add[1], a * 32)
                    g.tensor_tensor(out=spare[:, e:e + 1], in0=neg_half[:, 0:1], in1=neg_half[:, 1:2], op=ALU.add)\
                        .then_inc(X["e_spare0"] if e == 0 else X["e_spare1"], 1)
                    for i in range(2):
                        m = 2 * e + i
                        g.indirect_dma_start(
                            out=out, out_offset=bass.IndirectOffsetOnAxis(ap=etok[:, n % 2, m:m + 1], axis=0),
                            in_=ye[:, n % 2, m, :], in_offset=None, bounds_check=last_row,
                            compute_op=ALU.add).then_inc(e_add[e], 16)

            for n in range(2):
                add(n, n, None)
            with pool.Fori(1, E // 4) as j:
                for n in range(2):
                    add(j * 2 + n, n, j)
            for e in range(2):
                pool.wait_ge(e_add[e], (E // 2) * 32)

        @block.scalar
        def _(act):
            a = nc.scalar
            act.wait_ge(s_pre_p, 1)
            for i in range(2):
                act.dma_start(freq[i * 32:i * 32 + PLANES, :], colr("L0_attn_pos_freqs")).then_inc(s_small, 16)
            act.dma_start(setw[:, :], row("L0_attn_set_weights", SETS)).then_inc(s_small, 16)
            act.dma_start(pw_col[:, :], row("L0_attn_pos_weight", 1)).then_inc(s_small, 16)
            act.wait_ge(s_pre_v, 2)
            a.activation(setx[:, SETS:2 * SETS], setx[:, 0:SETS], ACT.Exp, accum_out=wcol[:, 1:2]).then_inc(s_pre_a, 1)
            a.activation(wcol[:, 2:3], pw_col[:, :], ACT.Exp, scale=-1.0).then_inc(s_pre_a, 1)
            act.wait_ge(s_pre_v, 3)
            a.activation(feat[0:PLANES, :], ph[0:PLANES, 1, :], ACT.Sin)
            a.activation(feat[32:40, :], ph[32:40, 1, :], ACT.Sin).then_inc(s_pre_a, 1)
            act.wait_ge(s_setup, 1)

            def position_part(y, s, done, ready, used):
                wait(act, S[ready], y)
                wait(act, S[used], y, 1)
                a.activation(pos_o[:, s, :], bank[:, 1 if s == 0 else 3, 0:L], ACT.Copy).then_inc(S[done], 1)

            def body(k):
                y, z = k.back(1), k.back(2)
                if k.runs():
                    wait(act, S["pe_th"], k)
                    wait(act, S["p_hb"], k, 2)
                    wait(act, S["v_st1"], k, 2)
                    a.activation(h[:, k.u, :, 0:2, :], bank[:, 7, :].rearrange("p (s t d) -> p s t d", s=2, t=2),
                                 ACT.Copy).then_inc(S["a_h"], 1)
                if z.runs():
                    wait(act, S["v_nb2"], z)
                    wait_dma(act, s_scat, z, 4 * NT, 2)
                    wait(act, S["pe_tx2b"], z, 2)
                    for i in range(2 * NT):
                        ins = a.activation(xs[:, z.u, i, 0:D], h2[:, z.u, i, :], ACT.Identity,
                                           bias=nb2[:, z.u, i:i + 1], scale=rs2[:, z.u, i:i + 1])
                    ins.then_inc(S["a_x2"], 1)
                if y.runs():
                    position_part(y, 0, "a_pa", "pe_pa", "v_tota")
                if z.runs():
                    for s, (done, ready) in enumerate((("a_x2ta", "pe_tx2a"), ("a_x2tb", "pe_tx2b"))):
                        if s == 0:
                            wait(act, S["pe_lgt"], z, 1)
                            wait(act, S["pe_ffb"], z, 1)
                        wait(act, S[ready], z)
                        a.activation(x2_t[:, s, :], bank[:, 4 + s, 0:L], ACT.Copy).then_inc(S[done], 1)
                if y.runs():
                    position_part(y, 1, "a_pb", "pe_pb", "v_totb")
                if k.runs():
                    wait(act, S["v_nb1"], k)
                    wait(act, S["pe_tx"], k, 2)
                    for i in range(2 * NT):
                        ins = a.activation(xh[:, k.u, i, :], h[:, k.u, i // NT, i % NT, :], ACT.Identity,
                                           bias=nb1[:, k.u, i:i + 1], scale=rs1[:, k.u, i:i + 1])
                    ins.then_inc(S["a_xh"], 1)
                if z.runs():
                    wait(act, S["pe_lgt"], z)
                    wait(act, S["pe_lg"], z, 1)
                    a.activation(lg_t[:, :], bank[:, 4, 0:L], ACT.Copy).then_inc(S["a_lgt"], 1)
                if z.runs():
                    for s, (done, ready, used) in enumerate((("a_sia", "pe_ffa", "v_m3a"), ("a_sib", "pe_ffb", "v_m3b"))):
                        wait(act, S[ready], z)
                        wait(act, S[used], z, 1)
                        a.activation(sl[:, s, :], bank[:, 6 if s == 0 else 1, 0:L], ACT.Silu).then_inc(S[done], 1)
                    wait(act, S["pe_lg"], z)
                    wait(act, S["v_imax"], z, 1)
                    a.activation(lg[:, :, :].rearrange("p (s t) e -> p t s e", s=2),
                                 bank[:, 7, 0:2 * NT * E].rearrange("p (t s e) -> p t s e", s=2, e=E), ACT.Copy).then_inc(S["a_lg"], 1)
                if k.runs():
                    wait(act, S["pe_tx"], k)
                    wait(act, S["pe_gb"], k, 2)
                    for s, (b, done) in enumerate(((3, "a_xta"), (7, "a_xtb"))):
                        a.activation(x_t[:, k.u, s, :], bank[:, b, 0:L], ACT.Copy).then_inc(S[done], 1)
                    wait(act, S["a_abs"], k, 2)
                    wait(act, S["pe_k"], k)
                    a.activation(ph_t[:, k.u, 0, :], bank[:, 6, 0:L], ACT.Tanh, bias=bk_col[:, :]).then_inc(S["a_thk"], 1)
                    wait(act, S["pe_q"], k)
                    a.activation(ph_t[:, k.u, 1, :], bank[:, 0, 0:L], ACT.Tanh, bias=bq_col[:, :]).then_inc(S["a_thq"], 1)
                    wait(act, S["a_thk"], k)
                    wait(act, S["a_thq"], k)
                    wait(act, S["a_sin"], k, 2)
                    a.activation(ph_a[:, k.u, :, :], ph_t[:, k.u, :, :], ACT.Abs, bias=cst("delta")).then_inc(S["a_abs"], 1)
                    wait(act, S["v_ea"], k, 2)
                    wait(act, S["v_eb"], k, 2)
                    for s, (done, ready, b) in enumerate((("a_ga", "pe_ga", 3), ("a_gb", "pe_gb", 7))):
                        wait(act, S[ready], k)
                        a.activation(gt[:, k.u, s, :], bank[:, b, 0:L], ACT.Tanh, bias=bg_half[:, :], scale=0.5)\
                            .then_inc(S[done], 1)
                    wait(act, S["a_abs"], k)
                    wait(act, S["pe_sc"], k, 2)
                    wait(act, S["v_qn"], k, 2)
                    a.activation(kq[:, k.u, :, :], ph_a[:, k.u, :, :], ACT.Sin, bias=half_pi[:, :], scale=-PI_LOW)\
                        .then_inc(S["a_sin"], 1)
                if z.runs():
                    wait(act, S["v_lohi"], z)
                    wait(act, S["v_sg"], z, 1)
                    a.activation(slo[:, :, :], lo[:, :, :], ACT.Silu)
                    a.activation(thi[:, :, :], hi[:, :, :], ACT.Tanh, scale=0.5).then_inc(S["a_small"], 1)
            steps(act, body)

            def expert(n, m, j):
                act.wait_ge(X["e_tr"], n + 1)
                if j is not None:
                    act.wait_ge(X["e_z"], n - 1)
                a.activation(xe_t[:, m % 2, :], bank[:, m % 2, :], ACT.Copy).then_inc(X["e_xt"], 1)
                act.wait_ge(X["e_z"], n + 1)
                if j is not None:
                    act.wait_ge(X["e_g"], n - 1)
                a.activation(ae[:, m % 2, :], bank[:, 2 + m % 2, 0:CAP], ACT.Silu).then_inc(X["e_silu"], 1)

            for n in range(2):
                expert(n, n, None)
            with act.Fori(1, E // 4) as j:
                for n in range(2):
                    expert(j * 2 + n, n, j)

        @block.tensor
        def _(pe):
            mm = nc.tensor.matmul
            tr = nc.tensor.transpose
            pe.wait_ge(s_const, 16)
            pe.wait_ge(s_pre_v, 1)
            for m in range(SHIFT):
                ins = tr(bank[0:KROWS, m // 4, (m % 4) * D:(m % 4 + 1) * D], w_pad[:, m, :], ident)
            ins.then_inc(s_pre_pe, 1)
            tr(bank[:, 4, 0:TILE], pos_raw[:, 0, :], ident)
            tr(bank[:, 4, TILE:NIMG], pos_raw[0:T1, 1, :], ident[0:T1, 0:T1])
            tr(bank[:, 5, 0:E], gate_raw[:, :], ident[0:E, 0:E]).then_inc(s_pre_pe, 1)

            def position_products():
                pe.wait_ge(s_pre_a, 3)
                mm(bank[:, 2, 0:L], feat[:, 0:TILE], feat[:, :], start=True, stop=True)
                mm(bank[:, 3, 0:L - TILE], feat[:, TILE:2 * TILE], feat[:, TILE:L], start=True, stop=False,
                   skip_group_check=True)
                mm(bank[:, 3, L - TILE:L], feat[:, NIMG:L], feat[:, NIMG:L], start=False, stop=True,
                   skip_group_check=True).then_inc(s_pre_pe, 1)
                pe.wait_ge(s_setup, 1)

            def project(y, s, src, done, free):
                wait(pe, S[src], y)
                wait(pe, S[free], y, 1)
                for i, (t0, _) in enumerate(TILES):
                    ins = mm(bank[:, 4 + s, i * D:(i + 1) * D], tot[:, s, t0:t0 + TILE], wo[:, :],
                             start=True, stop=True)
                ins.then_inc(S[done], 1)

            def scores(y, i):
                t0 = TILES[i][0]
                for s in range(2):
                    r = slice(64 * s, 64 * s + 64)
                    dst = (bank[:, 2 + 2 * s, 0:L], bank[:, 3 + 2 * s, 0:L - TILE], bank[:, 3 + 2 * s, L - TILE:L])[i]
                    ins = mm(dst, kq[r, y.u, 0, t0:t0 + TILE], qn[r, y.u, t0:L], start=(i < 2), stop=(i != 1),
                             skip_group_check=True)
                return ins

            def position_out(y, s, done):
                for i, (t0, nt) in enumerate(TILES):
                    c0 = (0, L, L + L - TILE)[i]
                    ins = mm(bank[:, 2 * s + 1, t0:L], v[0:nt, y.u, s, i, :], pos_a[0:nt, c0:c0 + L - t0],
                             start=(i == 0), stop=(i == NT - 1))
                ins.then_inc(S[done], 1)

            def phase_out(y, s, ready, done):
                wait(pe, S[ready], y)
                for i, (t0, nt) in enumerate(TILES):
                    c0 = (0, L, L + L - TILE)[i]
                    ins = mm(bank[:, 2 * s, t0:L], v[0:nt, y.u, s, i, :],
                             a_t[0:nt, y.u, s].rearrange("p a l -> p (a l)")[:, c0:c0 + L - t0],
                             start=(i == 0), stop=(i == NT - 1))
                ins.then_inc(S[done], 1)

            def body(k):
                y, z, w = k.back(1), k.back(2), k.back(3)
                if k.runs():
                    wait_dma(pe, s_shift, k, 2 * (COPIES - 1))
                    if first(k):
                        pe.wait_ge(s_wtok, 1)
                    wait(pe, S["a_thq"], k, 1)
                    wait(pe, S["v_va"], k, 1)
                    for s, done in enumerate(("pe_toka", "pe_tok")):
                        for m in range(SHIFT):
                            r = slice(0, KROWS if m + (COPIES - 1) * SHIFT < P else KROWS - CP)
                            ins = mm(bank[:, s, 0:NIMG], w_tok[r, m, :], xin[r, k.u, s, m:m + P * (NIMG - 1) + 1:P],
                                     start=(m == 0), stop=(m == SHIFT - 1))
                        ins.then_inc(S[done], 1)
                if first(k):
                    position_products()
                if y.runs():
                    wait(pe, S["a_sin"], y)
                    wait(pe, S["v_qn"], y)
                    wait(pe, S["v_vb"], y)
                    wait(pe, S["a_ga"], y)
                    wait(pe, S["v_fina"], y, 2)
                    wait(pe, S["v_finb"], y, 2)
                    scores(y, 0)
                if k.runs():
                    wait(pe, S["v_ht"], k)
                    wait(pe, S["a_gb"], k, 1)
                    for s in range(2):
                        for i in range(2):
                            ins = tr(bank[:, 7, (2 * s + i) * D:(2 * s + i + 1) * D],
                                     h_t[:, k.u, s, i * TILE:(i + 1) * TILE], ident)
                    ins.then_inc(S["pe_th"], 1)
                if y.runs():
                    scores(y, 1)
                    scores(y, 2).then_inc(S["pe_sc"], 1)
                if y.runs():
                    wait(pe, S["v_ht"], y, -1)
                    position_out(y, 0, "pe_pa")
                if w.runs():
                    wait(pe, S["v_both"], w)
                    wait(pe, S["a_thk"], w, -2)
                    wait(pe, S["a_sia"], w)
                    flat = both[:, :, :].rearrange("p t e -> p (t e)")
                    n = 2 * NT + 1
                    mm(bank[:, 6, 0:n * E], below[:, :], flat, start=True, stop=False)
                    for i in range(2 * NT):
                        nt = TILES[i % NT][1]
                        src = both[0:nt, i:i + 1, :].to_broadcast([nt, n - 1 - i, E])
                        ins = mm(bank[:, 6, (i + 1) * E:n * E], ones[0:nt, :], src, start=False, stop=(i == 2 * NT - 1))
                    ins.then_inc(S["pe_pf"], 1)
                if y.runs():
                    phase_out(y, 0, "v_ma", "pe_ta")
                if z.runs():
                    wait(pe, S["a_x2"], z)
                    wait(pe, S["v_mb"], z, -1)
                    wait(pe, S["v_fina"], z, 1)
                    wait(pe, S["v_finb"], z, 1)
                    for s, done in enumerate(("pe_tx2a", "pe_tx2b")):
                        for i, (t0, nt) in enumerate(TILES):
                            ins = tr(bank[:, 4 + s, t0:t0 + nt], xs[0:nt, z.u, s * NT + i, 0:D], ident[0:nt, 0:nt])
                        ins.then_inc(S[done], 1)
                if y.runs():
                    wait(pe, S["v_mb"], y)
                    position_out(y, 1, "pe_pb")
                    phase_out(y, 1, "v_mb", "pe_tb")
                if z.runs():
                    wait(pe, S["a_x2ta"], z)
                    wait(pe, S["a_x2tb"], z)
                    for s in range(2):
                        ins = mm(bank[E * s:E * s + E, 4, 0:L], gate_t[:, :], x2_t[:, s, :], start=True, stop=True)
                    ins.then_inc(S["pe_lgt"], 1)
                    wait(pe, S["v_cnt"], z, 1)
                    wait(pe, S["a_thk"], z, -1)
                    mm(bank[:, 6, 0:L], sw1[:, :], x2_t[:, 0, :], start=True, stop=True)
                    wait(pe, S["v_da"], z, -1)
                    wait(pe, S["v_m3a"], z, 1)
                    mm(bank[:, 0, 0:L], sw3[:, :], x2_t[:, 0, :], start=True, stop=True).then_inc(S["pe_ffa"], 1)
                    wait(pe, S["a_pa"], z, -1)
                    wait(pe, S["a_sib"], z, 1)
                    mm(bank[:, 1, 0:L], sw1[:, :], x2_t[:, 1, :], start=True, stop=True)
                    mm(bank[:, 5, 0:L], sw3[:, :], x2_t[:, 1, :], start=True, stop=True).then_inc(S["pe_ffb"], 1)
                    wait(pe, S["a_lgt"], z)
                    wait(pe, S["a_gb"], z, -1)
                    wait(pe, S["a_h"], z, -2)
                    wait(pe, S["a_lg"], z, 1)
                    for i, (t0, _) in enumerate(TILES):
                        ins = tr(bank[:, 7, i * TILE:(i + 1) * TILE], lg_t[:, t0:t0 + TILE], ident)
                    ins.then_inc(S["pe_lg"], 1)
                if y.runs():
                    project(y, 0, "v_tota", "pe_woa", "a_lgt")
                if k.runs():
                    wait(pe, S["a_xh"], k)
                    wait(pe, S["a_pb"], k, 1)
                    wait(pe, S["a_lg"], k, 2)
                    for s, b in enumerate((3, 7)):
                        for i, (t0, nt) in enumerate(TILES):
                            ins = tr(bank[:, b, t0:t0 + nt], xh[0:nt, k.u, s * NT + i, :], ident[0:nt, 0:nt])
                    ins.then_inc(S["pe_tx"], 1)
                if y.runs():
                    project(y, 1, "v_totb", "pe_wob", "v_m3b")
                if k.runs():
                    wait(pe, S["a_xta"], k)
                    mm(bank[:, 3, 0:L], wg[:, :], x_t[:, k.u, 0, :], start=True, stop=True).then_inc(S["pe_ga"], 1)
                    wait(pe, S["a_xtb"], k)
                    wait(pe, S["a_sia"], k, 2)
                    wait(pe, S["v_cnt"], k, 3)
                    wait(pe, S["v_da"], k, 1)
                    wait(pe, S["v_m3a"], k, 2)
                    for b, weights, done in ((6, wk, "pe_k"), (0, wq, "pe_q")):
                        for s in range(2):
                            ins = mm(bank[64 * s:64 * s + 64, b, 0:L], weights[:, :], x_t[:, k.u, s, :], start=True, stop=True)
                        ins.then_inc(S[done], 1)
                    wait(pe, S["a_pa"], k, 1)
                    wait(pe, S["a_sib"], k, 2)
                    wait(pe, S["v_db"], k, 1)
                    for s, done in enumerate(("pe_va", "pe_vb")):
                        for i, (t0, _) in enumerate(TILES):
                            ins = mm(bank[:, 1 + s, i * D:(i + 1) * D], x_t[:, k.u, s, t0:t0 + TILE], wv[:, :],
                                     start=True, stop=True)
                        ins.then_inc(S[done], 1)
                    mm(bank[:, 7, 0:L], wg[:, :], x_t[:, k.u, 1, :], start=True, stop=True).then_inc(S["pe_gb"], 1)
                if z.runs():
                    for s, (done, g, used) in enumerate((("pe_oa", "v_m3a", "v_h2a"), ("pe_ob", "v_m3b", "v_h2b"))):
                        wait(pe, S[g], z)
                        wait(pe, S[used], z, -1)
                        for i, (t0, _) in enumerate(TILES):
                            ins = mm(bank[:, 4 + s, i * D:(i + 1) * D], su[:, s, t0:t0 + TILE], sw2[:, :],
                                     start=True, stop=True)
                        ins.then_inc(S[done], 1)
            steps(pe, body)

            def expert(n, m, j):
                u = m % 2
                later = j is not None
                pe.wait_ge(e_load[u], (j + 1) * 64 if later else 64)
                if later:
                    pe.wait_ge(X["e_xt"], n - 1)
                for i in range(4):
                    ins = tr(bank[:, u, i * TILE:(i + 1) * TILE], rows[:, u, i, 0:D], ident)
                ins.then_inc(X["e_tr"], 1)
                pe.wait_ge(X["e_xt"], n + 1)
                if later:
                    pe.wait_ge(X["e_g"], n - 1)
                for i in range(2):
                    for e in range(2):
                        ins = mm(bank[64 * e:64 * e + 64, 2 + u, i * CAP:(i + 1) * CAP], w13[:, u, i, e * FH:(e + 1) * FH],
                                 xe_t[:, u, e * CAP:(e + 1) * CAP], start=True, stop=True)
                ins.then_inc(X["e_z"], 1)
                pe.wait_ge(X["e_g"], n + 1)
                if later:
                    pe.wait_ge(X["e_yv"], n - 1)
                for i in range(2):
                    for e in range(2):
                        r = slice(64 * e, 64 * e + 64)
                        ins = mm(bank[:, 4 + 2 * e + u, i * D:(i + 1) * D], ge[r, u, i * TILE:(i + 1) * TILE],
                                 w2[r, u, :], start=True, stop=True)
                ins.then_inc(X["e_y0"], 1)

            for n in range(2):
                expert(n, n, None)
            with pe.Fori(1, E // 4) as j:
                for n in range(2):
                    expert(j * 2 + n, n, j)

        @block.vector
        def _(dve):
            vv = nc.vector
            TS, TT, STT = vv.tensor_scalar, vv.tensor_tensor, vv.scalar_tensor_tensor
            chain = [0]

            def link(ins):
                chain[0] += 1
                ins.then_inc(s_zero, 1)
                dve.wait_ge(s_zero, chain[0])

            vv.memset(w_pad[:, SHIFT - 1, (COPIES - 1) * CP:KROWS], 0.0)
            vv.memset(xin[:, :, :, 0:P], 0.0).then_inc(s_pad, 1)
            vv.memset(h_t[:, :, :, NIMG:2 * TILE], 0.0)
            vv.memset(both[:, 2 * NT, :], 0.0)
            vv.memset(carry[:, 1, :], 0.0)
            vv.memset(ones[:, :], 1.0)
            vv.memset(half_pi[:, :], float(np.pi / 2))
            for i in range(4):
                vv.memset(ecur[:, 1, i:i + 1], float(i // 2 - 2))
            link(vv.memset(feat[:, :], 0.0))
            dve.wait_ge(s_wload, 16 * N_W)
            for n in range(COPIES):
                cols = min(SHIFT, P - n * SHIFT)
                ins = vv.tensor_copy(w_pad[:, 0:cols, n * CP:(n + 1) * CP],
                                     w_raw[:, :, n * SHIFT:n * SHIFT + cols].rearrange("h a b -> h b a"))
            ins.then_inc(s_pre_v, 1)
            dve.wait_ge(s_const, 16)
            dve.wait_ge(s_small, 16 * N_SMALL)
            vv.tensor_copy(below[:, :], cst("below"))
            TS(tokn[:, 1, :], cst("tok"), -2.0 * L, None, ALU.add)
            l_row = cst("pos", 40)
            link(vv.reduce_max(wcol[:, 0:1], setw[:, :], AX.X))
            TS(setx[:, 0:SETS], setw[:, :], wcol[:, 0:1], None, ALU.subtract).then_inc(s_pre_v, 1)
            dve.wait_ge(s_pre_pe, 1)
            for m in range(SHIFT):
                ins = vv.tensor_copy(w_tok[:, m, :], bank[0:KROWS, m // 4, (m % 4) * D:(m % 4 + 1) * D])
            ins.then_inc(s_wtok, 1)
            link(TS(ph[:, 0, :], l_row, freq[:, :], TWO_PI, ALU.mult, ALU.mult))
            link(TS(ph[:, 1, :], ph[:, 0, :], float(1 / (2 * np.pi)), None, ALU.mult))
            link(TS(ph[:, 2, :], ph[:, 1, :], ROUND, None, ALU.add))
            link(TS(ph[:, 1, :], ph[:, 2, :], -ROUND, None, ALU.add))
            link(STT(ph[:, 2, :], ph[:, 1, :], -TP1, ph[:, 0, :], ALU.mult, ALU.add))
            link(STT(ph[:, 3, :], ph[:, 1, :], -TP2, ph[:, 2, :], ALU.mult, ALU.add))
            link(STT(ph[:, 2, :], ph[:, 1, :], -TP3, ph[:, 3, :], ALU.mult, ALU.add))
            link(TS(ph[:, 0, :], ph[:, 2, :], cst("dpos", 40), None, ALU.subtract))
            link(STT(ph[:, 3, :], ph[:, 0, :], -1.0, ph[:, 0, :], ALU.mult, ALU.max))
            link(TS(ph[:, 2, :], ph[:, 3, :], -1.0, float(np.pi / 2), ALU.mult, ALU.add))
            TS(ph[:, 1, :], ph[:, 2, :], -PI_LOW, PI_LOW, ALU.max, ALU.min).then_inc(s_pre_v, 1)
            dve.wait_ge(s_pre_a, 2)
            link(vv.reciprocal(wcol[:, 3:4], wcol[:, 1:2]))
            link(TS(setx[:, 2 * SETS:3 * SETS], setx[:, SETS:2 * SETS], wcol[:, 3:4], None, ALU.mult))
            link(TT(setx[:, 3 * SETS:4 * SETS], setx[:, 2 * SETS:3 * SETS], cst("sel"), ALU.mult))
            link(vv.reduce_sum(wcol[:, 4:5], setx[:, 3 * SETS:4 * SETS], AX.X))
            TS(wn[:, :], cst("invn"), wcol[:, 4:5], None, ALU.mult)
            link(TS(wcol[:, 5:6], wcol[:, 2:3], 1.0, None, ALU.add))
            link(vv.reciprocal(wcol[:, 6:7], wcol[:, 5:6]))
            dve.wait_ge(s_pre_pe, 2)
            TS(pos_t[:, 1:NIMG], bank[:, 4, 1:NIMG], b_col[:, :], None, ALU.add)
            TS(pos_t[:, 0:1], bank[:, 4, 0:1], tok_col[:, :], None, ALU.add)
            vv.tensor_copy(gate_t[:, :], bank[:, 5, 0:E])
            dve.wait_ge(s_late, 16 * N_LATE)
            TS(bg_half[:, :], bg_col[:, :], 0.5, None, ALU.mult)
            dve.wait_ge(s_pre_pe, 3)
            link(STT(pos_a[:, 0:L], bank[:, 2, 0:L], wcol[:, 6:7], cst("maskn")[:, 0:L], ALU.mult, ALU.mult))
            link(STT(pos_a[:, L:2 * L], bank[:, 3, 0:L], wcol[:, 6:7], cst("maskn")[:, L:2 * L], ALU.mult, ALU.mult))
            vv.memset(wcol[:, 7:8], 0.0).then_inc(s_setup, 1)

            stats = {"1": (st1, ms1, dm1, m21, dd1, vs1, ve1), "2": (st2, ms2, dm2, m22, dd2, vs2, ve2)}

            def moments(q, n):
                st, ms, dm, m2, dd, vs, ve = stats[n]
                mean, square = (1, 4), (2, 5)
                wait(dve, S["v_st" + n], q)
                TT(ms[:, q.u], st[:, q.u, :, mean[0]], st[:, q.u, :, mean[1]], ALU.add)
                TT(dm[:, :], st[:, q.u, :, mean[0]], st[:, q.u, :, mean[1]], ALU.subtract)
                TT(m2[:, :], st[:, q.u, :, square[0]], st[:, q.u, :, square[1]], ALU.add).then_inc(S["v_mm" + n], 1)

            def square(q, n):
                st, ms, dm, m2, dd, vs, ve = stats[n]
                wait(dve, S["v_mm" + n], q)
                TT(dd[:, :], dm[:, :], dm[:, :], ALU.mult).then_inc(S["v_dd" + n], 1)

            def total(q, n):
                st, ms, dm, m2, dd, vs, ve = stats[n]
                wait(dve, S["v_dd" + n], q)
                STT(vs[:, :], dd[:, :], D / 4.0, m2[:, :], ALU.mult, ALU.add).then_inc(S["v_vs" + n], 1)

            def scaled(q, n):
                st, ms, dm, m2, dd, vs, ve = stats[n]
                wait(dve, S["v_vs" + n], q)
                TS(ve[:, q.u], vs[:, :], 1.0 / D, LN_EPS, ALU.mult, ALU.add).then_inc(S["v_ve" + n], 1)

            def mask(y, s, done):
                wait(dve, S["pe_sc"], y)
                wait(dve, S["pe_ta" if s == 0 else "pe_tb"], y, 2)
                TT(a_t[:, y.u, s, :, :], bank[:, 2 + 2 * s:4 + 2 * s, 0:L],
                   cst("mask").rearrange("p (a l) -> p a l", a=2), ALU.mult).then_inc(S[done], 1)

            def add_shared(z, s, done, ready):
                wait(dve, S[ready], z)
                TT(fin[:, z.u, s * NT:(s + 1) * NT, :], bank[:, 4 + s, 0:NT * D].rearrange("p (t d) -> p t d", d=D),
                   h2[:, z.u, s * NT:(s + 1) * NT, :], ALU.add).then_inc(S[done], 1)

            def bias_scale(q, ms, rs, nb, s_rs, s_nb):
                wait(dve, s_rs, q)
                STT(nb[:, q.u, :], ms[:, q.u, :], -0.5, rs[:, q.u, :], ALU.mult, ALU.mult).then_inc(s_nb, 1)

            def mix(y, s, pt, ap, d, e, f, used):
                wait(dve, S[pt], y)
                wait(dve, S[ap], y)
                TT(dif[:, s, :], bank[:, 2 * s, 0:L], pos_o[:, s, :], ALU.subtract).then_inc(S[d], 1)
                if s == 0:
                    wait(dve, S["a_gb"], y)
                wait(dve, S[d], y)
                STT(gdif[:, s, :], gt[:, y.u, s, :], 1.0, dif[:, s, :], ALU.add, ALU.mult).then_inc(S[e], 1)
                wait(dve, S[e], y)
                wait(dve, S[used], y, 1)
                STT(tot[:, s, :], pos_o[:, s, :], 2.0, gdif[:, s, :], ALU.mult, ALU.add).then_inc(S[f], 1)

            def body(k):
                y, z, w = k.back(1), k.back(2), k.back(3)
                if k.runs():
                    wait(dve, S["pe_th"], k, 2)
                    for s, ready in enumerate(("pe_toka", "pe_tok")):
                        wait(dve, S[ready], k)
                        ins = TT(h_t[:, k.u, s, 0:NIMG], bank[:, s, 0:NIMG], pos_t[:, :], ALU.add)
                    ins.then_inc(S["v_ht"], 1)
                if z.runs():
                    bias_scale(z, ms2, rs2, nb2, S["p_rs2"], S["v_nb2"])
                if k.runs():
                    wait_dma(dve, s_txt, k, 1)
                    for i in (2, NT + 2, 0, 1, NT, NT + 1):
                        if i == 0:
                            wait(dve, S["a_h"], k)
                        ins = vv.bn_stats(st1[:, k.u, i, :], h[:, k.u, i // NT, i % NT, :])
                    ins.then_inc(S["v_st1"], 1)
                    moments(k, "1")
                if y.runs():
                    mask(y, 0, "v_ma")
                if k.runs():
                    square(k, "1")
                if y.runs():
                    mask(y, 1, "v_mb")
                if k.runs():
                    total(k, "1")
                    scaled(k, "1")
                if w.runs():
                    wait(dve, S["pe_pf"], w)
                    prev, now = carry[:, 1 - w.u, :], carry[:, w.u, :]
                    TT(cnt[:, :, :], bank[:, 6, 0:2 * NT * E].rearrange("p (t e) -> p t e", e=E),
                       prev.rearrange("p (o e) -> p o e", o=1).to_broadcast([128, 2 * NT, E]), ALU.add)
                    TT(now, bank[:, 6, 2 * NT * E:(2 * NT + 1) * E], prev, ALU.add).then_inc(S["v_cnt"], 1)
                if w.runs():
                    wait(dve, S["v_cnt"], w)
                    for r in range(2):
                        ins = TT(picked[:, r, :, :], hot[:, r, :, :], cnt[:, :, :], ALU.mult)
                    ins.then_inc(S["v_pick"], 1)
                if w.runs():
                    wait(dve, S["v_pick"], w)
                    vv.reduce_sum(place[:, :, :].rearrange("p r t -> p (r t)"),
                                  picked[:, :, :, :].rearrange("p r t e -> p (r t) e"), AX.X).then_inc(S["v_place"], 1)
                    wait(dve, S["v_place"], w)
                    TS(over[:, :, :], place[:, :, :], CAP - 0.5, FAR, ALU.is_gt, ALU.mult)
                    STT(slotf[:, :, :], idx[:, :, :], float(CAP), place[:, :, :], ALU.mult, ALU.add).then_inc(S["v_over"], 1)
                if k.runs():
                    bias_scale(k, ms1, rs1, nb1, S["p_rs1"], S["v_nb1"])
                if w.runs():
                    wait(dve, S["v_over"], w)
                    wait_dma(dve, s_scat, w, 4 * NT, 2)
                    TT(slot[:, w.u, :, :], slotf[:, :, :], over[:, :, :], ALU.add).then_inc(S["v_sloti"], 1)
                if y.runs():
                    mix(y, 0, "pe_ta", "a_pa", "v_da", "v_ea", "v_tota", "pe_woa")
                    mix(y, 1, "pe_tb", "a_pb", "v_db", "v_eb", "v_totb", "pe_wob")
                if z.runs():
                    for s, (a, f, done, prev) in enumerate((("a_sia", "pe_ffa", "v_m3a", "pe_oa"),
                                                            ("a_sib", "pe_ffb", "v_m3b", "pe_ob"))):
                        wait(dve, S[prev], z, 1)
                        wait(dve, S[a], z)
                        TT(su[:, s, :], sl[:, s, :], bank[:, 0 if s == 0 else 5, 0:L], ALU.mult).then_inc(S[done], 1)
                    wait(dve, S["v_tok"], z, 1)
                    wait(dve, S["a_lg"], z)
                    TS(tokn[:, z.u, :], tokn[:, 1 - z.u, :], 2.0 * L, None, ALU.add).then_inc(S["v_tok"], 1)
                    for i in range(2 * NT):
                        ins = vv.max(top[:, i, :], lg[:, i, :])
                    ins.then_inc(S["v_max"], 1)
                if y.runs():
                    wait(dve, S["p_hbo"], y)
                    wait(dve, S["v_finb"], y, 2)
                    wait(dve, S["a_x2"], y, 2)
                    for s, (done, ready) in enumerate((("v_h2a", "pe_woa"), ("v_h2b", "pe_wob"))):
                        wait(dve, S[ready], y)
                        TT(h2[:, y.u, s * NT:(s + 1) * NT, :], bank[:, 4 + s, 0:NT * D].rearrange("p (t d) -> p t d", d=D),
                           hbo[:, y.u, s * NT:(s + 1) * NT, :], ALU.add).then_inc(S[done], 1)
                if z.runs():
                    wait(dve, S["a_small"], z, 1)
                    wait(dve, S["v_max"], z)
                    TS(lo[:, :, :], top[:, :, 0:2], -1.0, None, ALU.min)
                    TS(hi[:, :, :], top[:, :, 0:2], -1.0, None, ALU.max).then_inc(S["v_lohi"], 1)
                    for i in range(2 * NT):
                        ins = vv.max_index(topi[:, i, :], top[:, i, :], lg[:, i, :])
                    ins.then_inc(S["v_imax"], 1)
                if y.runs():
                    wait(dve, S["v_h2b"], y)
                    for i in range(2 * NT):
                        ins = vv.bn_stats(st2[:, y.u, i, :], h2[:, y.u, i, :])
                    ins.then_inc(S["v_st2"], 1)
                if z.runs():
                    wait(dve, S["v_imax"], z)
                    wait(dve, S["v_over"], z, 1)
                    vv.tensor_copy(idx[:, :, :].rearrange("p r t -> p t r"), topi[:, :, 0:2]).then_inc(S["v_idx"], 1)
                if k.runs():
                    for s, (done, ready, prev) in enumerate((("v_va", "pe_va", "pe_ta"), ("v_vb", "pe_vb", "pe_tb"))):
                        wait(dve, S[ready], k)
                        wait(dve, S[prev], k, 2)
                        TT(v[:, k.u, s, :, :], bank[:, 1 + s, 0:NT * D].rearrange("p (t d) -> p t d", d=D),
                           bv_row[:, :].rearrange("p (o d) -> p o d", o=1).to_broadcast([128, NT, D]), ALU.add)\
                            .then_inc(S[done], 1)
                if y.runs():
                    moments(y, "2")
                if z.runs():
                    wait(dve, S["v_idx"], z)
                    wait(dve, S["v_pick"], z, 1)
                    for r in range(2):
                        ins = TT(hot[:, r, :, :], cst("iota").rearrange("p (o e) -> p o e", o=1).to_broadcast([128, 2 * NT, E]),
                                 idx[:, r, :].rearrange("p (t o) -> p t o", o=1).to_broadcast([128, 2 * NT, E]), ALU.is_equal)
                    ins.then_inc(S["v_hot"], 1)
                if y.runs():
                    square(y, "2")
                if z.runs():
                    wait(dve, S["a_small"], z)
                    vv.reciprocal(rlo[:, :, :], lo[:, :, :]).then_inc(S["v_rlo"], 1)
                if y.runs():
                    total(y, "2")
                if z.runs():
                    wait(dve, S["v_hot"], z)
                    wait(dve, S["pe_pf"], z, 1)
                    TT(both[:, 0:2 * NT, :], hot[:, 0, :, :], hot[:, 1, :, :], ALU.add).then_inc(S["v_both"], 1)
                if y.runs():
                    scaled(y, "2")
                if z.runs():
                    wait(dve, S["v_rlo"], z)
                    STT(sgl[:, :, :], rlo[:, :, :], 0.5 / SIG_M1, slo[:, :, :], ALU.mult, ALU.mult).then_inc(S["v_sgl"], 1)
                    wait_dma(dve, s_store, z, NT, 2)
                    add_shared(z, 0, "v_fina", "pe_oa")
                    wait(dve, S["v_sgl"], z)
                    STT(sg[:, :, :], thi[:, :, :], 1.0, sgl[:, :, :], ALU.add, ALU.mult).then_inc(S["v_sg"], 1)
                    add_shared(z, 1, "v_finb", "pe_ob")
                    wait(dve, S["v_sg"], z)
                    STT(ssum[:, :], sg[:, :, 0], 1e-20, sg[:, :, 1], ALU.add, ALU.add).then_inc(S["v_ssum"], 1)
                if k.runs():
                    wait(dve, S["a_sin"], k)
                    wait(dve, S["pe_sc"], k, 2)
                    TT(qn[:, k.u, :], kq[:, k.u, 1, :], wn[:, :], ALU.mult).then_inc(S["v_qn"], 1)
                if z.runs():
                    wait(dve, S["v_ssum"], z)
                    vv.reciprocal(sinv[:, :], ssum[:, :]).then_inc(S["v_sinv"], 1)
                    vv.tensor_copy(xs[:, z.u, :, D + 2], idx[:, 0, :])
                    wait(dve, S["v_tok"], z)
                    vv.tensor_copy(xs[:, z.u, :, D + 3], tokn[:, z.u, :])
                    wait(dve, S["v_sinv"], z)
                    for r in range(2):
                        ins = STT(xs[:, z.u, :, D + r], sg[:, :, r], ROUTE, sinv[:, :], ALU.mult, ALU.mult)
                    ins.then_inc(S["v_meta"], 1)
            steps(dve, body)

            def expert(n, m, j):
                u = m % 2
                later = j is not None
                dve.wait_ge(e_load[u], (j + 1) * 64 if j is not None else 64)
                TS(ecur[:, u, :], ecur[:, 1 - u, :], 2.0, None, ALU.add).then_inc(X["e_cur"], 1)
                TT(ewd[:, :], rows[:, u, :, D], rows[:, u, :, D + 1], ALU.subtract).then_inc(X["e_wd"], 1)
                dve.wait_ge(X["e_cur"], n + 1)
                TT(esel[:, :], rows[:, u, :, D + 2], ecur[:, u, :], ALU.is_equal).then_inc(X["e_sel"], 1)
                dve.wait_ge(X["e_wd"], n + 1)
                dve.wait_ge(X["e_sel"], n + 1)
                TT(ewm[:, :], esel[:, :], ewd[:, :], ALU.mult).then_inc(X["e_wm"], 1)
                dve.wait_ge(X["e_wm"], n + 1)
                TT(ew[:, u, :], ewm[:, :], rows[:, u, :, D + 1], ALU.add).then_inc(X["e_w"], 1)
                if later:
                    dve.wait_ge(e_add[0], (n - 1) * 32)
                    dve.wait_ge(e_add[1], (n - 1) * 32)
                vv.tensor_copy(etok[:, u, :], rows[:, u, :, D + 3]).then_inc(X["e_tokn"], 1)
                dve.wait_ge(X["e_silu"], n + 1)
                TT(ge[:, u, :], ae[:, u, :], bank[:, 2 + u, CAP:2 * CAP], ALU.mult).then_inc(X["e_g"], 1)
                dve.wait_ge(X["e_w"], n + 1)
                dve.wait_ge(X["e_y0"], n + 1)
                for i in range(4):
                    e = i // 2
                    ins = TS(ye[:, u, i, :], bank[:, 4 + 2 * e + u, (i % 2) * D:(i % 2 + 1) * D], ew[:, u, i:i + 1], None,
                             ALU.mult)
                ins.then_inc(X["e_yv"], 1)

            for n in range(2):
                expert(n, n, None)
            with dve.Fori(1, E // 4) as j:
                for n in range(2):
                    expert(j * 2 + n, n, j)


_INS = ['x', 'txt', 'L0_tok_W', 'L0_tok_b', 'L0_tok_token', 'L0_tok_pos', 'L0_attn_Wk', 'L0_attn_bk', 'L0_attn_Wq',
        'L0_attn_bq', 'L0_attn_Wv', 'L0_attn_bv', 'L0_attn_set_weights', 'L0_attn_pos_freqs', 'L0_attn_Wg',
        'L0_attn_bg', 'L0_attn_pos_weight', 'L0_attn_Wo', 'L0_attn_bo', 'L0_ffn_gate_w', 'L0_ffn_w1', 'L0_ffn_w3',
        'L0_ffn_w2', 'L0_ffn_sw1', 'L0_ffn_sw3', 'L0_ffn_sw2']


def build(nc, arrays):
    t = {n: nc.dram_tensor(f"in_{n}", a.shape, F32, kind="ExternalInput").ap() for n, a in arrays.items()}
    out = nc.dram_tensor("out_rows", (TOKENS + CAP, D), F32, kind="ExternalOutput").ap()
    slots_d = nc.dram_tensor("slot_rows", (SLOTS, ROW), F32, kind="Internal").ap()
    program(nc, t, out, slots_d)


def kernel(**inputs):
    import concourse.bacc as _bacc
    from concourse.bass_utils import run_bass_kernel_spmd as _run

    nc = _bacc.Bacc("TRN2", target_bir_lowering=False, num_devices=1)
    arrays = {n: np.ascontiguousarray(inputs[n]) for n in _INS}
    arrays["consts"] = constants()
    build(nc, arrays)
    r = _run(nc, [{f"in_{n}": a for n, a in arrays.items()}], core_ids=[0])
    return r.results[0]["out_rows"][0:TOKENS].reshape(B, L, D)
```

```python
from contextlib import ExitStack

import numpy as np

import concourse.bass as bass
from concourse import mybir

F32 = mybir.dt.float32
BF16 = mybir.dt.bfloat16
I32 = mybir.dt.int32
U32 = mybir.dt.uint32
ALU = mybir.AluOpType
ACT = mybir.ActivationFunctionType
AX = mybir.AxisListType

B, C, H, G = 128, 3, 196, 14
P = H // G
D = 128
NIMG = G * G + 1
NTXT = 128
L = NIMG + NTXT
SETS, PLANES = 4, 8
HF = SETS * PLANES
E, TOPK, CAP, FH = 64, 2, 256, 64
PAIRS = B // 2
TILE = 128
TILES = [(0, TILE), (TILE, NIMG - TILE), (NIMG, NTXT)]
NT = len(TILES)
T1 = TILES[1][1]
CP = C * P
XW = P + G * H
COPIES = 3
SHIFT = 5
KROWS = COPIES * CP
W_COL, E_COL, P_COL, T_COL = D, D + 2, D + 4, D + 6
ROW = D + 7
SLOTS = E * CAP
TOKENS = B * L
SPARE = 4 * TILE
LN_EPS = 1e-5
ROUTE = 2.5
SIG_M1 = 1.0 / (1.0 + float(np.exp(1.0)))
PI_LOW = 3.1415925
TWO_PI = float(np.float32(2.0) * np.float32(np.pi))
TP1 = 6.28125
TP2 = float(np.float32(np.round((2 * np.pi - TP1) * 2**20) / 2**20))
TP3 = float(np.float32(2 * np.pi - TP1 - TP2))
ROUND = 1.5 * 2.0**23
FAR = 1.0e6

CONST = {}
_at = 0
for _n, _w in (("ident", 128), ("below", 128), ("mask", 2 * L), ("maskn", 2 * L), ("invn", L), ("iota", CAP),
               ("pos", L), ("tok", 2 * NT), ("sel", SETS), ("delta", 1), ("dpos", 1), ("dump", 8)):
    CONST[_n] = (_at, _at + _w)
    _at += _w
CW = _at


def constants():
    t = np.zeros((128, CW), np.float32)

    def put(name, v):
        a, b = CONST[name]
        t[:, a:b] = v

    p = np.arange(128)[:, None]
    put("ident", np.eye(128))
    put("below", p < np.arange(128)[None, :])
    l = np.arange(L)[None, :]
    invn = (0.5 / np.sqrt((l + 1) * PLANES)).astype(np.float32)
    m0 = p <= l
    q1 = np.arange(TILE, L)[None, :]
    m1 = (p + TILE <= q1) & (p < T1)
    q2 = np.arange(NIMG, L)[None, :]
    m2 = p + NIMG <= q2
    mask = np.concatenate([m0, m1, m2], 1).astype(np.float32)
    n = np.concatenate([invn[:, 0:L], invn[:, TILE:L], invn[:, NIMG:L]], 1)
    put("mask", mask)
    put("maskn", mask * n)
    put("invn", invn)
    put("iota", np.arange(CAP)[None, :])
    put("pos", l)
    put("tok", np.concatenate([s * L + t0 + p for s in range(2) for t0, _ in TILES], 1))
    put("sel", (p % HF) // PLANES == np.arange(SETS)[None, :])
    put("delta", -0.5 * (p % (2 * HF) < HF))
    put("dpos", np.pi / 2 * (p < PLANES))
    put("dump", TOKENS + p + TILE * (np.arange(8)[None, :] % 4))
    return t


class Pair:

    def __init__(self, twice, j, c):
        self.twice, self.j, self.c = twice, j, c

    def back(self, n):
        return Pair(self.twice, self.j, self.c - n)

    @property
    def u(self):
        return self.c % 2

    def runs(self):
        return self.j is not None or 0 <= self.c < PAIRS

    def count(self):
        return self.c + 1 if self.j is None else self.twice + (self.c + 1)

    def uses(self):
        return self.c // 2 + 1 if self.j is None else self.j + (self.c // 2 + 1)

    def number(self):
        return self.c if self.j is None else self.twice + self.c


def first(pair):
    return pair.j is None and pair.c == 0


SKEW = 3
HEAD = 4
TAIL0 = PAIRS


def steps(eng, body):
    for k in range(HEAD):
        body(Pair(None, None, k))
    with_loop = (TAIL0 - HEAD) // 2
    assert HEAD + 2 * with_loop == TAIL0 and HEAD % 2 == 0
    with eng.Fori(HEAD // 2, HEAD // 2 + with_loop) as j:
        twice = j * 2
        for u in range(2):
            body(Pair(twice, j, u))
    for k in range(TAIL0, TAIL0 + SKEW):
        body(Pair(None, None, k))


def wait(eng, sem, pair, back=0):
    q = pair.back(back)
    if q.j is not None or 0 <= q.c < PAIRS:
        eng.wait_ge(sem, q.count())


def wait_dma(eng, sems, pair, each, back=0):
    q = pair.back(back)
    if q.j is not None or q.c >= 0:
        eng.wait_ge(sems[q.u], q.uses() * (16 * each))


class Experts:

    def __init__(self, j, m):
        self.j, self.m = j, m

    def number(self):
        return self.j * 4 + self.m

    def next(self):
        return Experts(self.j, self.m + 1)

    @property
    def u(self):
        return self.m % 2

    @property
    def load(self):
        return self.m % 4

    def fixed(self):
        return isinstance(self.j, int)


def expert_pairs(eng, body):
    turns = E // 8
    for m in range(4):
        body(Experts(0, m))
    with eng.Fori(1, turns - 1) as j:
        for m in range(4):
            body(Experts(j, m))
    for m in range(4):
        body(Experts(turns - 1, m))


def wait_expert(eng, sem, pair, back=0, each=1):
    n = pair.number() + (1 - back)
    if not pair.fixed() or n > 0:
        eng.wait_ge(sem, n * each)


def is_first(pair):
    return pair.fixed() and pair.number() == 0


def is_last(pair):
    return pair.fixed() and pair.number() == E // 2 - 1


def program(nc, t, out, slots_d):
    ctx = ExitStack()
    with ctx:
        def sb(name, shape, dt=F32):
            return ctx.enter_context(nc.sbuf_tensor(name, shape, dt))

        def sem(name):
            return ctx.enter_context(nc.semaphore(name))

        def sems(name):
            return [sem(f"{name}{u}") for u in range(2)]

        const = sb("const", [128, CW])

        def cst(name, p=128):
            a, b = CONST[name]
            return const[0:p, a:b]

        ident = cst("ident")
        w_tok = sb("w_tok", [KROWS, SHIFT, D])
        pos_raw = sb("pos_raw", [128, 2, D])
        tok_col = sb("tok_col", [D, 1])
        b_col = sb("b_col", [D, 1])
        pos_t = sb("pos_t", [D, NIMG])
        wk = sb("wk", [D, 2 * HF])
        wq = sb("wq", [D, 2 * HF])
        bk_col = sb("bk_col", [128, 1])
        bq_col = sb("bq_col", [128, 1])
        wv = sb("wv", [D, D])
        wg = sb("wg", [D, D])
        wo = sb("wo", [D, D])
        bg_col = sb("bg_col", [D, 1])
        bg_half = sb("bg_half", [D, 1])
        bv_row = sb("bv_row", [128, D])
        bo_row = sb("bo_row", [128, D])
        gate_raw = sb("gate_raw", [E, D])
        gate_t = sb("gate_t", [D, E])
        sw1 = sb("sw1", [D, D])
        sw3 = sb("sw3", [D, D])
        sw2 = sb("sw2", [D, D])
        below = sb("below", [128, 128], BF16)
        ones = sb("ones", [128, 128], BF16)
        setw = sb("setw", [128, SETS])
        setx = sb("setx", [128, 4 * SETS])
        wcol = sb("wcol", [128, 8])
        wn = sb("wn", [128, L])
        freq = sb("freq", [40, 1])
        feat = sb("feat", [40, L])
        pos_a = sb("pos_a", [128, 2 * L])
        half_pi = sb("half_pi", [128, 1])
        pw_col = sb("pw_col", [128, 1])
        neg_half = sb("neg_half", [128, 2 * NT])

        xin = sb("xin", [128, 2, 2, XW])
        h_t = sb("h_t", [D, 2, 2, 2 * TILE])
        h = sb("h", [128, 2, 2, NT, D])
        xh = sb("xh", [128, 2, 2 * NT, D])
        st1 = sb("st1", [128, 2, 2 * NT, 6])
        ms1 = sb("ms1", [128, 2, 2 * NT])
        dm1 = sb("dm1", [128, 2 * NT])
        m21 = sb("m21", [128, 2 * NT])
        dd1 = sb("dd1", [128, 2 * NT])
        vs1 = sb("vs1", [128, 2 * NT])
        ve1 = sb("ve1", [128, 2, 2 * NT])
        rs1 = sb("rs1", [128, 2, 2 * NT])
        nb1 = sb("nb1", [128, 2, 2 * NT])
        hb = sb("hb", [128, 2 * NT, D])
        hbo = sb("hbo", [128, 2, 2 * NT, D])
        x_t = sb("x_t", [D, 2, 2, L])
        ph_t = sb("ph_t", [128, 2, 2, L])
        ph_a = sb("ph_a", [128, 2, 2, L])
        kq = sb("kq", [128, 2, 2, L])
        qn = sb("qn", [128, 2, L])
        v = sb("v", [128, 2, 2, NT, D])
        gt = sb("gt", [D, 2, 2, L])
        a_t = sb("a_t", [128, 2, 2, 2, L])
        pos_o = sb("pos_o", [D, 2, L])
        dif = sb("dif", [D, 2, L])
        gdif = sb("gdif", [D, 2, L])
        tot = sb("tot", [D, 2, L])
        h2 = sb("h2", [128, 2, 2 * NT, D])
        st2 = sb("st2", [128, 2, 2 * NT, 6])
        ms2 = sb("ms2", [128, 2, 2 * NT])
        dm2 = sb("dm2", [128, 2 * NT])
        m22 = sb("m22", [128, 2 * NT])
        dd2 = sb("dd2", [128, 2 * NT])
        vs2 = sb("vs2", [128, 2 * NT])
        ve2 = sb("ve2", [128, 2, 2 * NT])
        rs2 = sb("rs2", [128, 2, 2 * NT])
        nb2 = sb("nb2", [128, 2, 2 * NT])
        xs = sb("xs", [128, 2, 2 * NT, ROW])
        x2_t = sb("x2_t", [D, 2, L])
        lg_t = sb("lg_t", [2 * E, L])
        lg = sb("lg", [128, 2 * NT, E])
        top = sb("top", [128, 2 * NT, 8])
        topi = sb("topi", [128, 2 * NT, 8], U32)
        idx = sb("idx", [128, 2, 2 * NT])
        hot = sb("hot", [128, 2, 2 * NT, E], BF16)
        both = sb("both", [128, 2 * NT + 1, E], BF16)
        cnt = sb("cnt", [128, 2 * NT, E], BF16)
        picked = sb("picked", [128, 2, 2 * NT, E], BF16)
        place = sb("place", [128, 2, 2 * NT])
        over = sb("over", [128, 2, 2 * NT])
        slotf = sb("slotf", [128, 2, 2 * NT])
        slot = sb("slot", [128, 2, 2, 2 * NT], I32)
        carry = sb("carry", [128, 2, E])
        tokn = sb("tokn", [128, 2, 2 * NT])
        lo = sb("lo", [128, 2 * NT, 2])
        hi = sb("hi", [128, 2 * NT, 2])
        slo = sb("slo", [128, 2 * NT, 2])
        thi = sb("thi", [128, 2 * NT, 2])
        rlo = sb("rlo", [128, 2 * NT, 2])
        sgl = sb("sgl", [128, 2 * NT, 2])
        sg = sb("sg", [128, 2 * NT, 2])
        ssum = sb("ssum", [128, 2 * NT])
        sinv = sb("sinv", [128, 2 * NT])
        sl = sb("sl", [D, 2, L])
        su = sb("su", [D, 2, L])
        fin = sb("fin", [128, 2, 2 * NT, D])

        flat_a = a_t[:, :, :, :, :].rearrange("p u s a l -> p (u s a l)")
        w_raw = flat_a[:, 0:CP * P].rearrange("p (a b) -> p a b", b=P)
        w_pad = flat_a[:, CP * P:CP * P + SHIFT * KROWS].rearrange("p (m k) -> p m k", k=KROWS)
        ph = x_t[0:40, :, :, :].rearrange("p u s l -> p (u s) l")
        init_rows = sb("init_rows", [128, 8, ROW])

        flat_x = xin[:, :, :, :].rearrange("p u s w -> p (u s w)")
        at = [0]

        def part(*shape):
            n = int(np.prod(shape))
            a = flat_x[:, at[0]:at[0] + n]
            at[0] += n
            names = "abcd"[:len(shape)]
            return a.rearrange(f"p ({' '.join(names)}) -> p {' '.join(names)}", **dict(zip(names, shape)))

        spare = sb("spare", [128, 3])
        rows = part(4, 4, ROW)
        w13 = part(4, 2, 2 * FH)
        w2 = part(4, D)
        xe_t = part(2, 4 * TILE)
        ae = part(2, CAP)
        ge = part(2, CAP)
        ecur = sb("ecur", [128, 2, 4])
        esel = sb("esel", [128, 4])
        ewd = sb("ewd", [128, 4])
        ewm = sb("ewm", [128, 4])
        ew = sb("ew", [128, 2, 4])
        epd = sb("epd", [128, 2])
        esum = sb("esum", [128, 2])
        edif = sb("edif", [128, 2])
        epm = sb("epm", [128, 2])
        esame = sb("esame", [128, 2])
        eplace = sb("eplace", [128, 2])
        emate = sb("emate", [128, 2])
        ekept = sb("ekept", [128, 2])
        edump = sb("edump", [128, 2])
        emove = sb("emove", [128, 2])
        etokf = sb("etokf", [128, 2, 4])
        etok = sb("etok", [128, 4, 4], I32)
        ye = part(4, 4, D)
        mate = part(4, 2, CAP)
        ysum = part(4, 2, D)

        bank = ctx.enter_context(nc.psum_tensor("bank", [128, 8, 512], F32))

        s_const, s_wload, s_init, s_small = sem("s_const"), sem("s_wload"), sem("s_init"), sem("s_small")
        s_zero = sem("s_zero")
        s_late, s_wtok = sem("s_late"), sem("s_wtok")
        s_pre_v, s_pre_a, s_pre_p, s_pre_pe = sem("s_pre_v"), sem("s_pre_a"), sem("s_pre_p"), sem("s_pre_pe")
        s_setup = sem("s_setup")
        s_xin, s_txt, s_store, s_scat = sems("s_xin"), sems("s_txt"), sems("s_store"), sems("s_scat")
        s_shift = sems("s_shift")
        s_pad = sem("s_pad")
        names = """pe_toka pe_tok pe_th pe_tx pe_k pe_q pe_va pe_vb pe_ga pe_gb pe_sc pe_ta pe_pa pe_tb pe_pb pe_woa pe_wob
            pe_tx2a pe_tx2b pe_lgt pe_lg pe_ffa pe_ffb pe_pf pe_oa pe_ob
            v_ht v_st1 v_mm1 v_dd1 v_vs1 v_ve1 v_nb1 v_m3a v_m3b v_max v_ma v_mb v_imax v_idx v_hot v_both v_lohi v_rlo v_sgl v_sg
            v_ssum v_sinv v_meta v_fina v_finb v_da v_db v_ea v_eb v_tota v_totb v_cnt v_pick v_place v_over v_sloti
            v_tok v_va v_vb v_qn v_h2a v_h2b v_st2 v_mm2 v_dd2 v_vs2 v_ve2 v_nb2
            a_x2ta a_x2tb a_h a_lgt a_lg a_sia a_sib a_small a_xh a_pa a_pb a_xta a_xtb a_thk a_thq a_ga a_gb a_abs a_sin a_x2
            p_rs1 p_hb p_rs2 p_go p_hbo""".split()
        S = {n: sem(n) for n in names}
        enames = """e_tr e_xt e_z e_silu e_g e_y0 e_sel e_wd e_wm e_w e_cur e_spare e_yv e_comb e_sum
            e_prep e_psum e_same e_pm e_place e_mate e_mt e_kept e_move e_tok""".split()
        X = {n: sem(n) for n in enames}
        e_load = [sem(f"e_load{i}") for i in range(4)]
        e_add = sem("e_add")

        block = ctx.enter_context(nc.Block())

        N_W = 6
        N_SMALL = 4
        N_LATE = 8 + 4 + 6 + 3

        colr = lambda n: t[n].rearrange("(h o) -> h o", o=1)
        row = lambda n, w: t[n].rearrange("(o h) -> o h", o=1).to_broadcast([128, w])

        @block.sync
        def _(sp):
            sp.dma_start(w_raw[:, :, :], t["L0_tok_W"].rearrange("h (a b) -> h a b", b=P)).then_inc(s_wload, 16)
            sp.dma_start(const[:, :], t["consts"]).then_inc(s_const, 16)
            sp.dma_start(pos_raw[:, 0, :], t["L0_tok_pos"][0:TILE, :]).then_inc(s_wload, 16)
            sp.dma_start(pos_raw[0:T1, 1, :], t["L0_tok_pos"][TILE:NIMG, :]).then_inc(s_wload, 16)
            sp.dma_start(tok_col[:, :], t["L0_tok_token"].rearrange("o h -> h o")).then_inc(s_wload, 16)
            sp.dma_start(b_col[:, :], t["L0_tok_b"].rearrange("(h o) -> h o", o=1)).then_inc(s_wload, 16)
            sp.dma_start(gate_raw[:, :], t["L0_ffn_gate_w"]).then_inc(s_wload, 16)

            def late_loads():
                for i in range(4):
                    sp.dma_start(bk_col[i * HF:(i + 1) * HF, :], colr("L0_attn_bk")).then_inc(s_late, 16)
                    sp.dma_start(bq_col[i * HF:(i + 1) * HF, :], colr("L0_attn_bq")).then_inc(s_late, 16)
                for i in range(2):
                    sp.dma_start(wk[:, i * HF:(i + 1) * HF], t["L0_attn_Wk"]).then_inc(s_late, 16)
                    sp.dma_start(wq[:, i * HF:(i + 1) * HF], t["L0_attn_Wq"]).then_inc(s_late, 16)
                for name, dst in (("L0_attn_Wv", wv), ("L0_attn_Wg", wg), ("L0_attn_Wo", wo), ("L0_ffn_sw1", sw1),
                                  ("L0_ffn_sw3", sw3), ("L0_ffn_sw2", sw2)):
                    sp.dma_start(dst[:, :], t[name]).then_inc(s_late, 16)
                sp.dma_start(bg_col[:, :], colr("L0_attn_bg")).then_inc(s_late, 16)
                sp.dma_start(bv_row[:, :], row("L0_attn_bv", D)).then_inc(s_late, 16)
                sp.dma_start(bo_row[:, :], row("L0_attn_bo", D)).then_inc(s_late, 16)

            def empty_slots(part):
                sp.wait_ge(s_pre_p, 3)
                init_v = slots_d.rearrange("(n i p) r -> n p i r", p=128, i=8)
                for n in range(part * SLOTS // (128 * 8 * 2), (part + 1) * SLOTS // (128 * 8 * 2)):
                    sp.dma_start(init_v[n], init_rows[:, :, :]).then_inc(s_init, 16)
                if part == 1:
                    sp.dma_start(out[TOKENS:TOKENS + SPARE, :].rearrange("(i p) d -> p i d", p=128), init_rows[:, 0:4, 0:D])\
                        .then_inc(s_init, 16)

            def load(q):
                n = q.number()
                for i in range(2):
                    img = t["x"][bass.ds(n * 2 + i, 1)] if q.j is not None else t["x"][2 * q.c + i:2 * q.c + i + 1]
                    for c in range(C):
                        src = img[:, c].rearrange("o (g r) w -> r (o g) w", r=P)
                        dst = xin[c * P:(c + 1) * P, q.u, i, P:XW].rearrange("r (g w) -> r g w", w=H)
                        sp.dma_start(dst, src).then_inc(s_xin[q.u], 16)
                txt = t["txt"][bass.ds(n * 2, 2)] if q.j is not None else t["txt"][2 * q.c:2 * q.c + 2]
                return txt

            def shift(q):
                wait_dma(sp, s_xin, q, 2 * C)
                for i in range(2):
                    for n in range(1, COPIES):
                        sp.dma_start(xin[n * CP:(n + 1) * CP, q.u, i, P - n * SHIFT:XW - n * SHIFT],
                                     xin[0:CP, q.u, i, P:XW]).then_inc(s_shift[q.u], 16)

            def body(k):
                q = k
                if q.runs():
                    wait(sp, S["pe_tok"], q, 2)
                    txt = load(q)
                    wait(sp, S["a_xh"], q, 2)
                    wait(sp, S["p_hb"], q, 2)
                    sp.dma_start(h[:, q.u, :, 2, :], txt.rearrange("s p d -> p s d")).then_inc(s_txt[q.u], 16)
                if k.runs():
                    shift(k)
                if first(k):
                    late_loads()
                for part in range(2):
                    if first(k.back(part + 1)):
                        empty_slots(part)
                q = k.back(3)
                if q.runs():
                    wait(sp, S["v_fina"], q)
                    wait(sp, S["v_finb"], q)
                    n = q.number()
                    o = out[bass.ds(n * (2 * L), 2 * L), :] if q.j is not None else out[q.c * 2 * L:(q.c + 1) * 2 * L, :]
                    o = o.rearrange("(s l) d -> l s d", s=2)
                    f = fin[:, q.u, :, :].rearrange("p (s t) d -> p t s d", s=2)
                    for i, (t0, nt) in enumerate(TILES):
                        sp.dma_start(o[t0:t0 + nt], f[0:nt, i]).then_inc(s_store[q.u], 16)

            sp.wait_ge(s_pad, 1)
            steps(sp, body)
            for u in range(2):
                sp.wait_ge(s_scat[u], 16 * 4 * NT * (PAIRS // 2))
                sp.wait_ge(s_store[u], 16 * NT * (PAIRS // 2))
            rows_v = slots_d.rearrange("(a q p) r -> a p q r", p=128, q=4)
            w13_v = [t[n].rearrange("(a e) d h -> a d e h", e=2) for n in ("L0_ffn_w1", "L0_ffn_w3")]
            w2_v = t["L0_ffn_w2"].rearrange("(a e) h d -> a (e h) d", e=2)

            def fetch(q):
                n, b = q.number(), q.load
                wait_expert(sp, X["e_y0"], q, 4)
                wait_expert(sp, X["e_prep"], q, 4)
                one = lambda v: (v[n:n + 1] if q.fixed() else v[bass.ds(n, 1)])
                sp.dma_start(rows[:, b, :, :], one(rows_v).rearrange("o p q r -> (o p) q r")).then_inc(e_load[b], 16)
                for i in range(2):
                    sp.dma_start(w13[:, b, i, :].rearrange("p (e h) -> p e h", e=2),
                                 one(w13_v[i]).rearrange("o d e h -> (o d) e h")).then_inc(e_load[b], 16)
                sp.dma_start(w2[:, b, :], one(w2_v).rearrange("o k d -> (o k) d")).then_inc(e_load[b], 16)

            expert_pairs(sp, fetch)

        @block.gpsimd
        def _(pool):
            g = nc.gpsimd
            g.memset(neg_half[:, :], -0.5)
            g.memset(freq[:, :], 0.0).then_inc(s_pre_p, 1)
            g.memset(init_rows[:, :, 0:E_COL], 0.0).then_inc(s_pre_p, 1)
            g.memset(init_rows[:, :, E_COL:P_COL], -1.0)
            g.memset(init_rows[:, :, P_COL:T_COL], 0.0)
            pool.wait_ge(s_const, 16)
            g.tensor_copy(init_rows[:, :, T_COL], cst("dump")).then_inc(s_pre_p, 1)
            pool.wait_ge(s_pre_p, 3)

            def rstd(ve, rs, q, s_ve, s_rs):
                wait(pool, s_ve, q)
                g.tensor_tensor(out=rs[:, q.u], in0=ve[:, q.u], in1=neg_half[:, :], op=ALU.pow).then_inc(s_rs, 1)

            def scatter(q, s):
                for i, (t0, nt) in enumerate(TILES):
                    for r in range(TOPK):
                        g.indirect_dma_start(
                            out=slots_d, out_offset=bass.IndirectOffsetOnAxis(
                                ap=slot[0:nt, q.u, r, s * NT + i:s * NT + i + 1], axis=0),
                            in_=xs[0:nt, q.u, s * NT + i, :], in_offset=None, bounds_check=SLOTS - 1,
                            oob_is_err=False).then_inc(s_scat[q.u], 16)

            def body(k):
                if k.runs():
                    rstd(ve1, rs1, k, S["v_ve1"], S["p_rs1"])
                if k.back(3).runs():
                    wait(pool, S["v_sloti"], k, 3)
                    wait(pool, S["v_meta"], k, 3)
                    if first(k.back(3)):
                        pool.wait_ge(s_init, 16 * (SLOTS // 1024 + 1))
                    wait(pool, S["p_go"], k, 4)
                    g.tensor_tensor(out=spare[:, 2:3], in0=neg_half[:, 0:1], in1=neg_half[:, 1:2], op=ALU.add)\
                        .then_inc(S["p_go"], 1)
                    for s in range(2):
                        scatter(k.back(3), s)
                if k.back(1).runs():
                    rstd(ve2, rs2, k.back(1), S["v_ve2"], S["p_rs2"])
                if k.runs():
                    wait(pool, S["a_xh"], k)
                    wait(pool, S["p_hbo"], k, 1)
                    g.tensor_tensor(out=hb[:, :, :], in0=h[:, k.u].rearrange("p s t d -> p (s t) d"),
                                    in1=xh[:, k.u], op=ALU.add).then_inc(S["p_hb"], 1)
                    wait(pool, S["p_hb"], k)
                    wait(pool, S["v_h2b"], k, 2)
                    g.tensor_tensor(out=hbo[:, k.u], in0=hb[:, :, :],
                                    in1=bo_row[:, :].rearrange("p (o d) -> p o d", o=1).to_broadcast([128, 2 * NT, D]),
                                    op=ALU.add).then_inc(S["p_hbo"], 1)

            steps(pool, body)
            for u in range(2):
                pool.wait_ge(s_store[u], 16 * NT * (PAIRS // 2))

            last_row = pool.to_reg(TOKENS + SPARE - 1)

            def add(q):
                wait_expert(pool, X["e_yv"], q)
                wait_expert(pool, X["e_spare"], q, 1)
                wait_expert(pool, e_add, q, 1, 64)
                g.tensor_tensor(out=spare[:, 0:1], in0=neg_half[:, 0:1], in1=neg_half[:, 1:2], op=ALU.add)\
                    .then_inc(X["e_spare"], 1)
                for m in range(4):
                    src = ysum[:, q.load, m, :] if m < 2 else ye[:, q.load, m, :]
                    g.indirect_dma_start(
                        out=out, out_offset=bass.IndirectOffsetOnAxis(ap=etok[:, q.load, m:m + 1], axis=0),
                        in_=src, in_offset=None, bounds_check=last_row,
                        compute_op=ALU.add).then_inc(e_add, 16)

            expert_pairs(pool, add)
            pool.wait_ge(e_add, (E // 2) * 64)

        @block.scalar
        def _(act):
            a = nc.scalar
            act.wait_ge(s_pre_p, 1)
            for i in range(2):
                act.dma_start(freq[i * 32:i * 32 + PLANES, :], colr("L0_attn_pos_freqs")).then_inc(s_small, 16)
            act.dma_start(setw[:, :], row("L0_attn_set_weights", SETS)).then_inc(s_small, 16)
            act.dma_start(pw_col[:, :], row("L0_attn_pos_weight", 1)).then_inc(s_small, 16)
            act.wait_ge(s_pre_v, 2)
            a.activation(setx[:, SETS:2 * SETS], setx[:, 0:SETS], ACT.Exp, accum_out=wcol[:, 1:2]).then_inc(s_pre_a, 1)
            a.activation(wcol[:, 2:3], pw_col[:, :], ACT.Exp, scale=-1.0).then_inc(s_pre_a, 1)
            act.wait_ge(s_pre_v, 3)
            a.activation(feat[0:PLANES, :], ph[0:PLANES, 1, :], ACT.Sin)
            a.activation(feat[32:40, :], ph[32:40, 1, :], ACT.Sin).then_inc(s_pre_a, 1)
            act.wait_ge(s_setup, 1)

            def position_part(y, s, done, ready, used):
                wait(act, S[ready], y)
                wait(act, S[used], y, 1)
                a.activation(pos_o[:, s, :], bank[:, 1 if s == 0 else 3, 0:L], ACT.Copy).then_inc(S[done], 1)

            def body(k):
                y, z = k.back(1), k.back(2)
                if k.runs():
                    wait(act, S["pe_th"], k)
                    wait(act, S["p_hb"], k, 2)
                    wait(act, S["v_st1"], k, 2)
                    a.activation(h[:, k.u, :, 0:2, :], bank[:, 7, :].rearrange("p (s t d) -> p s t d", s=2, t=2),
                                 ACT.Copy).then_inc(S["a_h"], 1)
                if z.runs():
                    wait(act, S["v_nb2"], z)
                    wait_dma(act, s_scat, z, 4 * NT, 2)
                    wait(act, S["pe_tx2b"], z, 2)
                    for i in range(2 * NT):
                        ins = a.activation(xs[:, z.u, i, 0:D], h2[:, z.u, i, :], ACT.Identity,
                                           bias=nb2[:, z.u, i:i + 1], scale=rs2[:, z.u, i:i + 1])
                    ins.then_inc(S["a_x2"], 1)
                if y.runs():
                    position_part(y, 0, "a_pa", "pe_pa", "v_tota")
                if z.runs():
                    for s, (done, ready) in enumerate((("a_x2ta", "pe_tx2a"), ("a_x2tb", "pe_tx2b"))):
                        if s == 0:
                            wait(act, S["pe_lgt"], z, 1)
                            wait(act, S["pe_ffb"], z, 1)
                        wait(act, S[ready], z)
                        a.activation(x2_t[:, s, :], bank[:, 4 + s, 0:L], ACT.Copy).then_inc(S[done], 1)
                if y.runs():
                    position_part(y, 1, "a_pb", "pe_pb", "v_totb")
                if k.runs():
                    wait(act, S["v_nb1"], k)
                    wait(act, S["pe_tx"], k, 2)
                    for i in range(2 * NT):
                        ins = a.activation(xh[:, k.u, i, :], h[:, k.u, i // NT, i % NT, :], ACT.Identity,
                                           bias=nb1[:, k.u, i:i + 1], scale=rs1[:, k.u, i:i + 1])
                    ins.then_inc(S["a_xh"], 1)
                if z.runs():
                    wait(act, S["pe_lgt"], z)
                    wait(act, S["pe_lg"], z, 1)
                    a.activation(lg_t[:, :], bank[:, 4, 0:L], ACT.Copy).then_inc(S["a_lgt"], 1)
                if z.runs():
                    for s, (done, ready, used) in enumerate((("a_sia", "pe_ffa", "v_m3a"), ("a_sib", "pe_ffb", "v_m3b"))):
                        wait(act, S[ready], z)
                        wait(act, S[used], z, 1)
                        a.activation(sl[:, s, :], bank[:, 6 if s == 0 else 1, 0:L], ACT.Silu).then_inc(S[done], 1)
                    wait(act, S["pe_lg"], z)
                    wait(act, S["v_imax"], z, 1)
                    a.activation(lg[:, :, :].rearrange("p (s t) e -> p t s e", s=2),
                                 bank[:, 7, 0:2 * NT * E].rearrange("p (t s e) -> p t s e", s=2, e=E), ACT.Copy).then_inc(S["a_lg"], 1)
                if k.runs():
                    wait(act, S["pe_tx"], k)
                    wait(act, S["pe_gb"], k, 2)
                    for s, (b, done) in enumerate(((3, "a_xta"), (7, "a_xtb"))):
                        a.activation(x_t[:, k.u, s, :], bank[:, b, 0:L], ACT.Copy).then_inc(S[done], 1)
                    wait(act, S["a_abs"], k, 2)
                    wait(act, S["pe_k"], k)
                    a.activation(ph_t[:, k.u, 0, :], bank[:, 6, 0:L], ACT.Tanh, bias=bk_col[:, :]).then_inc(S["a_thk"], 1)
                    wait(act, S["pe_q"], k)
                    a.activation(ph_t[:, k.u, 1, :], bank[:, 0, 0:L], ACT.Tanh, bias=bq_col[:, :]).then_inc(S["a_thq"], 1)
                    wait(act, S["a_thk"], k)
                    wait(act, S["a_thq"], k)
                    wait(act, S["a_sin"], k, 2)
                    a.activation(ph_a[:, k.u, :, :], ph_t[:, k.u, :, :], ACT.Abs, bias=cst("delta")).then_inc(S["a_abs"], 1)
                    wait(act, S["v_ea"], k, 2)
                    wait(act, S["v_eb"], k, 2)
                    for s, (done, ready, b) in enumerate((("a_ga", "pe_ga", 3), ("a_gb", "pe_gb", 7))):
                        wait(act, S[ready], k)
                        a.activation(gt[:, k.u, s, :], bank[:, b, 0:L], ACT.Tanh, bias=bg_half[:, :], scale=0.5)\
                            .then_inc(S[done], 1)
                    wait(act, S["a_abs"], k)
                    wait(act, S["pe_sc"], k, 2)
                    wait(act, S["v_qn"], k, 2)
                    a.activation(kq[:, k.u, :, :], ph_a[:, k.u, :, :], ACT.Sin, bias=half_pi[:, :], scale=-PI_LOW)\
                        .then_inc(S["a_sin"], 1)
                if z.runs():
                    wait(act, S["v_lohi"], z)
                    wait(act, S["v_sg"], z, 1)
                    a.activation(slo[:, :, :], lo[:, :, :], ACT.Silu)
                    a.activation(thi[:, :, :], hi[:, :, :], ACT.Tanh, scale=0.5).then_inc(S["a_small"], 1)
            steps(act, body)

            def expert(q):
                wait_expert(act, X["e_tr"], q)
                wait_expert(act, X["e_z"], q, 2)
                a.activation(xe_t[:, q.u, :], bank[:, q.u, :], ACT.Copy).then_inc(X["e_xt"], 1)
                wait_expert(act, X["e_z"], q)
                wait_expert(act, X["e_g"], q, 2)
                a.activation(ae[:, q.u, :], bank[:, 2 + q.u, 0:CAP], ACT.Silu).then_inc(X["e_silu"], 1)

            expert_pairs(act, expert)

        @block.tensor
        def _(pe):
            mm = nc.tensor.matmul
            tr = nc.tensor.transpose
            pe.wait_ge(s_const, 16)
            pe.wait_ge(s_pre_v, 1)
            for m in range(SHIFT):
                ins = tr(bank[0:KROWS, m // 4, (m % 4) * D:(m % 4 + 1) * D], w_pad[:, m, :], ident)
            ins.then_inc(s_pre_pe, 1)
            tr(bank[:, 4, 0:TILE], pos_raw[:, 0, :], ident)
            tr(bank[:, 4, TILE:NIMG], pos_raw[0:T1, 1, :], ident[0:T1, 0:T1])
            tr(bank[:, 5, 0:E], gate_raw[:, :], ident[0:E, 0:E]).then_inc(s_pre_pe, 1)

            def position_products():
                pe.wait_ge(s_pre_a, 3)
                mm(bank[:, 2, 0:L], feat[:, 0:TILE], feat[:, :], start=True, stop=True)
                mm(bank[:, 3, 0:L - TILE], feat[:, TILE:2 * TILE], feat[:, TILE:L], start=True, stop=False,
                   skip_group_check=True)
                mm(bank[:, 3, L - TILE:L], feat[:, NIMG:L], feat[:, NIMG:L], start=False, stop=True,
                   skip_group_check=True).then_inc(s_pre_pe, 1)
                pe.wait_ge(s_setup, 1)

            def project(y, s, src, done, free):
                wait(pe, S[src], y)
                wait(pe, S[free], y, 1)
                for i, (t0, _) in enumerate(TILES):
                    ins = mm(bank[:, 4 + s, i * D:(i + 1) * D], tot[:, s, t0:t0 + TILE], wo[:, :],
                             start=True, stop=True)
                ins.then_inc(S[done], 1)

            def scores(y, i):
                t0 = TILES[i][0]
                for s in range(2):
                    r = slice(64 * s, 64 * s + 64)
                    dst = (bank[:, 2 + 2 * s, 0:L], bank[:, 3 + 2 * s, 0:L - TILE], bank[:, 3 + 2 * s, L - TILE:L])[i]
                    ins = mm(dst, kq[r, y.u, 0, t0:t0 + TILE], qn[r, y.u, t0:L], start=(i < 2), stop=(i != 1),
                             skip_group_check=True)
                return ins

            def position_out(y, s, done):
                for i, (t0, nt) in enumerate(TILES):
                    c0 = (0, L, L + L - TILE)[i]
                    ins = mm(bank[:, 2 * s + 1, t0:L], v[0:nt, y.u, s, i, :], pos_a[0:nt, c0:c0 + L - t0],
                             start=(i == 0), stop=(i == NT - 1))
                ins.then_inc(S[done], 1)

            def phase_out(y, s, ready, done):
                wait(pe, S[ready], y)
                for i, (t0, nt) in enumerate(TILES):
                    c0 = (0, L, L + L - TILE)[i]
                    ins = mm(bank[:, 2 * s, t0:L], v[0:nt, y.u, s, i, :],
                             a_t[0:nt, y.u, s].rearrange("p a l -> p (a l)")[:, c0:c0 + L - t0],
                             start=(i == 0), stop=(i == NT - 1))
                ins.then_inc(S[done], 1)

            def body(k):
                y, z, w = k.back(1), k.back(2), k.back(3)
                if k.runs():
                    wait_dma(pe, s_shift, k, 2 * (COPIES - 1))
                    if first(k):
                        pe.wait_ge(s_wtok, 1)
                    wait(pe, S["a_thq"], k, 1)
                    wait(pe, S["v_va"], k, 1)
                    for s, done in enumerate(("pe_toka", "pe_tok")):
                        for m in range(SHIFT):
                            r = slice(0, KROWS if m + (COPIES - 1) * SHIFT < P else KROWS - CP)
                            ins = mm(bank[:, s, 0:NIMG], w_tok[r, m, :], xin[r, k.u, s, m:m + P * (NIMG - 1) + 1:P],
                                     start=(m == 0), stop=(m == SHIFT - 1))
                        ins.then_inc(S[done], 1)
                if first(k):
                    position_products()
                if y.runs():
                    wait(pe, S["a_sin"], y)
                    wait(pe, S["v_qn"], y)
                    wait(pe, S["v_vb"], y)
                    wait(pe, S["a_ga"], y)
                    wait(pe, S["v_fina"], y, 2)
                    wait(pe, S["v_finb"], y, 2)
                    scores(y, 0)
                if k.runs():
                    wait(pe, S["v_ht"], k)
                    wait(pe, S["a_gb"], k, 1)
                    for s in range(2):
                        for i in range(2):
                            ins = tr(bank[:, 7, (2 * s + i) * D:(2 * s + i + 1) * D],
                                     h_t[:, k.u, s, i * TILE:(i + 1) * TILE], ident)
                    ins.then_inc(S["pe_th"], 1)
                if y.runs():
                    scores(y, 1)
                    scores(y, 2).then_inc(S["pe_sc"], 1)
                if y.runs():
                    wait(pe, S["v_ht"], y, -1)
                    position_out(y, 0, "pe_pa")
                if w.runs():
                    wait(pe, S["v_both"], w)
                    wait(pe, S["a_thk"], w, -2)
                    wait(pe, S["a_sia"], w)
                    flat = both[:, :, :].rearrange("p t e -> p (t e)")
                    n = 2 * NT + 1
                    mm(bank[:, 6, 0:n * E], below[:, :], flat, start=True, stop=False)
                    for i in range(2 * NT):
                        nt = TILES[i % NT][1]
                        src = both[0:nt, i:i + 1, :].to_broadcast([nt, n - 1 - i, E])
                        ins = mm(bank[:, 6, (i + 1) * E:n * E], ones[0:nt, :], src, start=False, stop=(i == 2 * NT - 1))
                    ins.then_inc(S["pe_pf"], 1)
                if y.runs():
                    phase_out(y, 0, "v_ma", "pe_ta")
                if z.runs():
                    wait(pe, S["a_x2"], z)
                    wait(pe, S["v_mb"], z, -1)
                    wait(pe, S["v_fina"], z, 1)
                    wait(pe, S["v_finb"], z, 1)
                    for s, done in enumerate(("pe_tx2a", "pe_tx2b")):
                        for i, (t0, nt) in enumerate(TILES):
                            ins = tr(bank[:, 4 + s, t0:t0 + nt], xs[0:nt, z.u, s * NT + i, 0:D], ident[0:nt, 0:nt])
                        ins.then_inc(S[done], 1)
                if y.runs():
                    wait(pe, S["v_mb"], y)
                    position_out(y, 1, "pe_pb")
                    phase_out(y, 1, "v_mb", "pe_tb")
                if z.runs():
                    wait(pe, S["a_x2ta"], z)
                    wait(pe, S["a_x2tb"], z)
                    for s in range(2):
                        ins = mm(bank[E * s:E * s + E, 4, 0:L], gate_t[:, :], x2_t[:, s, :], start=True, stop=True)
                    ins.then_inc(S["pe_lgt"], 1)
                    wait(pe, S["v_cnt"], z, 1)
                    wait(pe, S["a_thk"], z, -1)
                    mm(bank[:, 6, 0:L], sw1[:, :], x2_t[:, 0, :], start=True, stop=True)
                    wait(pe, S["v_da"], z, -1)
                    wait(pe, S["v_m3a"], z, 1)
                    mm(bank[:, 0, 0:L], sw3[:, :], x2_t[:, 0, :], start=True, stop=True).then_inc(S["pe_ffa"], 1)
                    wait(pe, S["a_pa"], z, -1)
                    wait(pe, S["a_sib"], z, 1)
                    mm(bank[:, 1, 0:L], sw1[:, :], x2_t[:, 1, :], start=True, stop=True)
                    mm(bank[:, 5, 0:L], sw3[:, :], x2_t[:, 1, :], start=True, stop=True).then_inc(S["pe_ffb"], 1)
                    wait(pe, S["a_lgt"], z)
                    wait(pe, S["a_gb"], z, -1)
                    wait(pe, S["a_h"], z, -2)
                    wait(pe, S["a_lg"], z, 1)
                    for i, (t0, _) in enumerate(TILES):
                        ins = tr(bank[:, 7, i * TILE:(i + 1) * TILE], lg_t[:, t0:t0 + TILE], ident)
                    ins.then_inc(S["pe_lg"], 1)
                if y.runs():
                    project(y, 0, "v_tota", "pe_woa", "a_lgt")
                if k.runs():
                    wait(pe, S["a_xh"], k)
                    wait(pe, S["a_pb"], k, 1)
                    wait(pe, S["a_lg"], k, 2)
                    for s, b in enumerate((3, 7)):
                        for i, (t0, nt) in enumerate(TILES):
                            ins = tr(bank[:, b, t0:t0 + nt], xh[0:nt, k.u, s * NT + i, :], ident[0:nt, 0:nt])
                    ins.then_inc(S["pe_tx"], 1)
                if y.runs():
                    project(y, 1, "v_totb", "pe_wob", "v_m3b")
                if k.runs():
                    wait(pe, S["a_xta"], k)
                    mm(bank[:, 3, 0:L], wg[:, :], x_t[:, k.u, 0, :], start=True, stop=True).then_inc(S["pe_ga"], 1)
                    wait(pe, S["a_xtb"], k)
                    wait(pe, S["a_sia"], k, 2)
                    wait(pe, S["v_cnt"], k, 3)
                    wait(pe, S["v_da"], k, 1)
                    wait(pe, S["v_m3a"], k, 2)
                    for b, weights, done in ((6, wk, "pe_k"), (0, wq, "pe_q")):
                        for s in range(2):
                            ins = mm(bank[64 * s:64 * s + 64, b, 0:L], weights[:, :], x_t[:, k.u, s, :], start=True, stop=True)
                        ins.then_inc(S[done], 1)
                    wait(pe, S["a_pa"], k, 1)
                    wait(pe, S["a_sib"], k, 2)
                    wait(pe, S["v_db"], k, 1)
                    for s, done in enumerate(("pe_va", "pe_vb")):
                        for i, (t0, _) in enumerate(TILES):
                            ins = mm(bank[:, 1 + s, i * D:(i + 1) * D], x_t[:, k.u, s, t0:t0 + TILE], wv[:, :],
                                     start=True, stop=True)
                        ins.then_inc(S[done], 1)
                    mm(bank[:, 7, 0:L], wg[:, :], x_t[:, k.u, 1, :], start=True, stop=True).then_inc(S["pe_gb"], 1)
                if z.runs():
                    for s, (done, g, used) in enumerate((("pe_oa", "v_m3a", "v_h2a"), ("pe_ob", "v_m3b", "v_h2b"))):
                        wait(pe, S[g], z)
                        wait(pe, S[used], z, -1)
                        for i, (t0, _) in enumerate(TILES):
                            ins = mm(bank[:, 4 + s, i * D:(i + 1) * D], su[:, s, t0:t0 + TILE], sw2[:, :],
                                     start=True, stop=True)
                        ins.then_inc(S[done], 1)
            steps(pe, body)

            def turn(q):
                pe.wait_ge(e_load[q.load], (q.j + (q.m // 4 + 1)) * 64)
                wait_expert(pe, X["e_xt"], q, 2)
                for i in range(4):
                    ins = tr(bank[:, q.u, i * TILE:(i + 1) * TILE], rows[:, q.load, i, 0:D], ident)
                ins.then_inc(X["e_tr"], 1)

            def hidden(q):
                wait_expert(pe, X["e_xt"], q)
                wait_expert(pe, X["e_g"], q, 2)
                for i in range(2):
                    for e in range(2):
                        ins = mm(bank[64 * e:64 * e + 64, 2 + q.u, i * CAP:(i + 1) * CAP],
                                 w13[:, q.load, i, e * FH:(e + 1) * FH], xe_t[:, q.u, e * CAP:(e + 1) * CAP],
                                 start=True, stop=True)
                ins.then_inc(X["e_z"], 1)

            def result(q):
                wait_expert(pe, X["e_g"], q)
                wait_expert(pe, X["e_tok"], q, 2)
                wait_expert(pe, X["e_yv"], q, 2)
                for i in range(2):
                    for e in range(2):
                        r = slice(64 * e, 64 * e + 64)
                        ins = mm(bank[:, 4 + 2 * e + q.u, i * D:(i + 1) * D], ge[r, q.u, i * TILE:(i + 1) * TILE],
                                 w2[r, q.load, :], start=True, stop=True)
                ins.then_inc(X["e_y0"], 1)

            def combine(q, back):
                u, b = (q.m - back) % 2, (q.m - back) % 4
                wait_expert(pe, X["e_mt"], q, back)
                wait_expert(pe, X["e_tok"], q, back)
                for i in range(2):
                    for m in range(2):
                        ins = mm(bank[:, 4 + u, CAP + i * D:CAP + (i + 1) * D], mate[:, b, m, i * TILE:(i + 1) * TILE],
                                 ye[:, b, 2 + m, :], start=(m == 0), stop=(m == 1))
                ins.then_inc(X["e_comb"], 1)

            def expert(q):
                if is_first(q):
                    turn(q)
                    hidden(q)
                if not is_last(q):
                    turn(q.next())
                if not is_first(q):
                    combine(q, 1)
                result(q)
                if not is_last(q):
                    hidden(q.next())
                else:
                    combine(q, 0)

            expert_pairs(pe, expert)

        @block.vector
        def _(dve):
            vv = nc.vector
            TS, TT, STT = vv.tensor_scalar, vv.tensor_tensor, vv.scalar_tensor_tensor
            chain = [0]

            def link(ins):
                chain[0] += 1
                ins.then_inc(s_zero, 1)
                dve.wait_ge(s_zero, chain[0])

            vv.memset(w_pad[:, SHIFT - 1, (COPIES - 1) * CP:KROWS], 0.0)
            vv.memset(xin[:, :, :, 0:P], 0.0).then_inc(s_pad, 1)
            vv.memset(h_t[:, :, :, NIMG:2 * TILE], 0.0)
            vv.memset(both[:, 2 * NT, :], 0.0)
            vv.memset(carry[:, 1, :], 0.0)
            vv.memset(ones[:, :], 1.0)
            vv.memset(half_pi[:, :], float(np.pi / 2))
            for i in range(4):
                vv.memset(ecur[:, 1, i:i + 1], float(i // 2 - 2))
            link(vv.memset(feat[:, :], 0.0))
            dve.wait_ge(s_wload, 16 * N_W)
            for n in range(COPIES):
                cols = min(SHIFT, P - n * SHIFT)
                ins = vv.tensor_copy(w_pad[:, 0:cols, n * CP:(n + 1) * CP],
                                     w_raw[:, :, n * SHIFT:n * SHIFT + cols].rearrange("h a b -> h b a"))
            ins.then_inc(s_pre_v, 1)
            dve.wait_ge(s_const, 16)
            dve.wait_ge(s_small, 16 * N_SMALL)
            vv.tensor_copy(below[:, :], cst("below"))
            TS(tokn[:, 1, :], cst("tok"), -2.0 * L, None, ALU.add)
            l_row = cst("pos", 40)
            link(vv.reduce_max(wcol[:, 0:1], setw[:, :], AX.X))
            TS(setx[:, 0:SETS], setw[:, :], wcol[:, 0:1], None, ALU.subtract).then_inc(s_pre_v, 1)
            dve.wait_ge(s_pre_pe, 1)
            for m in range(SHIFT):
                ins = vv.tensor_copy(w_tok[:, m, :], bank[0:KROWS, m // 4, (m % 4) * D:(m % 4 + 1) * D])
            ins.then_inc(s_wtok, 1)
            link(TS(ph[:, 0, :], l_row, freq[:, :], TWO_PI, ALU.mult, ALU.mult))
            link(TS(ph[:, 1, :], ph[:, 0, :], float(1 / (2 * np.pi)), None, ALU.mult))
            link(TS(ph[:, 2, :], ph[:, 1, :], ROUND, None, ALU.add))
            link(TS(ph[:, 1, :], ph[:, 2, :], -ROUND, None, ALU.add))
            link(STT(ph[:, 2, :], ph[:, 1, :], -TP1, ph[:, 0, :], ALU.mult, ALU.add))
            link(STT(ph[:, 3, :], ph[:, 1, :], -TP2, ph[:, 2, :], ALU.mult, ALU.add))
            link(STT(ph[:, 2, :], ph[:, 1, :], -TP3, ph[:, 3, :], ALU.mult, ALU.add))
            link(TS(ph[:, 0, :], ph[:, 2, :], cst("dpos", 40), None, ALU.subtract))
            link(STT(ph[:, 3, :], ph[:, 0, :], -1.0, ph[:, 0, :], ALU.mult, ALU.max))
            link(TS(ph[:, 2, :], ph[:, 3, :], -1.0, float(np.pi / 2), ALU.mult, ALU.add))
            TS(ph[:, 1, :], ph[:, 2, :], -PI_LOW, PI_LOW, ALU.max, ALU.min).then_inc(s_pre_v, 1)
            dve.wait_ge(s_pre_a, 2)
            link(vv.reciprocal(wcol[:, 3:4], wcol[:, 1:2]))
            link(TS(setx[:, 2 * SETS:3 * SETS], setx[:, SETS:2 * SETS], wcol[:, 3:4], None, ALU.mult))
            link(TT(setx[:, 3 * SETS:4 * SETS], setx[:, 2 * SETS:3 * SETS], cst("sel"), ALU.mult))
            link(vv.reduce_sum(wcol[:, 4:5], setx[:, 3 * SETS:4 * SETS], AX.X))
            TS(wn[:, :], cst("invn"), wcol[:, 4:5], None, ALU.mult)
            link(TS(wcol[:, 5:6], wcol[:, 2:3], 1.0, None, ALU.add))
            link(vv.reciprocal(wcol[:, 6:7], wcol[:, 5:6]))
            dve.wait_ge(s_pre_pe, 2)
            TS(pos_t[:, 1:NIMG], bank[:, 4, 1:NIMG], b_col[:, :], None, ALU.add)
            TS(pos_t[:, 0:1], bank[:, 4, 0:1], tok_col[:, :], None, ALU.add)
            vv.tensor_copy(gate_t[:, :], bank[:, 5, 0:E])
            dve.wait_ge(s_late, 16 * N_LATE)
            TS(bg_half[:, :], bg_col[:, :], 0.5, None, ALU.mult)
            dve.wait_ge(s_pre_pe, 3)
            link(STT(pos_a[:, 0:L], bank[:, 2, 0:L], wcol[:, 6:7], cst("maskn")[:, 0:L], ALU.mult, ALU.mult))
            link(STT(pos_a[:, L:2 * L], bank[:, 3, 0:L], wcol[:, 6:7], cst("maskn")[:, L:2 * L], ALU.mult, ALU.mult))
            vv.memset(wcol[:, 7:8], 0.0).then_inc(s_setup, 1)

            stats = {"1": (st1, ms1, dm1, m21, dd1, vs1, ve1), "2": (st2, ms2, dm2, m22, dd2, vs2, ve2)}

            def moments(q, n):
                st, ms, dm, m2, dd, vs, ve = stats[n]
                mean, square = (1, 4), (2, 5)
                wait(dve, S["v_st" + n], q)
                TT(ms[:, q.u], st[:, q.u, :, mean[0]], st[:, q.u, :, mean[1]], ALU.add)
                TT(dm[:, :], st[:, q.u, :, mean[0]], st[:, q.u, :, mean[1]], ALU.subtract)
                TT(m2[:, :], st[:, q.u, :, square[0]], st[:, q.u, :, square[1]], ALU.add).then_inc(S["v_mm" + n], 1)

            def square(q, n):
                st, ms, dm, m2, dd, vs, ve = stats[n]
                wait(dve, S["v_mm" + n], q)
                TT(dd[:, :], dm[:, :], dm[:, :], ALU.mult).then_inc(S["v_dd" + n], 1)

            def total(q, n):
                st, ms, dm, m2, dd, vs, ve = stats[n]
                wait(dve, S["v_dd" + n], q)
                STT(vs[:, :], dd[:, :], D / 4.0, m2[:, :], ALU.mult, ALU.add).then_inc(S["v_vs" + n], 1)

            def scaled(q, n):
                st, ms, dm, m2, dd, vs, ve = stats[n]
                wait(dve, S["v_vs" + n], q)
                TS(ve[:, q.u], vs[:, :], 1.0 / D, LN_EPS, ALU.mult, ALU.add).then_inc(S["v_ve" + n], 1)

            def mask(y, s, done):
                wait(dve, S["pe_sc"], y)
                wait(dve, S["pe_ta" if s == 0 else "pe_tb"], y, 2)
                TT(a_t[:, y.u, s, :, :], bank[:, 2 + 2 * s:4 + 2 * s, 0:L],
                   cst("mask").rearrange("p (a l) -> p a l", a=2), ALU.mult).then_inc(S[done], 1)

            def add_shared(z, s, done, ready):
                wait(dve, S[ready], z)
                TT(fin[:, z.u, s * NT:(s + 1) * NT, :], bank[:, 4 + s, 0:NT * D].rearrange("p (t d) -> p t d", d=D),
                   h2[:, z.u, s * NT:(s + 1) * NT, :], ALU.add).then_inc(S[done], 1)

            def bias_scale(q, ms, rs, nb, s_rs, s_nb):
                wait(dve, s_rs, q)
                STT(nb[:, q.u, :], ms[:, q.u, :], -0.5, rs[:, q.u, :], ALU.mult, ALU.mult).then_inc(s_nb, 1)

            def mix(y, s, pt, ap, d, e, f, used):
                wait(dve, S[pt], y)
                wait(dve, S[ap], y)
                TT(dif[:, s, :], bank[:, 2 * s, 0:L], pos_o[:, s, :], ALU.subtract).then_inc(S[d], 1)
                if s == 0:
                    wait(dve, S["a_gb"], y)
                wait(dve, S[d], y)
                STT(gdif[:, s, :], gt[:, y.u, s, :], 1.0, dif[:, s, :], ALU.add, ALU.mult).then_inc(S[e], 1)
                wait(dve, S[e], y)
                wait(dve, S[used], y, 1)
                STT(tot[:, s, :], pos_o[:, s, :], 2.0, gdif[:, s, :], ALU.mult, ALU.add).then_inc(S[f], 1)

            def body(k):
                y, z, w = k.back(1), k.back(2), k.back(3)
                if k.runs():
                    wait(dve, S["pe_th"], k, 2)
                    for s, ready in enumerate(("pe_toka", "pe_tok")):
                        wait(dve, S[ready], k)
                        ins = TT(h_t[:, k.u, s, 0:NIMG], bank[:, s, 0:NIMG], pos_t[:, :], ALU.add)
                    ins.then_inc(S["v_ht"], 1)
                if z.runs():
                    bias_scale(z, ms2, rs2, nb2, S["p_rs2"], S["v_nb2"])
                if k.runs():
                    wait_dma(dve, s_txt, k, 1)
                    for i in (2, NT + 2, 0, 1, NT, NT + 1):
                        if i == 0:
                            wait(dve, S["a_h"], k)
                        ins = vv.bn_stats(st1[:, k.u, i, :], h[:, k.u, i // NT, i % NT, :])
                    ins.then_inc(S["v_st1"], 1)
                    moments(k, "1")
                if y.runs():
                    mask(y, 0, "v_ma")
                if k.runs():
                    square(k, "1")
                if y.runs():
                    mask(y, 1, "v_mb")
                if k.runs():
                    total(k, "1")
                    scaled(k, "1")
                if w.runs():
                    wait(dve, S["pe_pf"], w)
                    prev, now = carry[:, 1 - w.u, :], carry[:, w.u, :]
                    TT(cnt[:, :, :], bank[:, 6, 0:2 * NT * E].rearrange("p (t e) -> p t e", e=E),
                       prev.rearrange("p (o e) -> p o e", o=1).to_broadcast([128, 2 * NT, E]), ALU.add)
                    TT(now, bank[:, 6, 2 * NT * E:(2 * NT + 1) * E], prev, ALU.add).then_inc(S["v_cnt"], 1)
                if w.runs():
                    wait(dve, S["v_cnt"], w)
                    for r in range(2):
                        ins = TT(picked[:, r, :, :], hot[:, r, :, :], cnt[:, :, :], ALU.mult)
                    ins.then_inc(S["v_pick"], 1)
                if w.runs():
                    wait(dve, S["v_pick"], w)
                    vv.reduce_sum(place[:, :, :].rearrange("p r t -> p (r t)"),
                                  picked[:, :, :, :].rearrange("p r t e -> p (r t) e"), AX.X).then_inc(S["v_place"], 1)
                    wait(dve, S["v_place"], w)
                    vv.tensor_copy(xs[:, w.u, :, P_COL:P_COL + 2], place[:, :, :].rearrange("p r t -> p t r"))
                    TS(over[:, :, :], place[:, :, :], CAP - 0.5, FAR, ALU.is_gt, ALU.mult)
                    STT(slotf[:, :, :], idx[:, :, :], float(CAP), place[:, :, :], ALU.mult, ALU.add).then_inc(S["v_over"], 1)
                if k.runs():
                    bias_scale(k, ms1, rs1, nb1, S["p_rs1"], S["v_nb1"])
                if w.runs():
                    wait(dve, S["v_over"], w)
                    wait_dma(dve, s_scat, w, 4 * NT, 2)
                    TT(slot[:, w.u, :, :], slotf[:, :, :], over[:, :, :], ALU.add).then_inc(S["v_sloti"], 1)
                if y.runs():
                    mix(y, 0, "pe_ta", "a_pa", "v_da", "v_ea", "v_tota", "pe_woa")
                    mix(y, 1, "pe_tb", "a_pb", "v_db", "v_eb", "v_totb", "pe_wob")
                if z.runs():
                    for s, (a, f, done, prev) in enumerate((("a_sia", "pe_ffa", "v_m3a", "pe_oa"),
                                                            ("a_sib", "pe_ffb", "v_m3b", "pe_ob"))):
                        wait(dve, S[prev], z, 1)
                        wait(dve, S[a], z)
                        TT(su[:, s, :], sl[:, s, :], bank[:, 0 if s == 0 else 5, 0:L], ALU.mult).then_inc(S[done], 1)
                    wait(dve, S["v_tok"], z, 1)
                    wait(dve, S["a_lg"], z)
                    TS(tokn[:, z.u, :], tokn[:, 1 - z.u, :], 2.0 * L, None, ALU.add).then_inc(S["v_tok"], 1)
                    for i in range(2 * NT):
                        ins = vv.max(top[:, i, :], lg[:, i, :])
                    ins.then_inc(S["v_max"], 1)
                if y.runs():
                    wait(dve, S["p_hbo"], y)
                    wait(dve, S["v_finb"], y, 2)
                    wait(dve, S["a_x2"], y, 2)
                    for s, (done, ready) in enumerate((("v_h2a", "pe_woa"), ("v_h2b", "pe_wob"))):
                        wait(dve, S[ready], y)
                        TT(h2[:, y.u, s * NT:(s + 1) * NT, :], bank[:, 4 + s, 0:NT * D].rearrange("p (t d) -> p t d", d=D),
                           hbo[:, y.u, s * NT:(s + 1) * NT, :], ALU.add).then_inc(S[done], 1)
                if z.runs():
                    wait(dve, S["a_small"], z, 1)
                    wait(dve, S["v_max"], z)
                    TS(lo[:, :, :], top[:, :, 0:2], -1.0, None, ALU.min)
                    TS(hi[:, :, :], top[:, :, 0:2], -1.0, None, ALU.max).then_inc(S["v_lohi"], 1)
                    for i in range(2 * NT):
                        ins = vv.max_index(topi[:, i, :], top[:, i, :], lg[:, i, :])
                    ins.then_inc(S["v_imax"], 1)
                if y.runs():
                    wait(dve, S["v_h2b"], y)
                    for i in range(2 * NT):
                        ins = vv.bn_stats(st2[:, y.u, i, :], h2[:, y.u, i, :])
                    ins.then_inc(S["v_st2"], 1)
                if z.runs():
                    wait(dve, S["v_imax"], z)
                    wait(dve, S["v_over"], z, 1)
                    vv.tensor_copy(idx[:, :, :].rearrange("p r t -> p t r"), topi[:, :, 0:2]).then_inc(S["v_idx"], 1)
                if k.runs():
                    for s, (done, ready, prev) in enumerate((("v_va", "pe_va", "pe_ta"), ("v_vb", "pe_vb", "pe_tb"))):
                        wait(dve, S[ready], k)
                        wait(dve, S[prev], k, 2)
                        TT(v[:, k.u, s, :, :], bank[:, 1 + s, 0:NT * D].rearrange("p (t d) -> p t d", d=D),
                           bv_row[:, :].rearrange("p (o d) -> p o d", o=1).to_broadcast([128, NT, D]), ALU.add)\
                            .then_inc(S[done], 1)
                if y.runs():
                    moments(y, "2")
                if z.runs():
                    wait(dve, S["v_idx"], z)
                    wait(dve, S["v_pick"], z, 1)
                    for r in range(2):
                        ins = TT(hot[:, r, :, :], cst("iota")[:, 0:E].rearrange("p (o e) -> p o e", o=1).to_broadcast([128, 2 * NT, E]),
                                 idx[:, r, :].rearrange("p (t o) -> p t o", o=1).to_broadcast([128, 2 * NT, E]), ALU.is_equal)
                    ins.then_inc(S["v_hot"], 1)
                if y.runs():
                    square(y, "2")
                if z.runs():
                    wait(dve, S["a_small"], z)
                    vv.reciprocal(rlo[:, :, :], lo[:, :, :]).then_inc(S["v_rlo"], 1)
                if y.runs():
                    total(y, "2")
                if z.runs():
                    wait(dve, S["v_hot"], z)
                    wait(dve, S["pe_pf"], z, 1)
                    TT(both[:, 0:2 * NT, :], hot[:, 0, :, :], hot[:, 1, :, :], ALU.add).then_inc(S["v_both"], 1)
                if y.runs():
                    scaled(y, "2")
                if z.runs():
                    wait(dve, S["v_rlo"], z)
                    STT(sgl[:, :, :], rlo[:, :, :], 0.5 / SIG_M1, slo[:, :, :], ALU.mult, ALU.mult).then_inc(S["v_sgl"], 1)
                    wait_dma(dve, s_store, z, NT, 2)
                    add_shared(z, 0, "v_fina", "pe_oa")
                    wait(dve, S["v_sgl"], z)
                    STT(sg[:, :, :], thi[:, :, :], 1.0, sgl[:, :, :], ALU.add, ALU.mult).then_inc(S["v_sg"], 1)
                    add_shared(z, 1, "v_finb", "pe_ob")
                    wait(dve, S["v_sg"], z)
                    STT(ssum[:, :], sg[:, :, 0], 1e-20, sg[:, :, 1], ALU.add, ALU.add).then_inc(S["v_ssum"], 1)
                if k.runs():
                    wait(dve, S["a_sin"], k)
                    wait(dve, S["pe_sc"], k, 2)
                    TT(qn[:, k.u, :], kq[:, k.u, 1, :], wn[:, :], ALU.mult).then_inc(S["v_qn"], 1)
                if z.runs():
                    wait(dve, S["v_ssum"], z)
                    vv.reciprocal(sinv[:, :], ssum[:, :]).then_inc(S["v_sinv"], 1)
                    vv.tensor_copy(xs[:, z.u, :, E_COL:E_COL + 2], idx[:, :, :].rearrange("p r t -> p t r"))
                    wait(dve, S["v_tok"], z)
                    vv.tensor_copy(xs[:, z.u, :, T_COL], tokn[:, z.u, :])
                    wait(dve, S["v_sinv"], z)
                    for r in range(2):
                        ins = STT(xs[:, z.u, :, W_COL + r], sg[:, :, r], ROUTE, sinv[:, :], ALU.mult, ALU.mult)
                    ins.then_inc(S["v_meta"], 1)
            steps(dve, body)

            def prepare(q):
                odd = slice(2, 4)
                col = lambda c, t: rows[:, q.load, t, c]
                every = slice(0, 4)
                u = q.u
                dve.wait_ge(e_load[q.load], (q.j + (q.m // 4 + 1)) * 64)
                wait_expert(dve, X["e_prep"], q, 1)
                TS(ecur[:, u, :], ecur[:, 1 - u, :], 2.0, None, ALU.add).then_inc(X["e_cur"], 1)
                TT(ewd[:, :], col(W_COL, every), col(W_COL + 1, every), ALU.subtract).then_inc(X["e_wd"], 1)
                TT(epd[:, :], col(P_COL + 1, odd), col(P_COL, odd), ALU.subtract)
                TT(esum[:, :], col(E_COL, odd), col(E_COL + 1, odd), ALU.add).then_inc(X["e_sum"], 1)
                wait_expert(dve, X["e_cur"], q)
                TT(esel[:, :], col(E_COL, every), ecur[:, u, :], ALU.is_equal).then_inc(X["e_sel"], 1)
                wait_expert(dve, X["e_sum"], q)
                STT(edif[:, :], ecur[:, u, odd], -2.0, esum[:, :], ALU.mult, ALU.add).then_inc(X["e_psum"], 1)
                wait_expert(dve, X["e_wd"], q)
                wait_expert(dve, X["e_sel"], q)
                TT(ewm[:, :], esel[:, :], ewd[:, :], ALU.mult).then_inc(X["e_wm"], 1)
                TT(epm[:, :], esel[:, odd], epd[:, :], ALU.mult).then_inc(X["e_pm"], 1)
                wait_expert(dve, X["e_psum"], q)
                TS(esame[:, :], edif[:, :], -1.0, -1000.0, ALU.is_equal, ALU.mult).then_inc(X["e_same"], 1)
                wait_expert(dve, X["e_wm"], q)
                TT(ew[:, u, :], ewm[:, :], col(W_COL + 1, every), ALU.add).then_inc(X["e_w"], 1)
                wait_expert(dve, X["e_pm"], q)
                TT(eplace[:, :], epm[:, :], col(P_COL, odd), ALU.add).then_inc(X["e_place"], 1)
                TT(edump[:, :], cst("dump")[:, odd], col(T_COL, odd), ALU.subtract)
                wait_expert(dve, X["e_place"], q)
                wait_expert(dve, X["e_same"], q)
                STT(emate[:, :], eplace[:, :], 1000.0, esame[:, :], ALU.add, ALU.add).then_inc(X["e_mate"], 1)
                vv.tensor_copy(etokf[:, u, 0:2], col(T_COL, slice(0, 2)))
                wait_expert(dve, X["e_mate"], q)
                TS(ekept[:, :], emate[:, :], CAP - 0.5, None, ALU.is_lt).then_inc(X["e_kept"], 1)
                wait_expert(dve, X["e_comb"], q, 4)
                for i in range(2):
                    ins = TS(mate[:, q.load, i, :], cst("iota"), emate[:, i:i + 1], None, ALU.is_equal)
                ins.then_inc(X["e_mt"], 1)
                wait_expert(dve, X["e_kept"], q)
                TT(emove[:, :], ekept[:, :], edump[:, :], ALU.mult).then_inc(X["e_move"], 1)
                wait_expert(dve, X["e_move"], q)
                TT(etokf[:, u, odd], emove[:, :], col(T_COL, odd), ALU.add).then_inc(X["e_prep"], 1)

            def gated(q):
                wait_expert(dve, X["e_silu"], q)
                wait_expert(dve, X["e_y0"], q, 2)
                TT(ge[:, q.u, :], ae[:, q.u, :], bank[:, 2 + q.u, CAP:2 * CAP], ALU.mult).then_inc(X["e_g"], 1)

            def weighted(q):
                wait_expert(dve, X["e_w"], q)
                wait_expert(dve, X["e_y0"], q)
                wait_expert(dve, e_add, q, 4, 64)
                for i in range(4):
                    TS(ye[:, q.load, i, :], bank[:, 4 + 2 * (i // 2) + q.u, (i % 2) * D:(i % 2 + 1) * D],
                       ew[:, q.u, i:i + 1], None, ALU.mult)
                wait_expert(dve, X["e_prep"], q)
                vv.tensor_copy(etok[:, q.load, :], etokf[:, q.u, :]).then_inc(X["e_tok"], 1)

            def finish(q, back):
                u, b = (q.m - back) % 2, (q.m - back) % 4
                wait_expert(dve, X["e_comb"], q, back)
                TT(ysum[:, b, :, :], bank[:, 4 + u, CAP:CAP + 2 * D].rearrange("p (i d) -> p i d", d=D),
                   ye[:, b, 0:2, :], ALU.add).then_inc(X["e_yv"], 1)

            def expert(q):
                if is_first(q):
                    prepare(q)
                    gated(q)
                if not is_last(q):
                    prepare(q.next())
                if not is_first(q):
                    finish(q, 1)
                if not is_last(q):
                    gated(q.next())
                weighted(q)
                if is_last(q):
                    finish(q, 0)

            expert_pairs(dve, expert)


_INS = ['x', 'txt', 'L0_tok_W', 'L0_tok_b', 'L0_tok_token', 'L0_tok_pos', 'L0_attn_Wk', 'L0_attn_bk', 'L0_attn_Wq',
        'L0_attn_bq', 'L0_attn_Wv', 'L0_attn_bv', 'L0_attn_set_weights', 'L0_attn_pos_freqs', 'L0_attn_Wg',
        'L0_attn_bg', 'L0_attn_pos_weight', 'L0_attn_Wo', 'L0_attn_bo', 'L0_ffn_gate_w', 'L0_ffn_w1', 'L0_ffn_w3',
        'L0_ffn_w2', 'L0_ffn_sw1', 'L0_ffn_sw3', 'L0_ffn_sw2']


def build(nc, arrays):
    t = {n: nc.dram_tensor(f"in_{n}", a.shape, F32, kind="ExternalInput").ap() for n, a in arrays.items()}
    out = nc.dram_tensor("out_rows", (TOKENS + SPARE, D), F32, kind="ExternalOutput").ap()
    slots_d = nc.dram_tensor("slot_rows", (SLOTS, ROW), F32, kind="Internal").ap()
    program(nc, t, out, slots_d)


def kernel(**inputs):
    import concourse.bacc as _bacc
    from concourse.bass_utils import run_bass_kernel_spmd as _run

    nc = _bacc.Bacc("TRN2", target_bir_lowering=False, num_devices=1)
    arrays = {n: np.ascontiguousarray(inputs[n]) for n in _INS}
    arrays["consts"] = constants()
    build(nc, arrays)
    r = _run(nc, [{f"in_{n}": a for n, a in arrays.items()}], core_ids=[0])
    return r.results[0]["out_rows"][0:TOKENS].reshape(B, L, D)
```
